# Optimizing a Trainium2 kernel written in Bass

```python
import numpy as np
import jax
import jax.numpy as jnp

def _softmax(x, axis=-1):
    return jax.nn.softmax(x, axis=axis)

def _gelu(x):
    return jax.nn.gelu(x, approximate=True)

def _silu(x):
    return jax.nn.silu(x)

def _sigmoid(x):
    return jax.nn.sigmoid(x)

def _layernorm(x, axis=-1, eps=1e-05):
    m = jnp.mean(x, axis=axis, keepdims=True)
    v = jnp.var(x, axis=axis, keepdims=True)
    return (x - m) / jnp.sqrt(v + eps)

def _scatter_add(tgt, idx, src, axis=0):
    return tgt.at[idx].add(src)

def _segment_sum(src, seg, n):
    return jax.ops.segment_sum(src, seg, n)
kernel_name = 'mk_gnn_ffn_d4_gnn_r64_41aa85'

def setup_inputs(seed: int=0):
    np.random.seed(seed)
    _w = jnp.asarray

    def _rec_inputs():
        import jax
        import jax.numpy as jnp
        _gk = jax.random.key(seed)
        x = -0.0003019 + 1 * jax.random.normal(jax.random.fold_in(_gk, 1), (625, 512), jnp.float32)
        _s = jax.random.randint(jax.random.fold_in(_gk, 2), (5000,), 0, 625, jnp.int32)
        _d = jax.random.randint(jax.random.fold_in(_gk, 3), (5000,), 0, 625, jnp.int32)
        _loop = jnp.arange(625, dtype=jnp.int32)
        src = jnp.concatenate([_s, _d, _loop])
        dst = jnp.concatenate([_d, _s, _loop])
        _o = jnp.argsort(dst, stable=True)
        src = src[_o]
        dst = dst[_o]
        edge_attr_96 = -4.21973e-05 + 0.999841 * jax.random.normal(jax.random.fold_in(_gk, 13), (10625, 96), jnp.float32)
        return (x, src, dst, edge_attr_96)
    x, src, dst, edge_attr_96 = _rec_inputs()

    def _L0_gnn_setup():
        import jax, jax.numpy as jnp
        import numpy as np
        N = 625
        IN_DIM = 512
        OUT_DIM = 512
        E_RAND = 10000
        SLOPE = 0.1
        key = jax.random.key(seed)
        k1, k2, k3, k4, k5 = jax.random.split(key, 5)
        features = jax.random.normal(k1, (N, IN_DIM), dtype=jnp.float32)
        src = jax.random.randint(k2, (E_RAND,), 0, N)
        dst = jax.random.randint(k3, (E_RAND,), 0, N)
        loops = jnp.arange(N)
        edges = jnp.stack([jnp.concatenate([src, loops]), jnp.concatenate([dst, loops])], axis=1).astype(jnp.int32)
        W = jax.random.normal(k4, (IN_DIM, OUT_DIM), dtype=jnp.float32) / np.sqrt(IN_DIM)
        b = jnp.zeros((OUT_DIM,), dtype=jnp.float32)
        a = jax.random.normal(k5, (2 * OUT_DIM, 1), dtype=jnp.float32) * np.sqrt(2.0 / (2 * OUT_DIM))
        return {'features': features, 'edges': edges, 'W': W, 'b': b, 'a': a}
    _L0_gnn_all = _L0_gnn_setup()
    _L0_gnn_in = {k: v for k, v in _L0_gnn_all.items() if k in ('W', 'b', 'a')}
    del _L0_gnn_all

    def _L0_ffn_setup():
        import jax, jax.numpy as jnp
        import numpy as np
        B, S, D = (4, 32, 512)
        I = 384
        E = 16
        K = 2

        def _inv_softplus(v):
            return float(np.log(np.expm1(v)))

        def swiglu5(h, alpha, gate_scale, up_shift, gate_clamp_raw, up_clamp_raw):
            gate_clamp = jax.nn.softplus(gate_clamp_raw)
            up_clamp = jax.nn.softplus(up_clamp_raw)
            g = jnp.clip(h[..., ::2], -gate_clamp, gate_clamp)
            u = jnp.clip(h[..., 1::2], -up_clamp, up_clamp)
            return g * jax.nn.sigmoid(g * alpha) * gate_scale * (u + up_shift)
        key = jax.random.key(seed)
        ks = jax.random.split(key, 10)
        std = 0.02
        raw = _inv_softplus(7.0)
        act = jnp.array([1.702, 1.0, 1.0, raw, raw], dtype=jnp.float32)
        return {'x': jax.random.normal(ks[0], (B, S, D), dtype=jnp.float32), 'gate_w': jax.random.normal(ks[1], (D, E), dtype=jnp.float32) * 0.01, 'gate_b': jnp.zeros((E,), dtype=jnp.float32), 'shared_w1': jax.random.normal(ks[2], (D, 2 * I), dtype=jnp.float32) * std, 'shared_b1': jnp.zeros((2 * I,), dtype=jnp.float32), 'shared_w2': jax.random.normal(ks[3], (I, D), dtype=jnp.float32) * std, 'shared_b2': jnp.zeros((D,), dtype=jnp.float32), 'shared_act': act, 'expert_w1': jax.random.normal(ks[4], (E, D, 2 * I), dtype=jnp.float32) * std, 'expert_b1': jnp.zeros((E, 2 * I), dtype=jnp.float32), 'expert_w2': jax.random.normal(ks[5], (E, I, D), dtype=jnp.float32) * std, 'expert_b2': jnp.zeros((E, D), dtype=jnp.float32), 'expert_act': jnp.tile(act[None, :], (E, 1))}
    _L0_ffn_all = _L0_ffn_setup()
    _L0_ffn_in = {k: v for k, v in _L0_ffn_all.items() if k in ('gate_w', 'gate_b', 'shared_w1', 'shared_b1', 'shared_w2', 'shared_b2', 'shared_act', 'expert_w1', 'expert_b1', 'expert_w2', 'expert_b2', 'expert_act')}
    del _L0_ffn_all

    def _L1_gnn_setup():
        import jax, jax.numpy as jnp
        import numpy as np
        N_NODES = 10000
        N_EDGES = 2500
        IN_DIM = 512
        OUT_DIM = 512
        LN_EPS = 1e-05
        key = jax.random.key(seed)
        k_x, k_src, k_ws, k_wn = jax.random.split(key, 4)
        x = jax.random.normal(k_x, (N_NODES, IN_DIM), dtype=jnp.float32)
        edge_src = jax.random.randint(k_src, (N_EDGES,), 0, N_NODES, dtype=jnp.int32)
        edge_dst = jnp.repeat(jnp.arange(N_NODES, dtype=jnp.int32), N_EDGES // N_NODES)
        deg = jnp.full((N_NODES,), float(N_EDGES // N_NODES), dtype=jnp.float32)
        scale = 1.0 / np.sqrt(IN_DIM)
        W_self = jax.random.normal(k_ws, (OUT_DIM, IN_DIM), dtype=jnp.float32) * scale
        W_neigh = jax.random.normal(k_wn, (OUT_DIM, IN_DIM), dtype=jnp.float32) * scale
        bias = jnp.zeros((OUT_DIM,), dtype=jnp.float32)
        gamma = jnp.ones((OUT_DIM,), dtype=jnp.float32)
        beta = jnp.zeros((OUT_DIM,), dtype=jnp.float32)
        return {'x': x, 'edge_src': edge_src, 'edge_dst': edge_dst, 'deg': deg, 'W_self': W_self, 'W_neigh': W_neigh, 'bias': bias, 'gamma': gamma, 'beta': beta}
    _L1_gnn_all = _L1_gnn_setup()
    _L1_gnn_in = {k: v for k, v in _L1_gnn_all.items() if k in ('W_self', 'W_neigh', 'bias', 'gamma', 'beta')}
    del _L1_gnn_all

    def _L1_ffn_setup():
        import jax, jax.numpy as jnp
        import numpy as np
        TOP_K = 2
        key = jax.random.key(seed)
        ks = jax.random.split(key, 4)
        b, t, d, e, h = (2, 32, 512, 8, 1024)
        scale = 0.02
        return {'x': jax.random.normal(ks[0], (b, t, d), dtype=jnp.float32), 'router_w': jax.random.normal(ks[1], (e, d), dtype=jnp.float32) * scale, 'router_b': jnp.zeros((e,), dtype=jnp.float32), 'fc1_w': jax.random.normal(ks[2], (e, 2 * h, d), dtype=jnp.float32) * scale, 'fc1_b': jnp.zeros((e, 2 * h), dtype=jnp.float32), 'fc2_w': jax.random.normal(ks[3], (e, d, h), dtype=jnp.float32) * scale, 'fc2_b': jnp.zeros((e, d), dtype=jnp.float32)}
    _L1_ffn_all = _L1_ffn_setup()
    _L1_ffn_in = {k: v for k, v in _L1_ffn_all.items() if k in ('router_w', 'router_b', 'fc1_w', 'fc1_b', 'fc2_w', 'fc2_b')}
    del _L1_ffn_all

    def _L2_gnn_setup():
        import jax, jax.numpy as jnp
        import numpy as np
        NODE_DIM, EDGE_DIM, HIDDEN, OUT = (512, 96, 1024, 512)
        N_NODES, N_EDGES = (50000, 12500)
        LN_EPS = 1e-05
        key = jax.random.key(seed)
        ks = jax.random.split(key, 12)
        node_feat = jax.random.normal(ks[0], (N_NODES, NODE_DIM), dtype=jnp.float32)
        edge_feat = jax.random.normal(ks[1], (N_EDGES, EDGE_DIM), dtype=jnp.float32)
        edge_index = jax.random.randint(ks[2], (2, N_EDGES), 0, N_NODES, dtype=jnp.int32)
        in_dim = NODE_DIM + EDGE_DIM

        def lin(k, fan_in, fan_out):
            bound = 1.0 / np.sqrt(fan_in)
            kw, kb = jax.random.split(k)
            W = jax.random.uniform(kw, (fan_in, fan_out), minval=-bound, maxval=bound, dtype=jnp.float32)
            b = jax.random.uniform(kb, (fan_out,), minval=-bound, maxval=bound, dtype=jnp.float32)
            return (W, b)
        W1, b1 = lin(ks[3], in_dim, HIDDEN)
        W2, b2 = lin(ks[4], HIDDEN, HIDDEN)
        W3, b3 = lin(ks[5], HIDDEN, OUT)
        gamma = jnp.ones((OUT,), dtype=jnp.float32)
        beta = jnp.zeros((OUT,), dtype=jnp.float32)
        return {'node_feat': node_feat, 'edge_feat': edge_feat, 'edge_index': edge_index, 'n_nodes': N_NODES, 'W1': W1, 'b1': b1, 'W2': W2, 'b2': b2, 'W3': W3, 'b3': b3, 'gamma': gamma, 'beta': beta}
    _L2_gnn_all = _L2_gnn_setup()
    _L2_gnn_in = {k: v for k, v in _L2_gnn_all.items() if k in ('W1', 'b1', 'W2', 'b2', 'W3', 'b3', 'gamma', 'beta')}
    del _L2_gnn_all

    def _L2_ffn_setup():
        import jax, jax.numpy as jnp
        import numpy as np
        H = 512
        FF = 4 * H
        E = 8
        K = 2
        B, S = (4, 64)
        key = jax.random.key(seed)
        ks = jax.random.split(key, 4)
        s = 0.02
        return {'x': jax.random.normal(ks[0], (B, S, H), dtype=jnp.float32), 'Wg': jax.random.normal(ks[1], (H, E), dtype=jnp.float32) * s, 'bg': jnp.zeros((E,), dtype=jnp.float32), 'W1': jax.random.normal(ks[2], (E, H, FF), dtype=jnp.float32) * s, 'b1': jnp.zeros((E, FF), dtype=jnp.float32), 'W2': jax.random.normal(ks[3], (E, FF, H), dtype=jnp.float32) * s, 'b2': jnp.zeros((E, H), dtype=jnp.float32)}
    _L2_ffn_all = _L2_ffn_setup()
    _L2_ffn_in = {k: v for k, v in _L2_ffn_all.items() if k in ('Wg', 'bg', 'W1', 'b1', 'W2', 'b2')}
    del _L2_ffn_all

    def _L3_gnn_setup():
        import jax, jax.numpy as jnp
        import numpy as np
        N_FRAMES = 2048
        D_FEAT = 512
        N_SHOTS = 32
        SHOT_LEN = N_FRAMES // N_SHOTS
        key = jax.random.key(seed)
        x = jax.random.normal(key, (N_FRAMES, D_FEAT), dtype=jnp.float32)
        starts = jnp.arange(N_SHOTS, dtype=jnp.int64) * SHOT_LEN
        ends = starts + (SHOT_LEN - 1)
        graph = jnp.stack([starts, ends], axis=1)
        return {'input': x, 'graph': graph}
    _L3_gnn_all = _L3_gnn_setup()
    _L3_gnn_in = {k: v for k, v in _L3_gnn_all.items() if k in ()}
    del _L3_gnn_all

    def _L3_ffn_setup():
        import jax, jax.numpy as jnp
        import numpy as np
        B, S, H, E, K = (8, 64, 512, 8, 2)
        key = jax.random.key(seed)
        ks = jax.random.split(key, 7)
        s_h = 1.0 / np.sqrt(H)
        s_2h = 1.0 / np.sqrt(2 * H)
        return {'x': jax.random.normal(ks[0], (B, S, H), dtype=jnp.float32), 'gate_w': jax.random.uniform(ks[1], (H, E), minval=-s_h, maxval=s_h, dtype=jnp.float32), 'gate_b': jax.random.uniform(ks[2], (E,), minval=-s_h, maxval=s_h, dtype=jnp.float32), 'w1': jax.random.uniform(ks[3], (E, H, 2 * H), minval=-s_h, maxval=s_h, dtype=jnp.float32), 'b1': jax.random.uniform(ks[4], (E, 2 * H), minval=-s_h, maxval=s_h, dtype=jnp.float32), 'w2': jax.random.uniform(ks[5], (E, 2 * H, H), minval=-s_2h, maxval=s_2h, dtype=jnp.float32), 'b2': jax.random.uniform(ks[6], (E, H), minval=-s_2h, maxval=s_2h, dtype=jnp.float32)}
    _L3_ffn_all = _L3_ffn_setup()
    _L3_ffn_in = {k: v for k, v in _L3_ffn_all.items() if k in ('gate_w', 'gate_b', 'w1', 'b1', 'w2', 'b2')}
    del _L3_ffn_all
    return {'x': x, 'src': src, 'dst': dst, 'edge_attr_96': edge_attr_96, 'L0_gnn_W': _L0_gnn_in['W'], 'L0_gnn_b': _L0_gnn_in['b'], 'L0_gnn_a': _L0_gnn_in['a'], 'L0_ffn_gate_w': _L0_ffn_in['gate_w'], 'L0_ffn_gate_b': _L0_ffn_in['gate_b'], 'L0_ffn_shared_w1': _L0_ffn_in['shared_w1'], 'L0_ffn_shared_b1': _L0_ffn_in['shared_b1'], 'L0_ffn_shared_w2': _L0_ffn_in['shared_w2'], 'L0_ffn_shared_b2': _L0_ffn_in['shared_b2'], 'L0_ffn_shared_act': _L0_ffn_in['shared_act'], 'L0_ffn_expert_w1': _L0_ffn_in['expert_w1'], 'L0_ffn_expert_b1': _L0_ffn_in['expert_b1'], 'L0_ffn_expert_w2': _L0_ffn_in['expert_w2'], 'L0_ffn_expert_b2': _L0_ffn_in['expert_b2'], 'L0_ffn_expert_act': _L0_ffn_in['expert_act'], 'L1_gnn_W_self': _L1_gnn_in['W_self'], 'L1_gnn_W_neigh': _L1_gnn_in['W_neigh'], 'L1_gnn_bias': _L1_gnn_in['bias'], 'L1_gnn_gamma': _L1_gnn_in['gamma'], 'L1_gnn_beta': _L1_gnn_in['beta'], 'L1_ffn_router_w': _L1_ffn_in['router_w'], 'L1_ffn_router_b': _L1_ffn_in['router_b'], 'L1_ffn_fc1_w': _L1_ffn_in['fc1_w'], 'L1_ffn_fc1_b': _L1_ffn_in['fc1_b'], 'L1_ffn_fc2_w': _L1_ffn_in['fc2_w'], 'L1_ffn_fc2_b': _L1_ffn_in['fc2_b'], 'L2_gnn_W1': _L2_gnn_in['W1'], 'L2_gnn_b1': _L2_gnn_in['b1'], 'L2_gnn_W2': _L2_gnn_in['W2'], 'L2_gnn_b2': _L2_gnn_in['b2'], 'L2_gnn_W3': _L2_gnn_in['W3'], 'L2_gnn_b3': _L2_gnn_in['b3'], 'L2_gnn_gamma': _L2_gnn_in['gamma'], 'L2_gnn_beta': _L2_gnn_in['beta'], 'L2_ffn_Wg': _L2_ffn_in['Wg'], 'L2_ffn_bg': _L2_ffn_in['bg'], 'L2_ffn_W1': _L2_ffn_in['W1'], 'L2_ffn_b1': _L2_ffn_in['b1'], 'L2_ffn_W2': _L2_ffn_in['W2'], 'L2_ffn_b2': _L2_ffn_in['b2'], 'L3_ffn_gate_w': _L3_ffn_in['gate_w'], 'L3_ffn_gate_b': _L3_ffn_in['gate_b'], 'L3_ffn_w1': _L3_ffn_in['w1'], 'L3_ffn_b1': _L3_ffn_in['b1'], 'L3_ffn_w2': _L3_ffn_in['w2'], 'L3_ffn_b2': _L3_ffn_in['b2']}

def reference(x, src, dst, edge_attr_96, L0_gnn_W, L0_gnn_b, L0_gnn_a, L0_ffn_gate_w, L0_ffn_gate_b, L0_ffn_shared_w1, L0_ffn_shared_b1, L0_ffn_shared_w2, L0_ffn_shared_b2, L0_ffn_shared_act, L0_ffn_expert_w1, L0_ffn_expert_b1, L0_ffn_expert_w2, L0_ffn_expert_b2, L0_ffn_expert_act, L1_gnn_W_self, L1_gnn_W_neigh, L1_gnn_bias, L1_gnn_gamma, L1_gnn_beta, L1_ffn_router_w, L1_ffn_router_b, L1_ffn_fc1_w, L1_ffn_fc1_b, L1_ffn_fc2_w, L1_ffn_fc2_b, L2_gnn_W1, L2_gnn_b1, L2_gnn_W2, L2_gnn_b2, L2_gnn_W3, L2_gnn_b3, L2_gnn_gamma, L2_gnn_beta, L2_ffn_Wg, L2_ffn_bg, L2_ffn_W1, L2_ffn_b1, L2_ffn_W2, L2_ffn_b2, L3_ffn_gate_w, L3_ffn_gate_b, L3_ffn_w1, L3_ffn_b1, L3_ffn_w2, L3_ffn_b2):
    import jax
    import jax.numpy as jnp

    def _L0_gnn_ref(features, edges, W, b, a):
        import jax, jax.numpy as jnp
        import numpy as np
        N = 625
        IN_DIM = 512
        OUT_DIM = 512
        E_RAND = 10000
        SLOPE = 0.1
        emb = features @ W + b
        a_src = a[:OUT_DIM, 0]
        a_dst = a[OUT_DIM:, 0]
        s_node = emb @ a_src
        t_node = emb @ a_dst
        src = edges[:, 0]
        dst = edges[:, 1]
        e = jnp.exp(jax.nn.leaky_relu(s_node[src] + t_node[dst], negative_slope=SLOPE))
        row_sum = jax.ops.segment_sum(e, src, num_segments=N)
        results = jax.ops.segment_sum(e[:, None] * emb[dst], src, num_segments=N)
        return results / row_sum[:, None]

    def _L0_ffn_ref(x, gate_w, gate_b, shared_w1, shared_b1, shared_w2, shared_b2, shared_act, expert_w1, expert_b1, expert_w2, expert_b2, expert_act):
        import jax, jax.numpy as jnp
        import numpy as np
        B, S, D = (4, 32, 512)
        I = 384
        E = 16
        K = 2

        def _inv_softplus(v):
            return float(np.log(np.expm1(v)))

        def swiglu5(h, alpha, gate_scale, up_shift, gate_clamp_raw, up_clamp_raw):
            gate_clamp = jax.nn.softplus(gate_clamp_raw)
            up_clamp = jax.nn.softplus(up_clamp_raw)
            g = jnp.clip(h[..., ::2], -gate_clamp, gate_clamp)
            u = jnp.clip(h[..., 1::2], -up_clamp, up_clamp)
            return g * jax.nn.sigmoid(g * alpha) * gate_scale * (u + up_shift)
        shape = x.shape
        xf = x.reshape(-1, shape[-1])
        h = xf @ shared_w1 + shared_b1
        t = swiglu5(h, shared_act[0], shared_act[1], shared_act[2], shared_act[3], shared_act[4])
        z = t @ shared_w2 + shared_b2
        gate_logits = xf @ gate_w + gate_b
        gate_probs = jax.nn.softmax(gate_logits, -1)
        w, idx = jax.lax.top_k(gate_probs, K)
        w = w / jnp.sum(w, axis=-1, keepdims=True)
        cw = jnp.sum(jax.nn.one_hot(idx, E, dtype=xf.dtype) * w[..., None], axis=1)
        he = jnp.einsum('nd,edh->enh', xf, expert_w1) + expert_b1[:, None, :]
        a = expert_act
        te = swiglu5(he, a[:, 0, None, None], a[:, 1, None, None], a[:, 2, None, None], a[:, 3, None, None], a[:, 4, None, None])
        oe = jnp.einsum('enh,ehd->end', te, expert_w2) + expert_b2[:, None, :]
        y = jnp.einsum('ne,end->nd', cw, oe)
        return (y + z).reshape(shape)

    def _L1_gnn_ref(x, edge_src, edge_dst, deg, W_self, W_neigh, bias, gamma, beta):
        import jax, jax.numpy as jnp
        import numpy as np
        N_NODES = 10000
        N_EDGES = 2500
        IN_DIM = 512
        OUT_DIM = 512
        LN_EPS = 1e-05
        n = x.shape[0]
        h_self = jnp.einsum('nd,od->no', x, W_self)
        neigh_sum = jax.ops.segment_sum(x[edge_src], edge_dst, num_segments=n)
        neigh_mean = neigh_sum / jnp.maximum(deg, 1.0)[:, None]
        h_neigh = jnp.einsum('nd,od->no', neigh_mean, W_neigh)
        h = h_self + h_neigh + bias
        mu = jnp.mean(h, axis=-1, keepdims=True)
        var = jnp.mean(jnp.square(h - mu), axis=-1, keepdims=True)
        h = (h - mu) * jax.lax.rsqrt(var + LN_EPS)
        return h * gamma + beta

    def _L1_ffn_ref(x, router_w, router_b, fc1_w, fc1_b, fc2_w, fc2_b):
        import jax, jax.numpy as jnp
        import numpy as np
        TOP_K = 2
        n_experts = router_w.shape[0]
        temp = 1.0
        logits = (jnp.einsum('btd,ed->bte', x, router_w) + router_b) / temp
        topk_val, topk_idx = jax.lax.top_k(logits, TOP_K)
        weights = jax.nn.softmax(topk_val, axis=-1)
        onehot = jax.nn.one_hot(topk_idx, n_experts, dtype=x.dtype)
        cw = jnp.einsum('btk,btke->bte', weights, onehot)
        h = jnp.einsum('btd,efd->btef', x, fc1_w) + fc1_b
        h1, h2 = jnp.split(h, 2, axis=-1)
        a = jax.nn.silu(h1) * h2
        y = jnp.einsum('bteh,edh->bted', a, fc2_w) + fc2_b
        out = jnp.einsum('bted,bte->btd', y, cw)
        return out

    def _L2_gnn_ref(node_feat, edge_feat, edge_index, n_nodes, W1, b1, W2, b2, W3, b3, gamma, beta):
        import jax, jax.numpy as jnp
        import numpy as np
        NODE_DIM, EDGE_DIM, HIDDEN, OUT = (512, 96, 1024, 512)
        N_NODES, N_EDGES = (50000, 12500)
        LN_EPS = 1e-05
        dst = edge_index[1]
        agg = jax.ops.segment_sum(edge_feat, dst, num_segments=n_nodes)
        inp = jnp.concatenate([node_feat, agg], axis=-1)
        h = jax.nn.relu(inp @ W1 + b1)
        h = jax.nn.relu(h @ W2 + b2)
        y = h @ W3 + b3
        mu = jnp.mean(y, axis=-1, keepdims=True)
        var = jnp.mean(jnp.square(y - mu), axis=-1, keepdims=True)
        return (y - mu) * jax.lax.rsqrt(var + LN_EPS) * gamma + beta

    def _L2_ffn_ref(x, Wg, bg, W1, b1, W2, b2):
        import jax, jax.numpy as jnp
        import numpy as np
        H = 512
        FF = 4 * H
        E = 8
        K = 2
        B, S = (4, 64)
        logits = x @ Wg + bg
        w, idx = jax.lax.top_k(logits, K)
        w = jax.nn.softmax(w, axis=-1)
        h = jax.nn.silu(jnp.einsum('bsh,ehf->ebsf', x, W1) + b1[:, None, None, :])
        y = jnp.einsum('ebsf,efh->ebsh', h, W2) + b2[:, None, None, :]
        comb = jnp.einsum('bske,bsk->ebs', jax.nn.one_hot(idx, E, dtype=x.dtype), w)
        return jnp.einsum('ebsh,ebs->bsh', y, comb)

    def _L3_gnn_ref(input, graph):
        import jax, jax.numpy as jnp
        import numpy as np
        N_FRAMES = 2048
        D_FEAT = 512
        N_SHOTS = 32
        SHOT_LEN = N_FRAMES // N_SHOTS
        n = input.shape[0]
        s = graph.shape[0]
        starts = graph[:, 0]
        counts = (graph[:, 1] - graph[:, 0] + 1).astype(input.dtype)
        seg_ids = jnp.searchsorted(starts, jnp.arange(n), side='right') - 1
        sums = jax.ops.segment_sum(input, seg_ids, num_segments=s)
        means = sums / counts[:, None]
        return means[seg_ids]

    def _L3_ffn_ref(x, gate_w, gate_b, w1, b1, w2, b2):
        import jax, jax.numpy as jnp
        import numpy as np
        B, S, H, E, K = (8, 64, 512, 8, 2)
        logits = jnp.einsum('bsh,he->bse', x, gate_w) + gate_b
        topk_vals, topk_idx = jax.lax.top_k(logits, K)
        topk_weights = jax.nn.softmax(topk_vals, axis=-1)
        mask = jax.nn.one_hot(topk_idx, E, dtype=topk_weights.dtype)
        weights = jnp.einsum('bske,bsk->bse', mask, topk_weights)
        h = jax.nn.relu(jnp.einsum('bsh,ehf->bsef', x, w1) + b1)
        expert_out = jnp.einsum('bsef,efh->bseh', h, w2) + b2
        return jnp.einsum('bseh,bse->bsh', expert_out, weights)
    edge_index = jnp.stack([src, dst])
    edge_index_t = jnp.stack([src, dst], axis=1)
    deg = jnp.maximum(jax.ops.segment_sum(jnp.ones(dst.shape, jnp.float32), dst, num_segments=625), 1.0)
    x = x + _L0_gnn_ref(_layernorm(x, axis=-1), edge_index_t, L0_gnn_W, L0_gnn_b, L0_gnn_a)
    x = x + _L0_ffn_ref(_layernorm(x, axis=-1)[None], L0_ffn_gate_w, L0_ffn_gate_b, L0_ffn_shared_w1, L0_ffn_shared_b1, L0_ffn_shared_w2, L0_ffn_shared_b2, L0_ffn_shared_act, L0_ffn_expert_w1, L0_ffn_expert_b1, L0_ffn_expert_w2, L0_ffn_expert_b2, L0_ffn_expert_act)[0]
    x = x + _L1_gnn_ref(_layernorm(x, axis=-1), src, dst, deg, L1_gnn_W_self, L1_gnn_W_neigh, L1_gnn_bias, L1_gnn_gamma, L1_gnn_beta)
    x = x + _L1_ffn_ref(_layernorm(x, axis=-1)[None], L1_ffn_router_w, L1_ffn_router_b, L1_ffn_fc1_w, L1_ffn_fc1_b, L1_ffn_fc2_w, L1_ffn_fc2_b)[0]
    x = x + _L2_gnn_ref(_layernorm(x, axis=-1), edge_attr_96, edge_index, 625, L2_gnn_W1, L2_gnn_b1, L2_gnn_W2, L2_gnn_b2, L2_gnn_W3, L2_gnn_b3, L2_gnn_gamma, L2_gnn_beta)
    x = x + _L2_ffn_ref(_layernorm(x, axis=-1)[None], L2_ffn_Wg, L2_ffn_bg, L2_ffn_W1, L2_ffn_b1, L2_ffn_W2, L2_ffn_b2)[0]
    x = x + _L3_gnn_ref(_layernorm(x, axis=-1), edge_index_t)
    x = x + _L3_ffn_ref(_layernorm(x, axis=-1)[None], L3_ffn_gate_w, L3_ffn_gate_b, L3_ffn_w1, L3_ffn_b1, L3_ffn_w2, L3_ffn_b2)[0]
    return x

_drawn_inputs = setup_inputs


def setup_inputs(seed=0):
    import zlib

    import numpy as np

    out = dict(_drawn_inputs(seed))
    spreads = {'L0_gnn_b': (0.0, 0.1),
     'L0_ffn_gate_b': (0.0, 0.1),
     'L0_ffn_shared_b1': (0.0, 0.1),
     'L0_ffn_shared_b2': (0.0, 0.1),
     'L0_ffn_expert_b1': (0.0, 0.566),
     'L0_ffn_expert_b2': (0.0, 0.1),
     'L1_gnn_bias': (0.0, 0.1),
     'L1_gnn_gamma': (1.0, 0.2),
     'L1_gnn_beta': (0.0, 0.1),
     'L1_ffn_router_b': (0.0, 0.666),
     'L1_ffn_fc1_b': (0.0, 0.8),
     'L1_ffn_fc2_b': (0.0, 0.412),
     'L2_gnn_gamma': (1.0, 0.2),
     'L2_gnn_beta': (0.0, 0.271),
     'L2_ffn_bg': (0.0, 0.994),
     'L2_ffn_b1': (0.0, 1.587),
     'L2_ffn_b2': (0.0, 0.578)}
    factors = {'L0_ffn_expert_w1': 2.945,
     'L1_ffn_router_w': 2.824,
     'L1_ffn_fc1_w': 6.296,
     'L1_ffn_fc2_w': 5.879,
     'L2_gnn_b1': 15.634,
     'L3_ffn_gate_w': 6.591,
     'L3_ffn_gate_b': 8.0,
     'L3_ffn_w1': 6.993,
     'L3_ffn_b1': 23.307,
     'L3_ffn_w2': 5.635,
     'L3_ffn_b2': 64.0,
     'L2_gnn_b2': 3.766,
     'L2_ffn_Wg': 3.961,
     'L2_ffn_W1': 3.13}
    for name, (base, spread) in spreads.items():
        noise = np.random.default_rng([zlib.crc32(name.encode()), seed]).standard_normal(out[name].shape)
        drawn = base * np.exp(spread * noise) if base else spread * noise
        out[name] = jnp.asarray(drawn.astype(out[name].dtype))
    for name, factor in factors.items():
        out[name] = (out[name] * factor).astype(out[name].dtype)
    return out
```

```python
from contextlib import ExitStack

import concourse.bass as bass
from concourse import mybir

F32 = mybir.dt.float32
BF = mybir.dt.bfloat16
F16 = mybir.dt.float16
I32 = mybir.dt.int32
U32 = mybir.dt.uint32
ALU = mybir.AluOpType
ACT = mybir.ActivationFunctionType
AX = mybir.AxisListType

N, D, P, TP, TC = 625, 512, 128, 125, 5
NE, EC = 10625, 85
DC = D // P
SLOTW, NSLOT = 4128, 7
CH, NCH = 128, 5
FAR = 1 << 20
WORK = 10944


class Eng:

    def __init__(self, sem):
        self.sem, self.n, self.ops, self.seen, self.stack = sem, 0, [], {}, []

    def wait(self, *tokens):
        for t in tokens:
            if t is None:
                continue
            if isinstance(t, list):
                self.wait(*t)
                continue
            sem, v = t
            if v > 0 and self.seen.get(sem.name, 0) < v:
                self.seen[sem.name] = v
                self.ops.append(("wait", sem, v))

    def do(self, fn, *tokens, sig=True):
        self.wait(*tokens)
        if sig:
            self.n += 1
        self.ops.append(("do", fn, self.sem if sig else None, 1))
        return (self.sem, self.n) if sig else None

    def dma(self, d, fn, *tokens):
        self.wait(*tokens)
        d.n += 16
        self.ops.append(("do", fn, d.sem, 16))
        return (d.sem, d.n)

    def begin(self, e, k, dmas):
        self.stack.append((e, k, self.ops, self.n, dict(self.seen), [(d, d.n) for d in dmas]))
        self.ops = []

    def end(self):
        e, k, outer, n, seen, dmas = self.stack.pop()
        outer.append(("if", e, k, self.ops, self.n - n, [(d, v, d.n - v) for d, v in dmas]))
        self.ops, self.seen = outer, seen

    def emit(self, eng, ops=None, regs=None):
        regs = {} if regs is None else regs
        for op in self.ops if ops is None else ops:
            if op[0] == "wait":
                eng.wait_ge(op[1], op[2])
            elif op[0] == "do":
                ins = op[1](eng)
                if op[2] is not None:
                    ins.then_inc(op[2], op[3])
            elif op[0] == "count":
                regs[op[1]] = eng.value_load(op[2], min_val=0, max_val=N)
            else:
                _, e, k, body, inc, dmas = op
                with eng.If(regs[e] > CH * k):
                    self.emit(eng, body, regs)
                with eng.Else():
                    for d, before, more in dmas:
                        if more:
                            eng.wait_ge(d.sem, before)
                            eng.sem_inc(d.sem, more)
                    if inc:
                        eng.drain().then_inc(self.sem, inc)


class Dma:
    def __init__(self, sem):
        self.sem, self.n = sem, 0


def program(nc, I, out):
    ctx = ExitStack()
    with ctx:
        def sb(name, shape, dt=F32):
            return ctx.enter_context(nc.sbuf_tensor(name, shape, dt))

        def sem(name):
            return ctx.enter_context(nc.semaphore(name))

        def dram(name, shape, dt=F32):
            return nc.dram_tensor(name, shape, dt, kind="Internal").ap()

        pe, act, dve, pool, sp = (Eng(sem("s_" + n)) for n in ("pe", "act", "dve", "pool", "sp"))
        bank = [ctx.enter_context(nc.psum_tensor(f"bank{i}", [P, 512], F32)) for i in range(8)]
        free = [None] * 8

        ring = sb("ring", [P, NSLOT * SLOTW])
        W = sb("work", [P, WORK])
        x = sb("x", [TP, TC, D])
        xn = sb("xn", [TP, TC, D])
        xnT = sb("xnT", [P, DC, N])
        ident = sb("ident", [P, P])
        onesf = sb("onesf", [P, P])
        onesb = sb("onesb", [P, P], BF)
        upper = sb("upper", [P, P], BF)
        iota = sb("iota", [P, N], F16)
        iotaE = sb("iotaE", [P, 16])
        tok = sb("tok", [TP, TC], I32)
        tokf = sb("tokf", [TP, TC])
        eps = sb("eps", [P, 1])
        gate = sb("gate", [P, 4, DC, 16])
        gbias = sb("gbias", [P, 4, 16])
        b1 = [sb(f"b1_{i}", [P, n]) for i, n in enumerate((17 * 6, 8 * 16, 8 * 16, 8 * 8))]
        gb1 = sb("gb1", [P, 16])
        actp = sb("actp", [P, 17, 5])
        spl = sb("spl", [P, 17, 5])
        spt = sb("spt", [P, 17, 5])
        ngc = sb("ngc", [P, 17, 5])
        b2 = sb("b2", [16, D])
        b2s = sb("b2s", [1, D])
        cwT = sb("cwT", [16, N])
        aggT = sb("aggT", [96, N])
        stats = sb("stats", [TP, TC, 6])
        mv = sb("mv", [TP, TC, 2])
        rstd = sb("rstd", [TP, TC])
        nmr = sb("nmr", [TP, TC])
        lg = sb("lg", [TP, TC, 16])
        mx = sb("mx", [TP, TC, 8])
        ix = sb("ix", [TP, TC, 8], U32)
        ixf = sb("ixf", [TP, 2, TC])
        s12 = sb("s12", [TP, 2 * TC, 16])
        t12 = sb("t12", [TP, 2 * TC, 16])
        sel = sb("sel", [TP, TC * 16], BF)
        rk = sb("rk", [TP, 2, TC])
        kk = sb("kk", [TP, 4, 2 * TC])
        qi = sb("qi", [TP, 2, TC], I32)
        dw = sb("dw", [TP, TC])
        wt = sb("wt", [TP, 2, TC])
        cw = sb("cw", [TP, TC, 16])
        cnt = sb("cnt", [1, 16], I32)
        idx = sb("idx", [P, 80], I32)
        far = sb("far", [P, 80], I32)
        seg = sb("seg", [TP, 12, TC])
        segi = sb("segi", [TP, 4, TC], I32)
        esrc = sb("esrc", [TP, 2, EC], I32)
        ef = sb("ef", [TP, 2, EC])
        sT = sb("sT", [TP, 4, TC])

        Y = dram("ybuf", [P * 80, D])
        xnd = dram("xnd", [N, D])
        tab = [dram(f"tab{i}", [P * n * NCH, 1], I32) for i, n in enumerate((16, 8, 8, 8))]

        d_in = Dma(sem("d_in"))
        d_x = Dma(sem("d_x"))
        d_e = Dma(sem("d_e"))
        d_z = Dma(sem("d_z"))
        d_v = Dma(sem("d_v"))
        d_b2 = Dma(sem("d_b2"))
        d_xn = Dma(sem("d_xn"))
        d_idx = Dma(sem("d_idx"))
        d_y = [Dma(sem(f"d_y{i}")) for i in range(2)]
        d_sc = Dma(sem("d_sc"))
        d_g = [Dma(sem(f"d_g{i}")) for i in range(6)]
        d_c = [Dma(sem(f"d_c{i}")) for i in range(10)]
        d_s = Dma(sem("d_s"))
        d_out = Dma(sem("d_out"))
        d_r = [Dma(sem(f"d_r{i}")) for i in range(NSLOT)]

        loads = []

        def plan(src, parts, words):
            loads.append((src, parts, words))
            return len(loads) - 1

        landed = {}

        def load(n, *tokens):
            if n >= len(loads):
                return
            src, parts, words = loads[n]
            s = n % NSLOT
            dst = ring[0:parts, s * SLOTW:s * SLOTW + words]
            landed[n] = sp.dma(d_r[s], lambda e: e.dma_start(dst, src), *tokens)

        def slot(n):
            _, parts, words = loads[n]
            s = n % NSLOT
            return ring[0:parts, s * SLOTW:s * SLOTW + words]

        def release(n, token):
            load(n + NSLOT, token)

        w_l0g = plan(I["L0_gnn_W"], P, 2048)
        w_sh1 = plan(I["sh_w1"], P, 3072)
        w_sh2 = plan(I["sh_w2"], P, 1536)
        w_l0 = []
        for e in range(0, 16, 2):
            a = plan(I["L0_w1"][e], P, 3072)
            c = plan(I["L0_w2"][e // 2], P, 3072)
            b = plan(I["L0_w1"][e + 1], P, 3072)
            w_l0 += [(a, c), (b, c)]
        w_l1g = plan(I["L1_gnn_W"], P, 4096)
        w_ea = [plan(I["ea0"], TP, 42 * 96), plan(I["ea1"], TP, 43 * 96)]
        w_l1 = [[plan(I["L1_w1"][e, 0], P, 4096), plan(I["L1_w1"][e, 1], P, 4096),
                 plan(I["L1_w2"][e], P, 4096)] for e in range(8)]
        w_l2g = [plan(I["L2_gnn_W1a"], P, 4096), plan(I["L2_gnn_W1b"], 96, 1024),
                 plan(I["L2_gnn_W2"][0], P, 4096), plan(I["L2_gnn_W2"][1], P, 4096),
                 plan(I["L2_gnn_W3"], P, 4096)]
        w_l2 = [[plan(I["L2_w1"][e, 0], P, 4096), plan(I["L2_w1"][e, 1], P, 4096),
                 plan(I["L2_w2"][e, 0], P, 4096), plan(I["L2_w2"][e, 1], P, 4096)] for e in range(8)]
        w_l3 = [[plan(I["L3_w1"][e], P, 4096), plan(I["L3_w2"][e], P, 4096)] for e in range(8)]

        x_in = I["x"].rearrange("(c p) d -> p c d", p=TP)
        out_v = out.rearrange("(c p) d -> p c d", p=TP)
        xnd_v = xnd.rearrange("(c p) d -> p c d", p=TP)
        for a, b in ((0, 120), (120, 125)):
            t_x = sp.dma(d_x, lambda e, a=a, b=b: e.dma_start(x[a:b], x_in[a:b]))
        for i, nm in enumerate(("src", "dst")):
            v = I[nm].rearrange("(p c) -> p c", p=TP)
            t_e = act.dma(d_e, lambda e, i=i, v=v: e.dma_start(esrc[:, i, :], v))
        load(0)
        vec = lambda i: W[0:TP, WORK - 1536 + 512 * i:WORK - 1024 + 512 * i]

        def load_vecs(names, *tokens):
            for i, nm in enumerate(names):
                v = I[nm].to_broadcast([TP, D])
                t = act.dma(d_v, lambda e, i=i, v=v: e.dma_start(vec(i), v), *tokens)
            return t

        for i, (nm, E) in enumerate((("L0", 16), ("L1", 8), ("L2", 8), ("L3", 8))):
            t_in = act.dma(d_in, lambda e, i=i, nm=nm, E=E: e.dma_start(gate[:, i, :, 0:E], I[nm + "_gate"]))
            t_in = act.dma(d_in, lambda e, i=i, nm=nm, E=E: e.dma_start(
                gbias[:, i, 0:E], I[nm + "_gb"].to_broadcast([P, E])))
            t_in = act.dma(d_in, lambda e, i=i, nm=nm: e.dma_start(b1[i][:, :], I[nm + "_b1"]))
        t_in = act.dma(d_in, lambda e: e.dma_start(gb1[:, :], I["L2_gnn_b"]))
        t_in = act.dma(d_in, lambda e: e.dma_start(b2s[:, :], I["sh_b2"]))
        t_in = act.dma(d_in, lambda e: e.dma_start(actp[:, :, :].rearrange("p a b -> p (a b)"),
                                                   I["act"].to_broadcast([P, 85])))
        t_vec = load_vecs(("L0_gnn_b", "L0_a_src", "L0_a_dst"))
        for n in range(1, NSLOT):
            load(n)

        t = pool.do(lambda e: e.memset(ident[:, :], 0.0))
        t_id = pool.do(lambda e: e.affine_select(out=ident[:, :], in_=ident[:, :], compare_op=ALU.not_equal,
                                                 fill=1.0, base=0, pattern=[[-1, P]], channel_multiplier=1), t)
        t_io = pool.do(lambda e: e.iota(iota[:, :], [[1, N]], base=0, channel_multiplier=0,
                                        allow_small_or_imprecise_dtypes=True))
        t_ones = dve.do(lambda e: e.memset(onesf[:, :], 1.0))
        t_onesb = dve.do(lambda e: e.memset(onesb[:, :], 1.0))
        t_eps = dve.do(lambda e: e.memset(eps[:, :], 1e-5))
        pool.do(lambda e: e.iota(iotaE[:, :], [[1, 16]], base=0, channel_multiplier=0,
                                 allow_small_or_imprecise_dtypes=True))
        pool.do(lambda e: e.iota(tok[:, :], [[TP, TC]], base=0, channel_multiplier=1))
        t_tokf = pool.do(lambda e: e.iota(tokf[:, :], [[TP, TC]], base=0, channel_multiplier=1,
                                          allow_small_or_imprecise_dtypes=True))
        pool.do(lambda e: e.memset(far[:, :], FAR))
        t = pool.do(lambda e: e.affine_select(out=upper[:, :], in_=onesb[:, :], compare_op=ALU.is_gt, fill=0.0,
                                              base=0, pattern=[[1, P]], channel_multiplier=-1), t_onesb)
        ZW = 1280
        zero = W[:, 8128:8128 + ZW]
        t_zero = pool.do(lambda e: e.memset(zero, 0.0))
        t_pc = t_zero
        for i in range(4):
            n = (16, 8, 8, 8)[i] * NCH
            t_z = act.dma(d_z, lambda e, i=i, n=n: e.dma_start(
                tab[i].rearrange("(p n) o -> p (n o)", p=P), far[:, 0:n]), t_pc)
        Yz = Y.rearrange("(p j) d -> p (j d)", p=P)
        for i in range(80 * D // ZW):
            t_z = act.dma(d_z, lambda e, i=i: e.dma_start(Yz[:, i * ZW:(i + 1) * ZW], zero))

        qf, low, high, d_, mid, val, g_, u_ = (seg[:, i, :] for i in range(8))
        mi = segi[:, 0, :]
        vi = segi[:, 1, :]
        src_g = I["src"].rearrange("(n o) -> n o", o=1)
        dst_g = I["dst"].rearrange("(n o) -> n o", o=1)

        def gather5(dst_t, src_ap, idx_t, *tokens):
            for c in range(TC):
                t = pool.dma(d_s, lambda e, c=c: e.indirect_dma_start(
                    out=dst_t[:, c:c + 1], out_offset=None, in_=src_ap,
                    in_offset=bass.IndirectOffsetOnAxis(ap=idx_t[:, c:c + 1], axis=0)), *tokens)
            return t

        def search_steps(levels, t):
            if t is None:
                pool.do(lambda e: e.memset(low, 0.0))
                t = pool.do(lambda e: e.memset(high, float(NE)))
            for _ in range(levels):
                t = pool.do(lambda e: e.tensor_tensor(d_, high, low, ALU.subtract), t)
                t = pool.do(lambda e: e.tensor_scalar(d_, d_, 0.5, -0.25, ALU.mult, ALU.add), t)
                t = pool.do(lambda e: e.tensor_scalar(d_, d_, 8388608.0, -8388608.0, ALU.add, ALU.add), t)
                t = pool.do(lambda e: e.tensor_tensor(mid, low, d_, ALU.add), t)
                t = pool.do(lambda e: e.tensor_copy(mi, mid), t)
                t = gather5(vi, src_g, mi, t)
                t = pool.do(lambda e: e.tensor_copy(val, vi), t)
                t = pool.do(lambda e: e.tensor_tensor(val, tokf[:, :], val, ALU.subtract), t)
                t = pool.do(lambda e: e.tensor_scalar(g_, val, 0.0, None, ALU.is_lt), t)
                pool.do(lambda e: e.tensor_tensor(u_, low, mid, ALU.subtract), t)
                t = pool.do(lambda e: e.tensor_tensor(d_, mid, high, ALU.subtract), t)
                pool.do(lambda e: e.tensor_tensor(u_, u_, g_, ALU.mult), t)
                t = pool.do(lambda e: e.tensor_tensor(d_, d_, g_, ALU.mult), t)
                pool.do(lambda e: e.tensor_tensor(low, mid, u_, ALU.add), t)
                t = pool.do(lambda e: e.tensor_tensor(high, high, d_, ALU.add), t)
            return t

        sg, gg, cs = seg[:, 8, :], seg[:, 9, :], seg[:, 10, :]

        def search_end(t):
            t = pool.do(lambda e: e.tensor_scalar(sg, high, 1.0, -1.0, ALU.mult, ALU.add), t)
            t = pool.do(lambda e: e.tensor_scalar(g_, sg, 0.0, None, ALU.is_lt), t)
            t = pool.do(lambda e: e.tensor_scalar(g_, g_, float(NE), 0.0, ALU.mult, ALU.add), t)
            t = pool.do(lambda e: e.tensor_tensor(gg, sg, g_, ALU.add), t)
            t = pool.do(lambda e: e.tensor_copy(mi, gg), t)
            gather5(segi[:, 2, :], src_g, mi, t)
            t = gather5(segi[:, 3, :], dst_g, mi, t)
            t = pool.do(lambda e: e.tensor_copy(cs, segi[:, 3, :]), t)
            t = pool.do(lambda e: e.tensor_copy(seg[:, 11, :], segi[:, 2, :]), t)
            t = pool.do(lambda e: e.tensor_tensor(cs, cs, seg[:, 11, :], ALU.subtract), t)
            return pool.do(lambda e: e.tensor_scalar(cs, cs, 1.0, 1.0, ALU.mult, ALU.add), t)

        t_seg = search_end(search_steps(14, None))

        xt = [t_x] * TC
        xn_free = []
        xnT_free = []

        def layernorm(after_bank0=0):
            for c in range(TC):
                t = dve.do(lambda e, c=c: e.bn_stats(stats[:, c, :], x[:, c, :]), xt[c], t_eps)
                t = dve.do(lambda e, c=c: e.bn_aggr(mv[:, c, :], stats[:, c, :]), t)
            t = act.do(lambda e: e.activation(rstd[:, :], mv[:, :, 1], ACT.Sqrt, bias=eps[0:TP, :]), t, xn_free)
            t = dve.do(lambda e: e.reciprocal(rstd[:, :], rstd[:, :]), t)
            t = dve.do(lambda e: e.scalar_tensor_tensor(nmr[:, :], mv[:, :, 0], -1.0, rstd[:, :], ALU.mult, ALU.mult), t)
            ts = []
            for c in range(TC):
                if c % 2 == 0:
                    ts.append(dve.do(lambda e, c=c: e.tensor_scalar(
                        xn[:, c, :], x[:, c, :], rstd[:, c:c + 1], nmr[:, c:c + 1], ALU.mult, ALU.add), t, xn_free))
                else:
                    ts.append(act.do(lambda e, c=c: e.activation(
                        xn[:, c, :], x[:, c, :], ACT.Identity, bias=nmr[:, c:c + 1], scale=rstd[:, c:c + 1]), t, xn_free))
            xn_free.clear()
            tT = []
            for c in range(TC):
                for d in range(DC):
                    t = pe.do(lambda e, c=c, d=d: e.transpose(
                        bank[c][:, d * TP:(d + 1) * TP], xn[:, c, d * P:(d + 1) * P], ident[0:TP, 0:TP]),
                        ts[c], t_id, free[c], sig=d == DC - 1)
                src = bank[c][:, 0:DC * TP].rearrange("p (d t) -> p d t", d=DC)
                dst = xnT[:, :, c * TP:(c + 1) * TP]
                if c % 2 == 0:
                    t = act.do(lambda e, s=src, d=dst: e.activation(d, s, ACT.Copy), t, xnT_free)
                else:
                    t = dve.do(lambda e, s=src, d=dst: e.tensor_copy(d, s), t, xnT_free)
                free[c] = t
                tT.append(t)
            xnT_free.clear()
            xn_free.append((pe.sem, pe.n))
            return ts, tT

        def rows_out(psum, c, t):
            return dve.do(lambda e: e.tensor_tensor(x[:, c, :], x[:, c, :], psum, ALU.add), t, xt[c])

        GT = [W[:, 3125 + 512 * i:3637 + 512 * i] for i in range(6)]
        XG = W[:, 6197:6709]
        YT = [W[:, 6709 + 512 * i:7221 + 512 * i] for i in range(2)]
        HT = W[:, 7733:7733 + 2048]
        TMP = W[:, 9781:9781 + 1152]
        CMB = [W[0:TP, 3125 + 512 * i:3637 + 512 * i] for i in range(6)] + \
              [W[0:TP, 7733 + 512 * i:8245 + 512 * i] for i in range(4)]
        mem = {"gt": [None] * 6, "yt": [None] * 2, "work": t_z, "b2": None}

        def moe(L, E, b2_src, expert, between, extra_bias):
            K = E * NCH
            t_b2 = act.dma(d_b2, lambda e: e.dma_start(b2[0:E, :], b2_src), mem["b2"])
            ts, tT = layernorm()
            t_xnd = None
            for a, b in ((0, 120), (120, 125)):
                t_xnd = act.dma(d_xn, lambda e, a=a, b=b: e.dma_start(xnd_v[a:b], xn[a:b]), ts)
            xn_free.append(t_xnd)
            lgp = bank[5][0:TP, 0:TC * E]
            for c in range(TC):
                for d in range(DC):
                    t = pe.do(lambda e, c=c, d=d: e.matmul(
                        lgp[:, c * E:(c + 1) * E], xnT[:, d, c * TP:(c + 1) * TP], gate[:, L, d, 0:E],
                        start=d == 0, stop=d == DC - 1), tT[c], t_in, free[5], sig=c == TC - 1 and d == DC - 1)
            lgv = lg[:, :, 0:E]
            t = dve.do(lambda e: e.tensor_tensor(
                lgv, lgp.rearrange("p (c e) -> p c e", e=E),
                gbias[0:TP, L:L + 1, 0:E].to_broadcast([TP, TC, E]), ALU.add), t, t_in)
            free[5] = t
            for c in range(TC):
                t2 = dve.do(lambda e, c=c: e.max(mx[:, c, :], lg[:, c, 0:E]), t)
            for c in range(TC):
                t2 = dve.do(lambda e, c=c: e.max_index(ix[:, c, :], mx[:, c, :], lg[:, c, 0:E]), t2)
            tw = dve.do(lambda e: e.tensor_tensor(dw[:, :], mx[:, :, 0], mx[:, :, 1], ALU.subtract))
            act.do(lambda e: e.activation(wt[:, 0, :], dw[:, :], ACT.Sigmoid), tw)
            tw = act.do(lambda e: e.activation(wt[:, 1, :], dw[:, :], ACT.Sigmoid, scale=-1.0))
            t = dve.do(lambda e: e.tensor_copy(ixf[:, :, :], ix[:, :, 0:2].rearrange("p c k -> p k c")), t2)
            ixv = ixf[:, :, :].rearrange("p k c -> p (k c)")
            sv, tv = s12[:, :, 0:E], t12[:, :, 0:E]
            t_s = dve.do(lambda e: e.tensor_tensor(
                sv, iotaE[0:TP, 0:E].rearrange("p (o e) -> p o e", o=1).to_broadcast([TP, 2 * TC, E]),
                ixv.rearrange("p (k o) -> p k o", o=1).to_broadcast([TP, 2 * TC, E]), ALU.is_equal), t, t_pc)
            sel_v = sel[:, 0:TC * E].rearrange("p (c e) -> p c e", e=E)
            t = dve.do(lambda e: e.tensor_tensor(sel_v, s12[:, 0:TC, 0:E], s12[:, TC:2 * TC, 0:E], ALU.add), t_s)
            rkp = bank[6][0:TP, 0:TC * E]
            pe.do(lambda e: e.matmul(rkp, upper[0:TP, 0:TP], sel[:, 0:TC * E], start=True, stop=True, skip_group_check=True),
                  t, free[6], t_pc, sig=False)
            for s in range(1, TC):
                tr = pe.do(lambda e, s=s: e.matmul(rkp[:, s * E:], onesb[0:TP, 0:TP], sel[:, 0:(TC - s) * E],
                                                   start=False, stop=True, skip_group_check=True),
                           t_onesb, sig=s == TC - 1)
            ctp = bank[7][0:TP, 0:E]
            for c in range(TC):
                tc = pe.do(lambda e, c=c: e.matmul(ctp, onesb[0:TP, 0:TP], sel[:, c * E:(c + 1) * E],
                                                   start=c == 0, stop=c == TC - 1), free[7], sig=c == TC - 1)
            t = dve.do(lambda e: e.tensor_tensor(
                t12[:, :, 0:E].rearrange("p (k c) e -> p k c e", k=2)[:, 0],
                s12[:, 0:TC, 0:E], rkp.rearrange("p (c e) -> p c e", e=E), ALU.mult), tr)
            t = dve.do(lambda e: e.tensor_tensor(
                t12[:, TC:2 * TC, 0:E], s12[:, TC:2 * TC, 0:E],
                rkp.rearrange("p (c e) -> p c e", e=E), ALU.mult))
            free[6] = t
            rv = rk[:, :, :].rearrange("p k c -> p (k c)")
            t = dve.do(lambda e: e.tensor_reduce(rv, tv, AX.X, ALU.add), t)
            k0, k1, k2, k3 = (kk[:, i, :] for i in range(4))
            t = dve.do(lambda e: e.tensor_scalar(k0, rv, float(CH), None, ALU.is_ge), t)
            for j in range(2, NCH):
                a, b = (k0, k1) if j % 2 == 0 else (k1, k0)
                t = dve.do(lambda e, a=a, b=b, j=j: e.scalar_tensor_tensor(
                    b, rv, float(CH * j), a, ALU.is_ge, ALU.add), t)
            kf = k1 if (NCH - 2) % 2 == 1 else k0
            t = dve.do(lambda e: e.tensor_scalar(k2, rv, float(K), None, ALU.mult), t)
            t = dve.do(lambda e: e.scalar_tensor_tensor(k3, ixv, float(NCH), k2, ALU.mult, ALU.add), t)
            t = dve.do(lambda e: e.scalar_tensor_tensor(k2, kf, 1.0 - CH * K, k3, ALU.mult, ALU.add), t)
            t_q = dve.do(lambda e: e.tensor_copy(qi[:, :, :].rearrange("p k c -> p (k c)"), k2), t)
            t_cnt = dve.do(lambda e: e.tensor_copy(cnt[0:1, 0:E], ctp[0:1, :]), tc)
            free[7] = t_cnt
            for k in range(2):
                for c in range(TC):
                    t_sc = pool.dma(d_sc, lambda e, k=k, c=c: e.indirect_dma_start(
                        out=tab[L], out_offset=bass.IndirectOffsetOnAxis(ap=qi[:, k, c:c + 1], axis=0),
                        in_=tok[:, c:c + 1], in_offset=None), t_q, t_z, t_pc)
            t_idx = act.dma(d_idx, lambda e: e.dma_start(
                idx[:, 0:K], tab[L].rearrange("(p n) o -> p (n o)", p=P)), t_sc)
            t = dve.do(lambda e: e.tensor_tensor(
                tv, sv, wt[:, :, :].rearrange("p k (c o) -> p (k c) o", o=1).to_broadcast([TP, 2 * TC, E]), ALU.mult), tw)
            t = dve.do(lambda e: e.tensor_tensor(cw[:, :, 0:E], t12[:, 0:TC, 0:E], t12[:, TC:2 * TC, 0:E], ALU.add), t)
            for c in range(TC):
                b, o = (6, c * TP) if c < 4 else (7, 0)
                tt = pe.do(lambda e, c=c, b=b, o=o: e.transpose(
                    bank[b][0:E, o:o + TP], cw[:, c, 0:E], ident[0:TP, 0:TP]), t, free[b])
                if c == 3:
                    t6 = act.do(lambda e: e.activation(cwT[0:E, 0:4 * TP], bank[6][0:E, 0:4 * TP], ACT.Copy), tt)
            t7 = act.do(lambda e: e.activation(cwT[0:E, 4 * TP:N], bank[7][0:E, 0:TP], ACT.Copy), tt)
            free[6], free[7] = t6, t7
            between(tT)
            for c in range(TC):
                last = not extra_bias
                t = pe.do(lambda e, c=c, last=last: e.matmul(
                    bank[c][0:TP, :], cwT[0:E, c * TP:(c + 1) * TP], b2[0:E, :], start=True, stop=last),
                    free[c], t7, t_b2, sig=last)
                if extra_bias:
                    t = extra_bias(c)
                xt[c] = free[c] = rows_out(bank[c][0:TP, :], c, t)
            mem["b2"] = (pe.sem, pe.n)
            xnT_free.append((pe.sem, pe.n))

            Yv = Y[0:P * K, :].rearrange("(p j) d -> p j d", j=K)
            for e_ in range(E):
                for k in range(NCH):
                    engs = (pe, act, dve)
                    v = e_ * NCH + k
                    b = e_ % 2 if k == 0 else k + 1
                    t_g = pool.dma(d_g[b], lambda e, v=v, b=b: e.indirect_dma_start(
                        out=GT[b], out_offset=None, in_=xnd,
                        in_offset=bass.IndirectOffsetOnAxis(ap=idx[:, v:v + 1], axis=0),
                        bounds_check=N - 1, oob_is_err=False), t_idx, t_xnd, mem["gt"][b], (d_g[b].sem, d_g[b].n), mem["work"])
                    if k == 1:
                        for en in engs:
                            en.wait(t_cnt)
                            en.ops.append(("count", (L, e_), cnt[0:1, e_:e_ + 1]))
                    if k >= 1:
                        for en in engs:
                            en.begin((L, e_), k, d_y if en is act else ())
                    for d in range(DC):
                        t = pe.do(lambda e, d=d, b=b: e.transpose(
                            bank[0][:, d * P:(d + 1) * P], GT[b][:, d * P:(d + 1) * P], ident[:, :]),
                            t_g, free[0], sig=d == DC - 1)
                    mem["gt"][b] = t
                    t = dve.do(lambda e: e.tensor_copy(XG, bank[0][:, :]), t, mem["work"])
                    free[0] = t
                    yb = 1 + v % 2
                    t = expert(e_, k, yb, t)
                    yt = YT[v % 2]
                    t = act.do(lambda e, yb=yb, yt=yt: e.activation(yt, bank[yb][:, :], ACT.Copy),
                               t, mem["yt"][v % 2], mem["work"])
                    free[yb] = t
                    mem["yt"][v % 2] = act.dma(d_y[v % 2], lambda e, v=v, yt=yt: e.dma_start(Yv[:, v, :], yt), t, t_z)
                for en in engs:
                    for k in range(1, NCH):
                        en.end()
                done(e_)
            t_y = list(mem["yt"])
            t_last = [(pe.sem, pe.n)] + [(d.sem, d.n) for d in d_g]
            t_c = []
            for c in range(TC):
                for k in range(2):
                    i = 2 * c + k
                    t_c.append(pool.dma(d_c[i], lambda e, i=i, c=c, k=k: e.indirect_dma_start(
                        out=CMB[i], out_offset=None, in_=Y[0:P * K, :],
                        in_offset=bass.IndirectOffsetOnAxis(ap=qi[:, k, c:c + 1], axis=0)), t_y, t_last))
            for c in range(TC):
                for k in range(2):
                    i = 2 * c + k
                    xt[c] = dve.do(lambda e, i=i, c=c, k=k: e.scalar_tensor_tensor(
                        x[:, c, :], CMB[i], wt[:, k, c:c + 1], x[:, c, :], ALU.mult, ALU.add), t_c[i], xt[c], tw)
            mem["work"] = xt[TC - 1]
            mem["gt"] = [xt[TC - 1]] * 6

        def done(e_):
            pass

        A = W[0:TP, 0:3125]
        AT = W[0:TP, 3125:6250].rearrange("p (c i) -> p c i", c=TC)
        ts, tT = layernorm()
        tef = dve.do(lambda e: e.tensor_copy(ef[:, :, :], esrc[:, :, :]), t_e)
        OH = W[0:TP, 6250:6250 + 6 * 313].bitcast(BF)
        oh_free = [None] * 3
        for c in range(EC):
            b = c % 3
            oh = [OH[:, (2 * b + i) * 626:(2 * b + i) * 626 + N] for i in range(2)]
            for i in range(2):
                t = dve.do(lambda e, i=i, c=c, oh=oh: e.tensor_scalar(
                    oh[i], iota[0:TP, :], ef[:, i, c:c + 1], None, ALU.is_equal), tef, t_io, oh_free[b])
            for m in range(TC):
                lhs = oh[1][:, m * TP:(m + 1) * TP]
                bb, o = (5, 113 * m) if m < 4 else (6, 0)
                pe.do(lambda e, m=m, lhs=lhs, c=c, oh=oh: e.matmul(
                    bank[m][0:TP, :], lhs, oh[0][:, 0:512], start=c == 0, stop=c == EC - 1),
                    t, free[m], free[5], free[6], sig=False)
                t_A = pe.do(lambda e, m=m, lhs=lhs, c=c, oh=oh, bb=bb, o=o: e.matmul(
                    bank[bb][0:TP, o:o + 113], lhs, oh[0][:, 512:N], start=c == 0 and m in (0, 4),
                    stop=c == EC - 1, skip_group_check=True), sig=m == TC - 1)
            oh_free[b] = t_A
        for m in range(TC):
            t = act.do(lambda e, m=m: e.activation(AT[:, m, 0:512], bank[m][0:TP, :], ACT.Copy), t_A)
            free[m] = t
        t_at = dve.do(lambda e: e.tensor_copy(
            AT[:, 0:4, 512:N], bank[5][0:TP, 0:452].rearrange("p (m i) -> p m i", m=4)), t_A)
        t_at2 = dve.do(lambda e: e.tensor_copy(AT[:, 4, 512:N], bank[6][0:TP, 0:113]))
        free[5], free[6] = t_at, t_at2
        t_Atr = []
        ats = [t, t_at, t_at2]
        for g in range(7):
            n = min(4, 25 - 4 * g)
            for j in range(n):
                f = 4 * g + j
                a, b = f // 5, f % 5
                t = pe.do(lambda e, g=g, j=j, a=a, b=b: e.transpose(
                    bank[g][0:TP, j * TP:(j + 1) * TP], AT[:, b, a * TP:(a + 1) * TP], ident[0:TP, 0:TP]),
                    ats, free[g], sig=j == n - 1)
            if g % 2:
                free[g] = act.do(lambda e, g=g, n=n: e.activation(
                    A[:, 500 * g:500 * g + n * TP], bank[g][0:TP, 0:n * TP], ACT.Copy), t)
            else:
                free[g] = dve.do(lambda e, g=g, n=n: e.tensor_copy(
                    A[:, 500 * g:500 * g + n * TP], bank[g][0:TP, 0:n * TP]), t)
        t_Adone = [free[5], free[6]]
        t_Atr = t

        emb = W[0:TP, 6250:6250 + 2560].rearrange("p (c d) -> p c d", c=TC)
        wg0 = slot(w_l0g).rearrange("p (k d) -> p k d", k=DC)
        temb = []
        for c in range(TC):
            for d in range(DC):
                t = pe.do(lambda e, c=c, d=d: e.matmul(
                    bank[c][0:TP, :], xnT[:, d, c * TP:(c + 1) * TP], wg0[:, d, :], start=d == 0, stop=d == DC - 1),
                    tT[c], landed[w_l0g], free[c], sig=d == DC - 1)
            t = dve.do(lambda e, c=c: e.tensor_tensor(emb[:, c, :], bank[c][0:TP, :], vec(0), ALU.add), t, t_vec, t_z)
            free[c] = t
            temb.append(t)
        release(w_l0g, (pe.sem, pe.n))
        xnT_free.append((pe.sem, pe.n))
        scr = W[0:TP, 8810:8810 + 512]
        ttr = None
        for c in range(TC):
            for i in range(2):
                ttr = dve.do(lambda e, c=c, i=i: e.tensor_tensor_reduce(
                    scr, emb[:, c, :], vec(1 + i), 1.0, 0.0, ALU.mult, ALU.add, sT[:, i, c:c + 1]),
                    temb[c], ttr, oh_free)
        dg = W[0:TP, 8810 + 512:8810 + 512 + TP]
        Sb = xn[:, :, :].rearrange("p c d -> p (c d)")[:, 0:N]
        u1 = xn[:, :, :].rearrange("p c d -> p (c d)")[:, 625:1250]
        u2 = xn[:, :, :].rearrange("p c d -> p (c d)")[:, 1250:1875]
        tp = None
        for c in range(TC):
            t = dve.do(lambda e, c=c: e.tensor_scalar(dg, ident[0:TP, 0:TP], sT[:, 0, c:c + 1], None, ALU.mult), ttr, tp, t_id)
            b, o = (5, c * TP) if c < 4 else (6, 0)
            tp = pe.do(lambda e, b=b, o=o: e.matmul(
                bank[b][0:TP, o:o + TP], onesf[0:TP, 0:TP], dg, start=True, stop=True), t, free[b], t_ones)
        act.do(lambda e: e.activation(Sb[:, 0:500], bank[5][0:TP, 0:500], ACT.Copy), tp, xn_free)
        t_S = act.do(lambda e: e.activation(Sb[:, 500:N], bank[6][0:TP, 0:TP], ACT.Copy))
        free[5] = free[6] = t_S
        tu = None
        tP = []
        for c in range(TC):
            t = dve.do(lambda e, c=c: e.tensor_scalar(u1, Sb, sT[:, 1, c:c + 1], None, ALU.add), t_S, tu)
            t = dve.do(lambda e: e.scalar_tensor_tensor(u2, u1, 0.1, u1, ALU.mult, ALU.max), t)
            t = dve.do(lambda e, c=c: e.scalar_tensor_tensor(u1, AT[:, c, :], 1e30, u2, ALU.mult, ALU.min), t)
            t = act.do(lambda e: e.activation(u2, u1, ACT.Exp), t)
            tu = dve.do(lambda e, c=c: e.tensor_tensor(AT[:, c, :], AT[:, c, :], u2, ALU.mult), t, t_Atr)
            tP.append(tu)
        rsum = bank[7][0:TP, 0:TC]
        for i in range(TC):
            for j in range(TC):
                lhs = AT[:, j, i * TP:(i + 1) * TP]
                pe.do(lambda e, i=i, j=j, lhs=lhs: e.matmul(
                    bank[i][0:TP, :], lhs, emb[:, j, :], start=j == 0, stop=j == TC - 1),
                    tP[j], temb[j], free[i], sig=False)
                t = pe.do(lambda e, i=i, j=j, lhs=lhs: e.matmul(
                    rsum[:, i:i + 1], lhs, onesf[0:TP, 0:1], start=j == 0, stop=j == TC - 1), free[7], sig=j == TC - 1)
            tr_ = t
        t = dve.do(lambda e: e.reciprocal(sT[:, 2, :], rsum), tr_)
        free[7] = t
        for i in range(TC):
            xt[i] = free[i] = dve.do(lambda e, i=i: e.scalar_tensor_tensor(
                x[:, i, :], bank[i][0:TP, :], sT[:, 2, i:i + 1], x[:, i, :], ALU.mult, ALU.add), t, xt[i])
        xn_free.append(tu)

        t = act.do(lambda e: e.activation(spt[:, :, :], actp[:, :, :], ACT.Abs), t_in)
        t = act.do(lambda e: e.activation(spt[:, :, :], spt[:, :, :], ACT.Exp, scale=-1.0), t)
        t = act.do(lambda e: e.activation(spt[:, :, :], spt[:, :, :], ACT.Ln, bias=onesf[:, 0:1]), t, t_ones)
        t = dve.do(lambda e: e.scalar_tensor_tensor(spl[:, :, :], actp[:, :, :], 0.0, spt[:, :, :], ALU.max, ALU.add), t, t_in)
        t_sp = dve.do(lambda e: e.tensor_scalar(ngc[:, :, :], spl[:, :, :], -1.0, None, ALU.mult), t)

        def swiglu(ei, G, U, S, H, t_gu, *tokens):
            p = lambda i: actp[:, ei, i:i + 1]
            t = dve.do(lambda e: e.tensor_scalar(G, G, ngc[:, ei, 3:4], spl[:, ei, 3:4], ALU.max, ALU.min), t_gu, t_sp)
            ts_ = act.do(lambda e: e.activation(S, G, ACT.Sigmoid, scale=p(0)), t)
            t1 = dve.do(lambda e: e.tensor_scalar(U, U, ngc[:, ei, 4:5], spl[:, ei, 4:5], ALU.max, ALU.min))
            t1 = dve.do(lambda e: e.scalar_tensor_tensor(U, U, p(2), G, ALU.add, ALU.mult), t1, t)
            return dve.do(lambda e: e.scalar_tensor_tensor(H, U, p(1), S, ALU.mult, ALU.mult), t1, ts_, *tokens)

        shT = W[:, 3125:3125 + 1875].rearrange("p (f n) -> p f n", f=3)

        def shared(tT):
            w1 = slot(w_sh1).rearrange("p (k f) -> p k f", k=DC)
            tG = None
            th = []
            for h0, n in ((0, 313), (313, 312)):
                base = 6709
                G, U, S = (W[:, base + 939 * i:base + 939 * i + 3 * n] for i in range(3))
                tg = []
                for f in range(6):
                    for d in range(DC):
                        t = pe.do(lambda e, f=f, d=d, h0=h0, n=n: e.matmul(
                            bank[f][:, 0:n], w1[:, d, f * P:(f + 1) * P], xnT[:, d, h0:h0 + n],
                            start=d == 0, stop=d == DC - 1), tT, landed[w_sh1], free[f], sig=d == DC - 1)
                    dst = (G if f < 3 else U)[:, (f % 3) * n:(f % 3 + 1) * n]
                    bias = b1[0][:, 96 + f:97 + f]
                    if f < 3:
                        t = act.do(lambda e, f=f, n=n, dst=dst, bias=bias: e.activation(
                            dst, bank[f][:, 0:n], ACT.Identity, bias=bias), t, t_in, th, mem["work"])
                    else:
                        t = dve.do(lambda e, f=f, n=n, dst=dst, bias=bias: e.tensor_scalar(
                            dst, bank[f][:, 0:n], bias, None, ALU.add), t, t_in, th, mem["work"])
                    free[f] = t
                    tg.append(t)
                Hv = shT[:, :, h0:h0 + n]
                v3 = lambda a: a.rearrange("p (f n) -> p f n", f=3)
                th.append(swiglu(16, v3(G), v3(U), v3(S), Hv, tg))
            release(w_sh1, t_pe())
            mem["sh"] = th

        def t_pe():
            return (pe.sem, pe.n)

        def shared_rows(c):
            w2 = slot(w_sh2).rearrange("p (k d) -> p k d", k=3)
            pe.do(lambda e: e.matmul(bank[c][0:TP, :], onesf[0:1, 0:TP], b2s[:, :], start=False, stop=False), t_in, sig=False)
            for f in range(3):
                t = pe.do(lambda e, f=f: e.matmul(bank[c][0:TP, :], shT[:, f, c * TP:(c + 1) * TP], w2[:, f, :],
                                                  start=False, stop=f == 2), mem["sh"], landed[w_sh2], sig=f == 2)
            if c == TC - 1:
                release(w_sh2, t)
                mem["work"] = t
            return t

        def mm1(psum, w, cols, t, *tokens):
            for j, f in enumerate(cols):
                for d in range(DC):
                    last = j == len(cols) - 1 and d == DC - 1
                    t2 = pe.do(lambda e, j=j, f=f, d=d: e.matmul(
                        psum[:, j * P:(j + 1) * P], w[:, d, f * P:(f + 1) * P], XG[:, d * P:(d + 1) * P],
                        start=d == 0, stop=d == DC - 1), t, *tokens, sig=last)
            return t2

        def mm2(yb, w, hs, first, last, *tokens):
            for j, h in enumerate(hs):
                t2 = pe.do(lambda e, j=j, h=h: e.matmul(
                    bank[yb][:, :], HT[:, h * P:(h + 1) * P], w[:, j, :],
                    start=first and j == 0, stop=last and j == len(hs) - 1), *tokens, sig=j == len(hs) - 1)
            return t2

        wv = lambda n, k: slot(n).rearrange("p (k f) -> p k f", k=k)

        def expert0(e_, k, yb, t_x):
            n1, n2 = w_l0[e_]
            w1 = wv(n1, DC)
            w2 = wv(n2, 6)[:, 3 * (e_ % 2):3 * (e_ % 2) + 3, :]
            gb, ub = (3, 4) if yb == 1 else (5, 6)
            G, U, S = (TMP[:, 384 * i:384 * i + 384] for i in range(3))
            tg = mm1(bank[gb], w1, [0, 1, 2], t_x, landed[n1], free[gb])
            for j in range(3):
                t = act.do(lambda e, j=j: e.activation(G[:, j * P:(j + 1) * P], bank[gb][:, j * P:(j + 1) * P],
                                                       ACT.Identity, bias=b1[0][:, e_ * 6 + j:e_ * 6 + j + 1]),
                           tg, mem.get("h0"), mem["work"])
            free[gb] = t
            tu = mm1(bank[ub], w1, [3, 4, 5], t_x, free[ub])
            for j in range(3):
                t2 = dve.do(lambda e, j=j: e.tensor_scalar(U[:, j * P:(j + 1) * P], bank[ub][:, j * P:(j + 1) * P],
                                                           b1[0][:, e_ * 6 + 3 + j:e_ * 6 + 4 + j], None, ALU.add),
                            tu, mem.get("h0"), mem["work"])
            free[ub] = t2
            t = swiglu(e_, G, U, S, HT[:, 0:384], [t, t2], mem.get("hp"))
            mem["h0"] = t
            t = mm2(yb, w2, [0, 1, 2], True, True, t, landed[n2], free[yb])
            mem["hp"] = t
            return t

        def expert1(e_, k, yb, t_x):
            na, nb, n2 = w_l1[e_]
            w2 = wv(n2, 8)
            tg = []
            for g, n1 in enumerate((na, nb)):
                w1 = wv(n1, DC)
                hb, ub = 3 + 2 * g, 4 + 2 * g
                S = TMP[:, 512 * g:512 * g + 512]
                th = mm1(bank[hb], w1, [0, 1, 2, 3], t_x, landed[n1], free[hb])
                tS = []
                for j in range(4):
                    c = e_ * 16 + 4 * g + j
                    tS.append(act.do(lambda e, j=j, c=c, S=S, hb=hb: e.activation(
                        S[:, j * P:(j + 1) * P], bank[hb][:, j * P:(j + 1) * P], ACT.Silu, bias=b1[1][:, c:c + 1]),
                        th, mem.get(("s", g)), mem["work"]))
                free[hb] = tS[-1]
                tu = mm1(bank[ub], w1, [4, 5, 6, 7], t_x, free[ub])
                for j in range(4):
                    c = e_ * 16 + 8 + 4 * g + j
                    h = 4 * g + j
                    t = dve.do(lambda e, j=j, c=c, h=h, S=S, ub=ub: e.scalar_tensor_tensor(
                        HT[:, h * P:(h + 1) * P], bank[ub][:, j * P:(j + 1) * P], b1[1][:, c:c + 1],
                        S[:, j * P:(j + 1) * P], ALU.add, ALU.mult), tu, tS[j], mem.get("hp"), mem["work"])
                free[ub] = t
                mem[("s", g)] = t
                tg.append(t)
            mm2(yb, w2[:, 0:4, :], [0, 1, 2, 3], True, False, tg[0], landed[n2], free[yb])
            t = mm2(yb, w2[:, 4:8, :], [4, 5, 6, 7], False, True, tg[1])
            mem["hp"] = t
            return t

        def expert2(e_, k, yb, t_x):
            n1, n2 = w_l2[e_][0:2], w_l2[e_][2:4]
            tg = []
            for g in range(4):
                w1 = wv(n1[g // 2], DC)
                hb = 3 + g
                th = mm1(bank[hb], w1, [4 * (g % 2) + j for j in range(4)], t_x, landed[n1[g // 2]], free[hb])
                for j in range(4):
                    h = 4 * g + j
                    t = act.do(lambda e, j=j, h=h, hb=hb: e.activation(
                        HT[:, h * P:(h + 1) * P], bank[hb][:, j * P:(j + 1) * P], ACT.Silu,
                        bias=b1[2][:, e_ * 16 + h:e_ * 16 + h + 1]), th, mem.get("hp"), mem["work"])
                free[hb] = t
                tg.append(t)
            for g in range(4):
                w2 = wv(n2[g // 2], 8)
                t = mm2(yb, w2[:, 4 * (g % 2):4 * (g % 2) + 4, :], [4 * g + j for j in range(4)], g == 0, g == 3,
                        tg[g], landed[n2[g // 2]], free[yb])
            mem["hp"] = t
            return t

        def expert3(e_, k, yb, t_x):
            n1, n2 = w_l3[e_]
            w1, w2 = wv(n1, DC), wv(n2, 8)
            tg = []
            for g in range(2):
                hb = 3 + 2 * g + (yb - 1)
                th = mm1(bank[hb], w1, [4 * g + j for j in range(4)], t_x, landed[n1], free[hb])
                for j in range(4):
                    h = 4 * g + j
                    t = dve.do(lambda e, j=j, h=h, hb=hb: e.tensor_scalar(
                        HT[:, h * P:(h + 1) * P], bank[hb][:, j * P:(j + 1) * P],
                        b1[3][:, e_ * 8 + h:e_ * 8 + h + 1], 0.0, ALU.add, ALU.max), th, mem.get("hp"), mem["work"])
                free[hb] = t
                tg.append(t)
            mm2(yb, w2[:, 0:4, :], [0, 1, 2, 3], True, False, tg[0], landed[n2], free[yb])
            t = mm2(yb, w2[:, 4:8, :], [4, 5, 6, 7], False, True, tg[1])
            mem["hp"] = t
            return t

        def done(e_):
            if e_ % 2 == 0:
                release(w_l0[e_][0], t_pe())
            else:
                release(w_l0[e_][1], t_pe())
                release(w_l0[e_][0], t_pe())

        moe(0, 16, I["L0_b2"], expert0, shared, shared_rows)

        t_vec = load_vecs(("L1_gnn_bias", "L1_gnn_gamma", "L1_gnn_beta"), mem["work"])
        ts, tT = layernorm()
        Av = A.rearrange("p (c i) -> p c i", c=TC)
        halves = ((0, 313), (313, 312))
        rdeg = W[:, 6209:6209 + N]
        for h, (h0, n) in enumerate(halves):
            for c in range(TC):
                t = pe.do(lambda e, h=h, h0=h0, n=n, c=c: e.matmul(
                    bank[5 + h][:, 0:n], onesf[0:TP, :], Av[:, c, h0:h0 + n], start=c == 0, stop=c == TC - 1),
                    free[5 + h], t_Adone, sig=c == TC - 1)
            t = dve.do(lambda e, h=h, h0=h0, n=n: e.tensor_scalar(
                rdeg[:, h0:h0 + n], bank[5 + h][:, 0:n], 1.0, None, ALU.max), t, mem["work"])
            free[5 + h] = t
        t_rd = dve.do(lambda e: e.reciprocal(rdeg, rdeg), t)
        nmT = W[:, 3125:3125 + 2500].rearrange("p (k n) -> p k n", k=DC)
        tn = []
        for m in range(DC):
            for h, (h0, n) in enumerate(halves):
                b = (2 * m + h) % 8
                for c in range(TC):
                    t = pe.do(lambda e, m=m, b=b, h0=h0, n=n, c=c: e.matmul(
                        bank[b][:, 0:n], xn[:, c, m * P:(m + 1) * P], Av[:, c, h0:h0 + n],
                        start=c == 0, stop=c == TC - 1), ts[c], free[b], sig=c == TC - 1)
                free[b] = dve.do(lambda e, m=m, b=b, h0=h0, n=n: e.tensor_tensor(
                    nmT[:, m, h0:h0 + n], bank[b][:, 0:n], rdeg[:, h0:h0 + n], ALU.mult), t, t_rd, mem["work"])
                tn.append(free[b])
        xn_free.append(t_pe())
        hrow = W[0:TP, 6840:6840 + 2560].rearrange("p (c d) -> p c d", c=TC)

        def norm_rows(c, psum, t, t_vec):
            h = hrow[:, c, :]
            t = dve.do(lambda e: e.tensor_tensor(h, psum, vec(0), ALU.add), t, t_vec, mem["work"])
            tf = t
            t = dve.do(lambda e: e.bn_stats(stats[:, c, :], h), t)
            t = dve.do(lambda e: e.bn_aggr(mv[:, c, :], stats[:, c, :]), t)
            t = act.do(lambda e: e.activation(rstd[:, c:c + 1], mv[:, c, 1:2], ACT.Sqrt, bias=eps[0:TP, :]), t)
            t = dve.do(lambda e: e.reciprocal(rstd[:, c:c + 1], rstd[:, c:c + 1]), t)
            t = dve.do(lambda e: e.tensor_scalar(h, h, mv[:, c, 0:1], rstd[:, c:c + 1], ALU.subtract, ALU.mult), t)
            t = pool.do(lambda e: e.tensor_tensor(h, h, vec(1), ALU.mult), t, t_vec)
            t = pool.do(lambda e: e.tensor_tensor(h, h, vec(2), ALU.add), t)
            xt[c] = dve.do(lambda e: e.tensor_tensor(x[:, c, :], x[:, c, :], h, ALU.add), t, xt[c])
            return tf

        wg1 = wv(w_l1g, 8)
        for c in range(TC):
            for d in range(8):
                lhs = (xnT if d < DC else nmT)[:, d % DC, c * TP:(c + 1) * TP]
                t = pe.do(lambda e, c=c, d=d, lhs=lhs: e.matmul(bank[c][0:TP, :], lhs, wg1[:, d, :], start=d == 0, stop=d == 7),
                          tT[c], tn, landed[w_l1g], free[c], sig=d == 7)
            free[c] = norm_rows(c, bank[c][0:TP, :], t, t_vec)
        release(w_l1g, t_pe())
        xnT_free.append(t_pe())
        mem["work"] = xt[TC - 1]
        mem["gt"] = [mem["work"]] * 6

        def edges(tT):
            OF = [W[0:TP, 7733 + 625 * i:7733 + 625 * (i + 1)] for i in range(4)]
            fr = [None] * 4
            for c in range(EC):
                b = c % 4
                t = dve.do(lambda e, b=b, c=c: e.tensor_scalar(
                    OF[b], iota[0:TP, :], ef[:, 1, c:c + 1], None, ALU.is_equal), fr[b], mem["work"])
                n, o = (w_ea[0], c) if c < 42 else (w_ea[1], c - 42)
                lhs = slot(n)[:, o * 96:(o + 1) * 96]
                for h, (h0, nn) in enumerate(halves):
                    t2 = pe.do(lambda e, b=b, c=c, lhs=lhs, h=h, h0=h0, nn=nn: e.matmul(
                        bank[h][0:96, 0:nn], lhs, OF[b][:, h0:h0 + nn], start=c == 0, stop=c == EC - 1),
                        t, landed[n], free[h], sig=h == 1)
                fr[b] = t2
                if c in (41, 84):
                    release(n, t2)
            for h, (h0, nn) in enumerate(halves):
                free[h] = act.do(lambda e, h=h, h0=h0, nn=nn: e.activation(
                    aggT[:, h0:h0 + nn], bank[h][0:96, 0:nn], ACT.Copy), t2)
            mem["agg"] = free[1]
            mem["work"] = t2

        def done(e_):
            for n in w_l1[e_]:
                release(n, t_pe())

        moe(1, 8, I["L1_b2"], expert1, edges, None)

        t_vec = load_vecs(("L2_gnn_b3", "L2_gnn_gamma", "L2_gnn_beta"), mem["work"])
        ts, tT = layernorm()
        h1 = W[:, 0:5000].rearrange("p (f n) -> p f n", f=8)
        h2 = xnT
        w1a, w1b = wv(w_l2g[0], DC), slot(w_l2g[1])
        th1 = []
        for f in range(8):
            for h, (h0, n) in enumerate(halves):
                b = (2 * f + h) % 8
                for d in range(DC + 1):
                    lhs = w1a[:, d, f * P:(f + 1) * P] if d < DC else w1b[:, f * P:(f + 1) * P]
                    rhs = xnT[:, d, h0:h0 + n] if d < DC else aggT[:, h0:h0 + n]
                    t = pe.do(lambda e, b=b, n=n, d=d, lhs=lhs, rhs=rhs: e.matmul(
                        bank[b][:, 0:n], lhs, rhs, start=d == 0, stop=d == DC), tT, mem["agg"],
                        landed[w_l2g[0]], landed[w_l2g[1]], free[b], sig=d == DC)
                free[b] = act.do(lambda e, b=b, n=n, h0=h0, f=f: e.activation(
                    h1[:, f, h0:h0 + n], bank[b][:, 0:n], ACT.Relu, bias=gb1[:, f:f + 1]), t, t_in, mem["work"])
                th1.append(free[b])
        release(w_l2g[0], t_pe())
        release(w_l2g[1], t_pe())
        h2a = W[:, 5000:6850]
        h2f = xnT[:, :, :].rearrange("p k n -> p (k n)")[:, 0:2500]
        t_h1 = t_pe()
        last_mm = None
        w3 = wv(w_l2g[4], 8)
        ycols = {0: [], 1: []}
        H2 = {0: h2f, 1: h2f}
        th2_free = [t_h1]
        H2all = [xnT[:, :, :].rearrange("p k n -> p (k n)"), None]
        t_n = None
        for g, (c0, c1) in enumerate(((0, 2), (2, 4), (4, 5))):
            h0, n = c0 * TP, (c1 - c0) * TP
            hv = H2all[0][:, 0:8 * n].rearrange("p (f n) -> p f n", f=8)
            th2 = []
            for f in range(8):
                b = f
                for d in range(8):
                    w2 = wv(w_l2g[2 + d // 4], DC)
                    t = pe.do(lambda e, b=b, n=n, d=d, f=f, h0=h0, w2=w2: e.matmul(
                        bank[b][:, 0:n], w2[:, d % 4, f * P:(f + 1) * P], h1[:, d, h0:h0 + n],
                        start=d == 0, stop=d == 7), th1, landed[w_l2g[2]], landed[w_l2g[3]], free[b], sig=d == 7)
                free[b] = act.do(lambda e, b=b, n=n, f=f, hv=hv: e.activation(
                    hv[:, f, :], bank[b][:, 0:n], ACT.Relu, bias=gb1[:, 8 + f:9 + f]), t, th2_free)
                th2.append(free[b])
            for c in range(c0, c1):
                b = c
                for f in range(8):
                    t = pe.do(lambda e, b=b, f=f, c=c, hv=hv, c0=c0: e.matmul(
                        bank[b][0:TP, :], hv[:, f, (c - c0) * TP:(c - c0 + 1) * TP], w3[:, f, :],
                        start=f == 0, stop=f == 7), th2, landed[w_l2g[4]], free[b], sig=f == 7)
                free[b] = norm_rows(c, bank[b][0:TP, :], t, t_vec)
            th2_free = [t_pe()]
        for n in w_l2g[2:5]:
            release(n, t_pe())
        xnT_free.append(t_pe())
        mem["work"] = xt[TC - 1]
        mem["gt"] = [mem["work"]] * 6

        def done(e_):
            for n in w_l2[e_]:
                release(n, t_pe())

        moe(2, 8, I["L2_b2"], expert2, lambda tT: None, None)

        ts, tT = layernorm()
        xnT_free.append(tT)
        inv = sT[:, 3, :]
        t_inv = dve.do(lambda e: e.reciprocal(inv, cs), t_seg)
        B3 = W[0:TP, 0:3125].rearrange("p (c i) -> p c i", c=TC)
        dgs = [W[0:TP, 3125 + TP * i:3125 + TP * (i + 1)] for i in range(TC)]
        for c in range(TC):
            t = dve.do(lambda e, c=c: e.tensor_scalar(dgs[c], ident[0:TP, 0:TP], gg[:, c:c + 1], None, ALU.mult),
                       t_seg, mem["work"])
            b, o = (5, c * TP) if c < 4 else (6, 0)
            t = pe.do(lambda e, b=b, o=o, c=c: e.matmul(
                bank[b][0:TP, o:o + TP], onesf[0:TP, 0:TP], dgs[c], start=True, stop=True), t, free[b])
        tB = []
        for c in range(TC):
            dve.do(lambda e, c=c: e.tensor_scalar(B3[:, c, 0:500], bank[5][0:TP, 0:500], sg[:, c:c + 1], None, ALU.is_equal), t)
            tB.append(dve.do(lambda e, c=c: e.tensor_scalar(B3[:, c, 500:N], bank[6][0:TP, 0:TP], sg[:, c:c + 1], None, ALU.is_equal)))
        free[5] = free[6] = tB[-1]
        for i in range(TC):
            for j in range(TC):
                t = pe.do(lambda e, i=i, j=j: e.matmul(
                    bank[i][0:TP, :], B3[:, j, i * TP:(i + 1) * TP], xn[:, j, :], start=j == 0, stop=j == TC - 1),
                    ts[j], tB[j], free[i], sig=j == TC - 1)
            xt[i] = free[i] = dve.do(lambda e, i=i: e.scalar_tensor_tensor(
                x[:, i, :], bank[i][0:TP, :], inv[:, i:i + 1], x[:, i, :], ALU.mult, ALU.add), t, xt[i], t_inv)
        xn_free.append(t_pe())
        mem["work"] = [mem["work"], t_pe()]

        def done(e_):
            for n in w_l3[e_]:
                release(n, t_pe())

        moe(3, 8, I["L3_b2"], expert3, lambda tT: None, None)

        for c in range(TC):
            for a, b in ((0, 120), (120, 125)):
                t_out = act.dma(d_out, lambda e, a=a, b=b, c=c: e.dma_start(out_v[a:b, c, :], x[a:b, c, :]), xt[c])
        act.wait(t_out)

        block = ctx.enter_context(nc.Block())

        @block.sync
        def _(eng):
            sp.emit(eng)

        @block.gpsimd
        def _(eng):
            pool.emit(eng)

        @block.scalar
        def _(eng):
            act.emit(eng)

        @block.vector
        def _(eng):
            dve.emit(eng)

        @block.tensor
        def _(eng):
            pe.emit(eng)


def kernel(**a):
    import numpy as np
    import concourse.bacc as bacc
    from concourse.bass_utils import run_bass_kernel_spmd

    a = {k: np.asarray(v) for k, v in a.items()}

    def blocks(w):
        *lead, k, f = w.shape
        w = w.reshape(*lead, k // P, P, f)
        return np.moveaxis(w, -2, -3).reshape(*lead, P, k // P * f)

    def split_gu(w):
        return np.concatenate([w[..., 0::2], w[..., 1::2]], -1)

    def cols(b):
        return b.reshape(-1, P).T

    row = lambda v: v.reshape(1, -1)
    ins = {
        "x": a["x"], "src": a["src"], "dst": a["dst"],
        "L0_gnn_W": blocks(a["L0_gnn_W"]), "L0_gnn_b": row(a["L0_gnn_b"]),
        "L0_a_src": row(a["L0_gnn_a"][:D]), "L0_a_dst": row(a["L0_gnn_a"][D:]),
        "act": row(np.concatenate([a["L0_ffn_expert_act"], a["L0_ffn_shared_act"][None]], 0)),
        "sh_w1": blocks(split_gu(a["L0_ffn_shared_w1"])), "sh_w2": blocks(a["L0_ffn_shared_w2"]),
        "sh_b2": row(a["L0_ffn_shared_b2"]),
        "L0_w1": blocks(split_gu(a["L0_ffn_expert_w1"])),
        "L0_w2": np.concatenate([blocks(a["L0_ffn_expert_w2"][0::2]), blocks(a["L0_ffn_expert_w2"][1::2])], -1),
        "L0_b1": cols(split_gu(np.concatenate([a["L0_ffn_expert_b1"], a["L0_ffn_shared_b1"][None]], 0))),
        "L0_b2": a["L0_ffn_expert_b2"],
        "L1_gnn_W": blocks(np.concatenate([a["L1_gnn_W_self"].T, a["L1_gnn_W_neigh"].T], 0)),
        "L1_gnn_bias": row(a["L1_gnn_bias"]), "L1_gnn_gamma": row(a["L1_gnn_gamma"]), "L1_gnn_beta": row(a["L1_gnn_beta"]),
        "L1_b1": cols(a["L1_ffn_fc1_b"]), "L1_b2": a["L1_ffn_fc2_b"],
        "L1_w2": blocks(np.swapaxes(a["L1_ffn_fc2_w"], 1, 2)),
        "L2_gnn_W1a": blocks(a["L2_gnn_W1"][:D]), "L2_gnn_W1b": a["L2_gnn_W1"][D:],
        "L2_gnn_W2": blocks(a["L2_gnn_W2"].reshape(2, 512, 1024)), "L2_gnn_W3": blocks(a["L2_gnn_W3"]),
        "L2_gnn_b": cols(np.stack([a["L2_gnn_b1"], a["L2_gnn_b2"]])),
        "L2_gnn_b3": row(a["L2_gnn_b3"]), "L2_gnn_gamma": row(a["L2_gnn_gamma"]), "L2_gnn_beta": row(a["L2_gnn_beta"]),
        "L2_w1": blocks(np.moveaxis(a["L2_ffn_W1"].reshape(8, D, 2, 1024), 2, 1)),
        "L2_w2": blocks(a["L2_ffn_W2"].reshape(8, 2, 1024, D)),
        "L2_b1": cols(a["L2_ffn_b1"]), "L2_b2": a["L2_ffn_b2"],
        "L3_w1": blocks(a["L3_ffn_w1"]), "L3_w2": blocks(a["L3_ffn_w2"]),
        "L3_b1": cols(a["L3_ffn_b1"]), "L3_b2": a["L3_ffn_b2"],
        "L0_gb": row(a["L0_ffn_gate_b"]), "L1_gb": row(a["L1_ffn_router_b"]),
        "L2_gb": row(a["L2_ffn_bg"]), "L3_gb": row(a["L3_ffn_gate_b"]),
    }
    f1 = np.swapaxes(a["L1_ffn_fc1_w"], 1, 2).reshape(8, D, 2, 2, 512)
    ins["L1_w1"] = blocks(np.ascontiguousarray(np.transpose(f1, (0, 3, 1, 2, 4))).reshape(8, 2, D, 1024))
    for nm, g in (("L0", a["L0_ffn_gate_w"]), ("L1", a["L1_ffn_router_w"].T), ("L2", a["L2_ffn_Wg"]), ("L3", a["L3_ffn_gate_w"])):
        ins[nm + "_gate"] = np.moveaxis(g.reshape(DC, P, -1), 1, 0)
    ea = a["edge_attr_96"].reshape(TP, EC, 96)
    ins["ea0"] = ea[:, :42].reshape(TP, -1)
    ins["ea1"] = ea[:, 42:].reshape(TP, -1)

    nc = bacc.Bacc("TRN2", target_bir_lowering=False, num_devices=1)
    arrays, aps = {}, {}
    for k, v in ins.items():
        v = np.ascontiguousarray(v)
        arrays["in_" + k] = v
        aps[k] = nc.dram_tensor("in_" + k, v.shape, mybir.dt.from_np(v.dtype), kind="ExternalInput").ap()
    out = nc.dram_tensor("out_x", (N, D), F32, kind="ExternalOutput").ap()
    program(nc, aps, out)
    r = run_bass_kernel_spmd(nc, [arrays], core_ids=[0])
    return r.results[0]["out_x"]
```

```python
from contextlib import ExitStack

import concourse.bass as bass
from concourse import mybir

F32 = mybir.dt.float32
BF = mybir.dt.bfloat16
F16 = mybir.dt.float16
I32 = mybir.dt.int32
U32 = mybir.dt.uint32
ALU = mybir.AluOpType
ACT = mybir.ActivationFunctionType
AX = mybir.AxisListType

N, D, P, TP, TC = 625, 512, 128, 125, 5
NE, EC = 10625, 85
DC = D // P
SLOTW, NSLOT = 4128, 6
CH, NCH = 128, 5
FAR = 1 << 20
WORK = 15029


class Eng:

    def __init__(self, sem):
        self.sem, self.n, self.ops, self.seen, self.stack = sem, 0, [], {}, []

    def wait(self, *tokens):
        for t in tokens:
            if t is None:
                continue
            if isinstance(t, list):
                self.wait(*t)
                continue
            sem, v = t
            if v > 0 and self.seen.get(sem.name, 0) < v:
                self.seen[sem.name] = v
                self.ops.append(("wait", sem, v))

    def do(self, fn, *tokens, sig=True):
        self.wait(*tokens)
        if sig:
            self.n += 1
        self.ops.append(("do", fn, self.sem if sig else None, 1))
        return (self.sem, self.n) if sig else None

    def dma(self, d, fn, *tokens):
        self.wait(*tokens)
        d.n += 16
        self.ops.append(("do", fn, d.sem, 16))
        return (d.sem, d.n)

    def begin(self, e, k, dmas=()):
        self.stack.append((e, k, self.ops, self.n, dict(self.seen), [(d, d.n) for d in dmas]))
        self.ops = []

    def end(self):
        e, k, outer, n, seen, dmas = self.stack.pop()
        outer.append(("if", e, k, self.ops, self.n - n, [(d.sem, v, d.n - v) for d, v in dmas if d.n > v]))
        self.ops, self.seen = outer, seen

    def emit(self, eng, ops=None, regs=None):
        regs = {} if regs is None else regs
        for op in self.ops if ops is None else ops:
            if op[0] == "wait":
                eng.wait_ge(op[1], op[2])
            elif op[0] == "do":
                ins = op[1](eng)
                if op[2] is not None:
                    ins.then_inc(op[2], op[3])
            elif op[0] == "count":
                regs[op[1]] = eng.value_load(op[2], min_val=0, max_val=N)
            else:
                _, e, k, body, inc, skipped = op
                with eng.If(regs[e] > CH * k):
                    self.emit(eng, body, regs)
                with eng.Else():
                    for sem, before, more in skipped:
                        eng.wait_ge(sem, before)
                        eng.inc_swdge_sem([sem], [more])
                    if inc:
                        eng.drain().then_inc(self.sem, inc)


class Dma:
    def __init__(self, sem):
        self.sem, self.n = sem, 0


def program(nc, I, out):
    ctx = ExitStack()
    with ctx:
        def sb(name, shape, dt=F32):
            return ctx.enter_context(nc.sbuf_tensor(name, shape, dt))

        def sem(name):
            return ctx.enter_context(nc.semaphore(name))

        def dram(name, shape, dt=F32):
            return nc.dram_tensor(name, shape, dt, kind="Internal").ap()

        pe, act, dve, pool, sp = (Eng(sem("s_" + n)) for n in ("pe", "act", "dve", "pool", "sp"))
        bank = [ctx.enter_context(nc.psum_tensor(f"bank{i}", [P, 512], F32)) for i in range(8)]
        free = [None] * 8

        ring = sb("ring", [P, NSLOT * SLOTW])
        W = sb("work", [P, WORK])
        x = sb("x", [TP, TC, D])
        xn = sb("xn", [TP, TC, D])
        xnT = sb("xnT", [P, DC, N])
        ident = sb("ident", [P, P])
        onesf = sb("onesf", [P, P])
        onesb = sb("onesb", [P, P], BF)
        upper = sb("upper", [P, P], BF)
        iota = sb("iota", [P, N], F16)
        iotaE = sb("iotaE", [P, 16])
        tok = sb("tok", [TP, TC], I32)
        tokf = sb("tokf", [TP, TC])
        eps = sb("eps", [P, 1])
        gate = sb("gate", [P, 4, DC, 16])
        gbias = sb("gbias", [P, 4, 16])
        b1 = [sb(f"b1_{i}", [P, n]) for i, n in enumerate((17 * 6, 8 * 16, 8 * 16, 8 * 8))]
        gb1 = sb("gb1", [P, 16])
        actp = sb("actp", [P, 17, 5])
        spl = sb("spl", [P, 17, 5])
        spt = sb("spt", [P, 17, 5])
        ngc = sb("ngc", [P, 17, 5])
        b2 = sb("b2", [16, D])
        b2s = sb("b2s", [1, D])
        cwT = sb("cwT", [16, N])
        aggT = sb("aggT", [96, N])
        stats = sb("stats", [TP, TC, 6])
        mv = sb("mv", [TP, TC, 2])
        rstd = sb("rstd", [TP, TC])
        nmr = sb("nmr", [TP, TC])
        lg = sb("lg", [TP, TC, 16])
        mx = sb("mx", [TP, TC, 8])
        ix = sb("ix", [TP, TC, 8], U32)
        ixf = sb("ixf", [TP, 2, TC])
        s12 = sb("s12", [TP, 2 * TC, 16])
        t12 = sb("t12", [TP, 2 * TC, 16])
        sel = sb("sel", [TP, TC * 16], BF)
        rk = sb("rk", [TP, 2, TC])
        kk = sb("kk", [TP, 4, 2 * TC])
        dw = sb("dw", [TP, TC])
        wt = sb("wt", [TP, 2, TC])
        cw = sb("cw", [TP, TC, 16])
        cnt = sb("cnt", [1, 16], I32)
        idx = sb("idx", [P, 160], I32)
        idz = sb("idz", [P, 160])
        tok1 = sb("tok1", [TP, 2, TC])
        seg = sb("seg", [TP, 12, TC])
        segi = sb("segi", [TP, 4, TC], I32)
        esrc = sb("esrc", [TP, 2, EC], I32)
        ef = sb("ef", [TP, 2, EC])
        sT = sb("sT", [TP, 4, TC])

        Y = dram("ybuf", [2 * N, D])
        xnd = dram("xnd", [N, D])

        d_in = Dma(sem("d_in"))
        d_x = Dma(sem("d_x"))
        d_e = Dma(sem("d_e"))
        d_v = Dma(sem("d_v"))
        d_b2 = Dma(sem("d_b2"))
        d_xn = Dma(sem("d_xn"))
        d_y = [Dma(sem(f"d_y{i}")) for i in range(6)]
        d_g = [Dma(sem(f"d_g{i}")) for i in range(8)]
        d_c = [Dma(sem(f"d_c{i}")) for i in range(TC)]
        d_s = Dma(sem("d_s"))
        d_out = Dma(sem("d_out"))
        d_r = [Dma(sem(f"d_r{i}")) for i in range(NSLOT)]

        loads = []

        def plan(src, parts, words):
            loads.append((src, parts, words))
            return len(loads) - 1

        landed = {}

        def load(n, *tokens):
            if n >= len(loads):
                return
            src, parts, words = loads[n]
            s = n % NSLOT
            dst = ring[0:parts, s * SLOTW:s * SLOTW + words]
            landed[n] = sp.dma(d_r[s], lambda e: e.dma_start(dst, src), *tokens)

        def slot(n):
            _, parts, words = loads[n]
            s = n % NSLOT
            return ring[0:parts, s * SLOTW:s * SLOTW + words]

        held = []

        def release(n, token):
            load(n + NSLOT, token)

        def hold(n, token):
            held.append((n + NSLOT, token))

        def unhold(*tokens):
            for n, token in held:
                load(n, token, *tokens)
            held.clear()

        w_l0g = plan(I["L0_gnn_W"], P, 2048)
        w_sh1 = plan(I["sh_w1"], P, 3072)
        w_sh2 = plan(I["sh_w2"], P, 1536)
        w_l0 = []
        for e in range(0, 16, 2):
            a = plan(I["L0_w1"][e], P, 3072)
            c = plan(I["L0_w2"][e // 2], P, 3072)
            b = plan(I["L0_w1"][e + 1], P, 3072)
            w_l0 += [(a, c), (b, c)]
        w_l1g = plan(I["L1_gnn_W"], P, 4096)
        w_ea = [plan(I["ea0"], TP, 42 * 96), plan(I["ea1"], TP, 43 * 96)]
        w_l1 = [[plan(I["L1_w1"][e, 0], P, 4096), plan(I["L1_w1"][e, 1], P, 4096),
                 plan(I["L1_w2"][e], P, 4096)] for e in range(8)]
        w_l2g = [plan(I["L2_gnn_W1a"], P, 4096), plan(I["L2_gnn_W1b"], 96, 1024),
                 plan(I["L2_gnn_W2"][0], P, 4096), plan(I["L2_gnn_W2"][1], P, 4096),
                 plan(I["L2_gnn_W3"], P, 4096)]
        w_l2 = [[plan(I["L2_w1"][e, 0], P, 4096), plan(I["L2_w1"][e, 1], P, 4096),
                 plan(I["L2_w2"][e, 0], P, 4096), plan(I["L2_w2"][e, 1], P, 4096)] for e in range(8)]
        w_l3 = [[plan(I["L3_w1"][e], P, 4096), plan(I["L3_w2"][e], P, 4096)] for e in range(8)]

        x_in = I["x"].rearrange("(c p) d -> p c d", p=TP)
        out_v = out.rearrange("(c p) d -> p c d", p=TP)
        xnd_v = xnd.rearrange("(c p) d -> p c d", p=TP)
        for i, nm in enumerate(("src", "dst")):
            v = I[nm].rearrange("(p c) -> p c", p=TP)
            t_e = sp.dma(d_e, lambda e, i=i, v=v: e.dma_start(esrc[:, i, :], v))
        for a, b in ((0, 120), (120, 125)):
            t_x = sp.dma(d_x, lambda e, a=a, b=b: e.dma_start(x[a:b], x_in[a:b]))
        load(0)
        t_yt0 = pool.do(lambda e: e.memset(W[:, 11957:15029], 0.0))
        vec = lambda i: W[0:TP, WORK - 1536 + 512 * i:WORK - 1024 + 512 * i]

        def load_vecs(names, *tokens):
            for i, nm in enumerate(names):
                v = I[nm].to_broadcast([TP, D])
                t = act.dma(d_v, lambda e, i=i, v=v: e.dma_start(vec(i), v), *tokens)
            return t

        for i, (nm, E) in enumerate((("L0", 16), ("L1", 8), ("L2", 8), ("L3", 8))):
            t_in = act.dma(d_in, lambda e, i=i, nm=nm, E=E: e.dma_start(gate[:, i, :, 0:E], I[nm + "_gate"]))
            t_in = act.dma(d_in, lambda e, i=i, nm=nm, E=E: e.dma_start(
                gbias[:, i, 0:E], I[nm + "_gb"].to_broadcast([P, E])))
            t_in = act.dma(d_in, lambda e, i=i, nm=nm: e.dma_start(b1[i][:, :], I[nm + "_b1"]))
        t_in = act.dma(d_in, lambda e: e.dma_start(gb1[:, :], I["L2_gnn_b"]))
        t_in = act.dma(d_in, lambda e: e.dma_start(b2s[:, :], I["sh_b2"]))
        t_in = act.dma(d_in, lambda e: e.dma_start(actp[:, :, :].rearrange("p a b -> p (a b)"),
                                                   I["act"].to_broadcast([P, 85])))
        t_vec = load_vecs(("L0_gnn_b", "L0_a_src", "L0_a_dst"), t_yt0)
        for n in range(1, NSLOT):
            load(n)

        t = pool.do(lambda e: e.memset(ident[:, :], 0.0))
        t_id = pool.do(lambda e: e.affine_select(out=ident[:, :], in_=ident[:, :], compare_op=ALU.not_equal,
                                                 fill=1.0, base=0, pattern=[[-1, P]], channel_multiplier=1), t)
        t_io = pool.do(lambda e: e.iota(iota[:, :], [[1, N]], base=0, channel_multiplier=0,
                                        allow_small_or_imprecise_dtypes=True))
        t_ones = dve.do(lambda e: e.memset(onesf[:, :], 1.0))
        t_onesb = dve.do(lambda e: e.memset(onesb[:, :], 1.0))
        t_eps = dve.do(lambda e: e.memset(eps[:, :], 1e-5))
        pool.do(lambda e: e.iota(iotaE[:, :], [[1, 16]], base=0, channel_multiplier=0,
                                 allow_small_or_imprecise_dtypes=True))
        pool.do(lambda e: e.iota(tok[:, :], [[TP, TC]], base=0, channel_multiplier=1))
        t_tokf = pool.do(lambda e: e.iota(tokf[:, :], [[TP, TC]], base=0, channel_multiplier=1,
                                          allow_small_or_imprecise_dtypes=True))
        t = pool.do(lambda e: e.affine_select(out=upper[:, :], in_=onesb[:, :], compare_op=ALU.is_gt, fill=0.0,
                                              base=0, pattern=[[1, P]], channel_multiplier=-1), t_onesb)
        for j in range(2):
            pool.do(lambda e, j=j: e.tensor_scalar(tok1[:, j, :], tokf[:, :], 1.0, 1.0 + N * j, ALU.mult, ALU.add), t_tokf)
        t_pc = pool.do(lambda e: e.memset(W[:, 3125:7221], 0.0))

        qf, low, high, d_, mid, val, g_, u_ = (seg[:, i, :] for i in range(8))
        mi = segi[:, 0, :]
        vi = segi[:, 1, :]
        src_g = I["src"].rearrange("(n o) -> n o", o=1)
        dst_g = I["dst"].rearrange("(n o) -> n o", o=1)

        def gather5(dst_t, src_ap, idx_t, *tokens):
            for c in range(TC):
                t = pool.dma(d_s, lambda e, c=c: e.indirect_dma_start(
                    out=dst_t[:, c:c + 1], out_offset=None, in_=src_ap,
                    in_offset=bass.IndirectOffsetOnAxis(ap=idx_t[:, c:c + 1], axis=0)), *tokens)
            return t

        def search_steps(levels, t):
            if t is None:
                pool.do(lambda e: e.memset(low, 0.0))
                t = pool.do(lambda e: e.memset(high, float(NE)))
            for _ in range(levels):
                t = pool.do(lambda e: e.tensor_tensor(d_, high, low, ALU.subtract), t)
                t = pool.do(lambda e: e.tensor_scalar(d_, d_, 0.5, -0.25, ALU.mult, ALU.add), t)
                t = pool.do(lambda e: e.tensor_scalar(d_, d_, 8388608.0, -8388608.0, ALU.add, ALU.add), t)
                t = pool.do(lambda e: e.tensor_tensor(mid, low, d_, ALU.add), t)
                t = pool.do(lambda e: e.tensor_copy(mi, mid), t)
                t = gather5(vi, src_g, mi, t)
                t = pool.do(lambda e: e.tensor_copy(val, vi), t)
                t = pool.do(lambda e: e.tensor_tensor(val, tokf[:, :], val, ALU.subtract), t)
                t = pool.do(lambda e: e.tensor_scalar(g_, val, 0.0, None, ALU.is_lt), t)
                pool.do(lambda e: e.tensor_tensor(u_, low, mid, ALU.subtract), t)
                t = pool.do(lambda e: e.tensor_tensor(d_, mid, high, ALU.subtract), t)
                pool.do(lambda e: e.tensor_tensor(u_, u_, g_, ALU.mult), t)
                t = pool.do(lambda e: e.tensor_tensor(d_, d_, g_, ALU.mult), t)
                pool.do(lambda e: e.tensor_tensor(low, mid, u_, ALU.add), t)
                t = pool.do(lambda e: e.tensor_tensor(high, high, d_, ALU.add), t)
            return t

        sg, gg, cs = seg[:, 8, :], seg[:, 9, :], seg[:, 10, :]

        def search_end(t):
            t = pool.do(lambda e: e.tensor_scalar(sg, high, 1.0, -1.0, ALU.mult, ALU.add), t)
            t = pool.do(lambda e: e.tensor_scalar(g_, sg, 0.0, None, ALU.is_lt), t)
            t = pool.do(lambda e: e.tensor_scalar(g_, g_, float(NE), 0.0, ALU.mult, ALU.add), t)
            t = pool.do(lambda e: e.tensor_tensor(gg, sg, g_, ALU.add), t)
            t = pool.do(lambda e: e.tensor_copy(mi, gg), t)
            gather5(segi[:, 2, :], src_g, mi, t)
            t = gather5(segi[:, 3, :], dst_g, mi, t)
            t = pool.do(lambda e: e.tensor_copy(cs, segi[:, 3, :]), t)
            t = pool.do(lambda e: e.tensor_copy(seg[:, 11, :], segi[:, 2, :]), t)
            t = pool.do(lambda e: e.tensor_tensor(cs, cs, seg[:, 11, :], ALU.subtract), t)
            return pool.do(lambda e: e.tensor_scalar(cs, cs, 1.0, 1.0, ALU.mult, ALU.add), t)

        t_seg = search_end(search_steps(14, None))

        def t_pe():
            return (pe.sem, pe.n)

        xt = [t_x] * TC
        xn_free = []
        xnT_free = []
        xnT_bank = [0, 1, 2, 3, 4]

        warm = sb("warm", [1, 1])

        def table(func):
            act.do(lambda e: e.activation(warm[:, :], eps[0:1, :], func), t_eps, sig=False)

        def ln_tile(c):
            t = dve.do(lambda e: e.bn_stats(stats[:, c, :], x[:, c, :]), xt[c])
            t = dve.do(lambda e: e.bn_aggr(mv[:, c, :], stats[:, c, :]), t)
            t = act.do(lambda e: e.activation(rstd[:, c:c + 1], mv[:, c, 1:2], ACT.Sqrt, bias=eps[0:TP, :]), t, t_eps, xn_free)
            t = dve.do(lambda e: e.reciprocal(rstd[:, c:c + 1], rstd[:, c:c + 1]), t)
            t = dve.do(lambda e: e.scalar_tensor_tensor(
                nmr[:, c:c + 1], mv[:, c, 0:1], -1.0, rstd[:, c:c + 1], ALU.mult, ALU.mult), t)
            return act.do(lambda e: e.activation(
                xn[:, c, :], x[:, c, :], ACT.Identity, bias=nmr[:, c:c + 1], scale=rstd[:, c:c + 1]), t, xn_free)

        def xnT_tile(c, t, banks=xnT_bank):
            b = banks[c]
            for d in range(DC):
                t2 = pe.do(lambda e, d=d: e.transpose(
                    bank[b][:, d * TP:(d + 1) * TP], xn[:, c, d * P:(d + 1) * P], ident[0:TP, 0:TP]),
                    t, t_id, free[b], sig=d == DC - 1)
            src = bank[b][:, 0:DC * TP].rearrange("p (d t) -> p d t", d=DC)
            free[b] = act.do(lambda e: e.activation(xnT[:, :, c * TP:(c + 1) * TP], src, ACT.Copy), t2, xnT_free)
            return free[b]

        def layernorm():
            ts = [ln_tile(c) for c in range(TC)]
            xn_free.clear()
            tT = [xnT_tile(c, ts[c]) for c in range(TC)]
            xnT_free.clear()
            xn_free.append(t_pe())
            return ts, tT

        def rows_out(psum, c, t):
            return dve.do(lambda e: e.tensor_tensor(x[:, c, :], x[:, c, :], psum, ALU.add), t, xt[c])

        GT = [W[:, 3125 + 512 * i:3637 + 512 * i] for i in range(8)]
        XG = [W[:, 7221 + 512 * i:7733 + 512 * i] for i in range(3)]
        HT = W[:, 8757:10805]
        TMP = W[:, 10805:11957]
        YT = [W[:, 11957 + 512 * i:12469 + 512 * i] for i in range(6)]
        CMB = W[0:TP, 3125:3125 + 5120].rearrange("p (c j d) -> p c j d", c=TC, j=2)
        S1 = HT[0:TP, 0:640].bitcast(F16).rearrange("p (i s) -> p i s", i=2 * TC)
        R1 = HT[0:TP, 640:1440].bitcast(F16).rearrange("p (i s) -> p i s", i=2 * TC)
        Yv = Y.rearrange("(j c p) d -> p c j d", j=2, p=TP)
        mem = {"gt": [None] * 8, "yt": [None] * 6, "work": None, "b2": None, "xg": [None] * 3}

        def moe(L, E, b2_src, expert, between, extra_bias, group=1):
            K = E * NCH
            t_b2 = act.dma(d_b2, lambda e: e.dma_start(b2[0:E, :], b2_src), mem["b2"])
            ts, tT = layernorm()
            t_xnd = None
            for a, b in ((0, 120), (120, 125)):
                t_xnd = sp.dma(d_xn, lambda e, a=a, b=b: e.dma_start(xnd_v[a:b], xn[a:b]), ts)
            xn_free.append(t_xnd)
            table(ACT.Sigmoid)
            lgp = bank[5][0:TP, 0:TC * E]
            t_r = None
            for c in range(TC):
                for d in range(DC):
                    t = pe.do(lambda e, c=c, d=d: e.matmul(
                        lgp[:, c * E:(c + 1) * E], xnT[:, d, c * TP:(c + 1) * TP], gate[:, L, d, 0:E],
                        start=d == 0, stop=d == DC - 1), tT[c], t_in, free[5], sig=c == TC - 1 and d == DC - 1)
            lgv = lg[:, :, 0:E]
            t = dve.do(lambda e: e.tensor_tensor(
                lgv, lgp.rearrange("p (c e) -> p c e", e=E),
                gbias[0:TP, L:L + 1, 0:E].to_broadcast([TP, TC, E]), ALU.add), t, t_in)
            free[5] = t
            for c in range(TC):
                t2 = dve.do(lambda e, c=c: e.max(mx[:, c, :], lg[:, c, 0:E]), t)
            for c in range(TC):
                t2 = dve.do(lambda e, c=c: e.max_index(ix[:, c, :], mx[:, c, :], lg[:, c, 0:E]), t2)
            t = dve.do(lambda e: e.tensor_copy(ixf[:, :, :], ix[:, :, 0:2].rearrange("p c k -> p k c")), t2)
            ixv = ixf[:, :, :].rearrange("p k c -> p (k c)")
            sv, tv = s12[:, :, 0:E], t12[:, :, 0:E]
            t_s = dve.do(lambda e: e.tensor_tensor(
                sv, iotaE[0:TP, 0:E].rearrange("p (o e) -> p o e", o=1).to_broadcast([TP, 2 * TC, E]),
                ixv.rearrange("p (k o) -> p k o", o=1).to_broadcast([TP, 2 * TC, E]), ALU.is_equal), t, t_pc)
            sel_v = sel[:, 0:TC * E].rearrange("p (c e) -> p c e", e=E)
            t = dve.do(lambda e: e.tensor_tensor(sel_v, s12[:, 0:TC, 0:E], s12[:, TC:2 * TC, 0:E], ALU.add), t_s)
            rkp = bank[6][0:TP, 0:TC * E]
            pe.do(lambda e: e.matmul(rkp, upper[0:TP, 0:TP], sel[:, 0:TC * E], start=True, stop=True,
                                     skip_group_check=True), t, free[6], t_pc, sig=False)
            for s in range(1, TC):
                tr = pe.do(lambda e, s=s: e.matmul(rkp[:, s * E:], onesb[0:TP, 0:TP], sel[:, 0:(TC - s) * E],
                                                   start=False, stop=True, skip_group_check=True),
                           t_onesb, sig=s == TC - 1)
            ctp = bank[7][0:TP, 0:E]
            for c in range(TC):
                tc = pe.do(lambda e, c=c: e.matmul(ctp, onesb[0:TP, 0:TP], sel[:, c * E:(c + 1) * E],
                                                   start=c == 0, stop=c == TC - 1), free[7], sig=c == TC - 1)
            t = dve.do(lambda e: e.tensor_tensor(
                t12[:, 0:TC, 0:E], s12[:, 0:TC, 0:E], rkp.rearrange("p (c e) -> p c e", e=E), ALU.mult), tr)
            t = dve.do(lambda e: e.tensor_tensor(
                t12[:, TC:2 * TC, 0:E], s12[:, TC:2 * TC, 0:E],
                rkp.rearrange("p (c e) -> p c e", e=E), ALU.mult))
            free[6] = t
            rv = rk[:, :, :].rearrange("p k c -> p (k c)")
            t = dve.do(lambda e: e.tensor_reduce(rv, tv, AX.X, ALU.add), t)
            k0, k1, k2, k3 = (kk[:, i, :] for i in range(4))
            t = dve.do(lambda e: e.tensor_scalar(k0, rv, float(CH), None, ALU.is_ge), t)
            for j in range(2, NCH):
                a, b = (k0, k1) if j % 2 == 0 else (k1, k0)
                t = dve.do(lambda e, a=a, b=b, j=j: e.scalar_tensor_tensor(
                    b, rv, float(CH * j), a, ALU.is_ge, ALU.add), t)
            kf = k1 if (NCH - 2) % 2 == 1 else k0
            dve.do(lambda e: e.scalar_tensor_tensor(k2, ixv, float(NCH), kf, ALU.mult, ALU.add), t)
            t = dve.do(lambda e: e.scalar_tensor_tensor(k3, kf, -float(CH), rv, ALU.mult, ALU.add), t)
            idp = bank[5][:, 0:2 * K]
            for i in range(2 * TC):
                j, c = divmod(i, TC)
                dve.do(lambda e, i=i: e.tensor_scalar(
                    S1[:, i, :], iota[0:TP, 0:P], k3[:, i:i + 1], None, ALU.is_equal),
                    t, t_io, mem["work"], mem.get("hp"))
                dve.do(lambda e, i=i, c=c: e.tensor_scalar(
                    R1[:, i, 0:K], iota[0:TP, 0:K], k2[:, i:i + 1], tok1[:, 0, c:c + 1], ALU.is_equal, ALU.mult))
                t2 = dve.do(lambda e, i=i, j=j, c=c: e.tensor_scalar(
                    R1[:, i, K:2 * K], iota[0:TP, 0:K], k2[:, i:i + 1], tok1[:, j, c:c + 1], ALU.is_equal, ALU.mult))
                ti = pe.do(lambda e, i=i: e.matmul(idp, S1[:, i, :], R1[:, i, 0:2 * K], start=i == 0, stop=i == 2 * TC - 1),
                           t2, free[5], sig=i == 2 * TC - 1)
            t = dve.do(lambda e: e.tensor_scalar(idz[:, 0:2 * K], idp, 0.0, float(FAR), ALU.is_equal, ALU.mult), ti)
            t_idx = dve.do(lambda e: e.scalar_tensor_tensor(
                idx[:, 0:2 * K], idp, -1.0, idz[:, 0:2 * K], ALU.add, ALU.add), t, mem.get("y"))
            free[5] = t_idx
            t_cnt = dve.do(lambda e: e.tensor_copy(cnt[0:1, 0:E], ctp[0:1, :]), tc)
            free[7] = t_cnt

            def gather(e_, k):
                b = e_ % 3 if k == 0 else 3 + e_ % 2 if k == 1 else 3 + k
                v = e_ * NCH + k
                t = pool.dma(d_g[b], lambda e: e.indirect_dma_start(
                    out=GT[b], out_offset=None, in_=xnd,
                    in_offset=bass.IndirectOffsetOnAxis(ap=idx[:, v:v + 1], axis=0),
                    bounds_check=N - 1, oob_is_err=False), t_idx, t_xnd, mem["gt"][b], (d_g[b].sem, d_g[b].n), mem["work"])
                return b, t

            def scatter(e_, k, t):
                y = e_ % 2 if k == 0 else 1 + k
                v = K + e_ * NCH + k
                s = d_y[e_ % 2 if k == 0 else k + 1]
                t = pool.dma(s, lambda e: e.indirect_dma_start(
                    out=Y, out_offset=bass.IndirectOffsetOnAxis(ap=idx[:, v:v + 1], axis=0),
                    in_=YT[y], in_offset=None, bounds_check=2 * N - 1, oob_is_err=False), t)
                mem["yt"][y] = t

            def gathers(e_, ks):
                d_of = lambda k: d_g[e_ % 3 if k == 0 else 3 + e_ % 2 if k == 1 else 3 + k]
                for i, k in enumerate(ks):
                    if k:
                        pool.begin((L, e_), k, [d_of(j) for j in ks[i:]])
                    got[e_, k] = gather(e_, k)
                for k in ks:
                    if k:
                        pool.end()

            def scatters(e_):
                for k in range(1, NCH):
                    pool.begin((L, e_), k, d_y[k + 1:])
                    scatter(e_, k, t_o[e_, k])
                for k in range(1, NCH):
                    pool.end()

            got, t_o = {}, {}
            pool.wait(t_cnt)
            for e_ in range(E):
                pool.ops.append(("count", (L, e_), cnt[0:1, e_:e_ + 1]))
            gathers(0, [0])
            unhold(got[0, 0][1])
            gathers(1, [0])
            gathers(0, [1])
            gathers(0, [2, 3, 4])
            gathers(1, [1])
            tw = dve.do(lambda e: e.tensor_tensor(dw[:, :], mx[:, :, 0], mx[:, :, 1], ALU.subtract))
            act.do(lambda e: e.activation(wt[:, 0, :], dw[:, :], ACT.Sigmoid), tw)
            tw = act.do(lambda e: e.activation(wt[:, 1, :], dw[:, :], ACT.Sigmoid, scale=-1.0))
            t = dve.do(lambda e: e.tensor_tensor(
                tv, sv, wt[:, :, :].rearrange("p k (c o) -> p (k c) o", o=1).to_broadcast([TP, 2 * TC, E]), ALU.mult), tw)
            t = dve.do(lambda e: e.tensor_tensor(cw[:, :, 0:E], t12[:, 0:TC, 0:E], t12[:, TC:2 * TC, 0:E], ALU.add), t)
            for c in range(TC):
                b, o = (6, c * TP) if c < 4 else (7, 0)
                tt = pe.do(lambda e, c=c, b=b, o=o: e.transpose(
                    bank[b][0:E, o:o + TP], cw[:, c, 0:E], ident[0:TP, 0:TP]), t, free[b])
                if c == 3:
                    t6 = act.do(lambda e: e.activation(cwT[0:E, 0:4 * TP], bank[6][0:E, 0:4 * TP], ACT.Copy), tt)
            t7 = act.do(lambda e: e.activation(cwT[0:E, 4 * TP:N], bank[7][0:E, 0:TP], ACT.Copy), tt)
            free[6], free[7] = t6, t7
            if L in (1, 2):
                table(ACT.Silu)
            between(tT)
            for c in range(TC):
                last = not extra_bias
                t = pe.do(lambda e, c=c, last=last: e.matmul(
                    bank[c][0:TP, :], cwT[0:E, c * TP:(c + 1) * TP], b2[0:E, :], start=True, stop=last),
                    free[c], t7, t_b2, sig=last)
                if extra_bias:
                    t = extra_bias(c)
                xt[c] = free[c] = rows_out(bank[c][0:TP, :], c, t)
            mem["b2"] = t_pe()
            xnT_free.append(t_pe())

            def bring(e_, k):
                b, t_g = got[e_, k]
                x_ = e_ % 2 if k == 0 else 2
                tb = 7 if k == 0 and e_ % 2 else 0
                for d in range(DC):
                    t = pe.do(lambda e, d=d: e.transpose(
                        bank[tb][:, d * P:(d + 1) * P], GT[b][:, d * P:(d + 1) * P], ident[:, :]),
                        t_g, free[tb], sig=d == DC - 1)
                mem["gt"][b] = t
                free[tb] = dve.do(lambda e: e.tensor_copy(XG[x_], bank[tb][:, :]), t, mem["xg"][x_], mem["work"])
                return XG[x_], free[tb]

            def leave(e_, k, yb, t):
                y = e_ % 2 if k == 0 else 1 + k
                t = act.do(lambda e: e.activation(YT[y], bank[yb][:, :], ACT.Copy), t, mem["yt"][y], mem["work"])
                free[yb] = t
                return t

            ready = {e_: bring(e_, 0) for e_ in range(group)}
            for e0 in range(0, E, group):
                es = range(e0, e0 + group)
                second = []
                for e_ in es:
                    second.append(expert(e_, 1 + e_ % 2, *ready[e_]))
                    mem["xg"][e_ % 2] = t_pe()
                    if e_ + 2 < E:
                        gathers(e_ + 2, [0])
                for e_ in range(e0 + group, min(E, e0 + 2 * group)):
                    ready[e_] = bring(e_, 0)
                for e_, m2 in zip(es, second):
                    t_o[e_, 0] = leave(e_, 0, 1 + e_ % 2, m2())
                    scatter(e_, 0, t_o[e_, 0])
                for e_ in es:
                    for en in (pe, act, dve):
                        en.wait(t_cnt)
                        en.ops.append(("count", (L, e_), cnt[0:1, e_:e_ + 1]))
                    for k in range(1, NCH):
                        for en in (pe, act, dve):
                            en.begin((L, e_), k)
                        xg, t = bring(e_, k)
                        yb = 1 + (e_ + k) % 2
                        m2 = expert(e_, yb, xg, t)
                        mem["xg"][2] = t_pe()
                        t_o[e_, k] = leave(e_, k, yb, m2())
                    for en in (pe, act, dve):
                        for k in range(1, NCH):
                            en.end()
                    scatters(e_)
                    if e_ + 2 < E:
                        gathers(e_ + 2, [1])
                    if e_ + 1 < E:
                        gathers(e_ + 1, [2, 3, 4])
                    done(e_, hold if e_ >= E - group else release)
            table(ACT.Sqrt)
            t_y = [(d.sem, d.n) for d in d_y]
            mem["y"] = t_y
            t_last = [t_pe()] + [(d.sem, d.n) for d in d_g]
            for c in range(TC):
                for a, b in ((0, 120), (120, 125)):
                    t_c = act.dma(d_c[c], lambda e, a=a, b=b, c=c: e.dma_start(CMB[a:b, c], Yv[a:b, c]), t_y, t_last)
                for j in range(2):
                    xt[c] = dve.do(lambda e, c=c, j=j: e.scalar_tensor_tensor(
                        x[:, c, :], CMB[:, c, j, :], wt[:, j, c:c + 1], x[:, c, :], ALU.mult, ALU.add), t_c, xt[c], tw)
            unhold(t_c)
            mem["work"] = xt[TC - 1]
            mem["gt"] = [xt[TC - 1]] * 8

        def done(e_, rel):
            pass

        A = W[0:TP, 0:3125]
        AT = W[0:TP, 3125:6250].rearrange("p (c i) -> p c i", c=TC)
        t = act.do(lambda e: e.activation(spt[:, :, :], actp[:, :, :], ACT.Abs), t_in)
        t = act.do(lambda e: e.activation(spt[:, :, :], spt[:, :, :], ACT.Exp, scale=-1.0), t)
        t_ln = act.do(lambda e: e.activation(spt[:, :, :], spt[:, :, :], ACT.Ln, bias=onesf[:, 0:1]), t, t_ones)
        tef = dve.do(lambda e: e.tensor_copy(ef[:, :, :], esrc[:, :, :]), t_e)
        OH = W[0:TP, 7221:7221 + 6 * 313].bitcast(BF)
        oh_free = [None] * 3
        ts = []
        for c in range(EC):
            b = c % 3
            oh = [OH[:, (2 * b + i) * 626:(2 * b + i) * 626 + N] for i in range(2)]
            for i in range(2):
                t = dve.do(lambda e, i=i, c=c, oh=oh: e.tensor_scalar(
                    oh[i], iota[0:TP, :], ef[:, i, c:c + 1], None, ALU.is_equal), tef, t_io, oh_free[b])
            for m in range(TC):
                lhs = oh[1][:, m * TP:(m + 1) * TP]
                bb, o = (5, 113 * m) if m < 4 else (6, 0)
                pe.do(lambda e, m=m, lhs=lhs, c=c, oh=oh: e.matmul(
                    bank[m][0:TP, :], lhs, oh[0][:, 0:512], start=c == 0, stop=c == EC - 1), t, sig=False)
                t_A = pe.do(lambda e, m=m, lhs=lhs, c=c, oh=oh, bb=bb, o=o: e.matmul(
                    bank[bb][0:TP, o:o + 113], lhs, oh[0][:, 512:N], start=c == 0 and m in (0, 4),
                    stop=c == EC - 1, skip_group_check=True), sig=m == TC - 1)
            oh_free[b] = t_A
            if c >= 20 and c % 8 == 0 and len(ts) < TC:
                ts.append(ln_tile(len(ts)))
        t = dve.do(lambda e: e.scalar_tensor_tensor(spl[:, :, :], actp[:, :, :], 0.0, spt[:, :, :], ALU.max, ALU.add), t_ln, t_in)
        t_sp = dve.do(lambda e: e.tensor_scalar(ngc[:, :, :], spl[:, :, :], -1.0, None, ALU.mult), t)
        tT = []
        for m in range(TC):
            ev = lambda e, m=m: e.activation(AT[:, m, 0:512], bank[m][0:TP, :], ACT.Copy)
            if m % 2 == 0:
                free[m] = act.do(ev, t_A, t_pc)
            else:
                free[m] = dve.do(lambda e, m=m: e.tensor_copy(AT[:, m, 0:512], bank[m][0:TP, :]), t_A, t_pc)
            tT.append(xnT_tile(m, ts[m], [7, 0, 1, 2, 3]))
        xn_free.append(t_pe())
        t_at = dve.do(lambda e: e.tensor_copy(
            AT[:, 0:4, 512:N], bank[5][0:TP, 0:452].rearrange("p (m i) -> p m i", m=4)), t_A, t_pc)
        t_at2 = dve.do(lambda e: e.tensor_copy(AT[:, 4, 512:N], bank[6][0:TP, 0:113]))
        free[5], free[6] = t_at, t_at2
        ats = [free[0], free[1], free[2], free[3], free[4], t_at, t_at2]

        emb = W[0:TP, 6250:6250 + 2560].rearrange("p (c d) -> p c d", c=TC)
        wg0 = slot(w_l0g).rearrange("p (k d) -> p k d", k=DC)
        temb = []
        for c in range(TC):
            b = (4, 5, 6, 7, 0)[c]
            for d in range(DC):
                t = pe.do(lambda e, c=c, d=d, b=b: e.matmul(
                    bank[b][0:TP, :], xnT[:, d, c * TP:(c + 1) * TP], wg0[:, d, :], start=d == 0, stop=d == DC - 1),
                    tT[c], landed[w_l0g], free[b], sig=d == DC - 1)
            t = dve.do(lambda e, c=c, b=b: e.tensor_tensor(emb[:, c, :], bank[b][0:TP, :], vec(0), ALU.add), t, t_vec, t_pc)
            free[b] = t
            temb.append(t)
        release(w_l0g, t_pe())
        xnT_free.append(t_pe())
        t_Adone = []
        for g in range(7):
            b = (1, 2, 3, 4, 5, 6, 7)[g]
            n = min(4, 25 - 4 * g)
            for j in range(n):
                f = 4 * g + j
                a_, b_ = f // 5, f % 5
                t = pe.do(lambda e, b=b, j=j, a_=a_, b_=b_: e.transpose(
                    bank[b][0:TP, j * TP:(j + 1) * TP], AT[:, b_, a_ * TP:(a_ + 1) * TP], ident[0:TP, 0:TP]),
                    ats, free[b], sig=j == n - 1)
            free[b] = act.do(lambda e, g=g, b=b, n=n: e.activation(
                A[:, 500 * g:500 * g + n * TP], bank[b][0:TP, 0:n * TP], ACT.Copy), t)
            t_Adone.append(free[b])
        t_Atr = t
        scr = W[0:TP, 8810:8810 + 512]
        ttr = None
        for c in range(TC):
            for i in range(2):
                ttr = dve.do(lambda e, c=c, i=i: e.tensor_tensor_reduce(
                    scr, emb[:, c, :], vec(1 + i), 1.0, 0.0, ALU.mult, ALU.add, sT[:, i, c:c + 1]),
                    temb[c], ttr, oh_free)
        dgl = [W[0:TP, 9322 + TP * c:9322 + TP * (c + 1)] for c in range(TC)]
        xnf = xn[:, :, :].rearrange("p c d -> p (c d)")
        Sb = xnf[:, 0:N]
        ub = [xnf[:, N * (1 + i):N * (2 + i)] for i in range(3)]
        for c in range(TC):
            t = dve.do(lambda e, c=c: e.tensor_scalar(dgl[c], ident[0:TP, 0:TP], sT[:, 0, c:c + 1], None, ALU.mult), ttr, t_id)
            b, o = (5, c * TP) if c < 4 else (6, 0)
            tp = pe.do(lambda e, b=b, o=o, c=c: e.matmul(
                bank[b][0:TP, o:o + TP], onesf[0:TP, 0:TP], dgl[c], start=True, stop=True), t, free[b], t_ones)
        act.do(lambda e: e.activation(Sb[:, 0:500], bank[5][0:TP, 0:500], ACT.Copy), tp, xn_free)
        t_S = act.do(lambda e: e.activation(Sb[:, 500:N], bank[6][0:TP, 0:TP], ACT.Copy))
        free[5] = free[6] = t_S
        rsum = bank[7][0:TP, 0:TC]
        tu = [None] * 3
        for c in range(TC):
            u = ub[c % 3]
            t = act.do(lambda e, c=c, u=u: e.activation(u, Sb, ACT.Identity, bias=sT[:, 1, c:c + 1]), t_S, tu[c % 3])
            t = dve.do(lambda e, u=u: e.scalar_tensor_tensor(u, u, 0.1, u, ALU.mult, ALU.max), t)
            t = dve.do(lambda e, c=c, u=u: e.scalar_tensor_tensor(u, AT[:, c, :], 1e30, u, ALU.mult, ALU.min), t, ats)
            t = act.do(lambda e, u=u: e.activation(u, u, ACT.Exp), t)
            tu[c % 3] = t = dve.do(lambda e, c=c, u=u: e.tensor_tensor(AT[:, c, :], AT[:, c, :], u, ALU.mult), t, t_Atr)
            for i in range(TC):
                lhs = AT[:, c, i * TP:(i + 1) * TP]
                pe.do(lambda e, i=i, c=c, lhs=lhs: e.matmul(
                    bank[i][0:TP, :], lhs, emb[:, c, :], start=c == 0, stop=c == TC - 1),
                    t, temb, free[i], sig=False)
                tr_ = pe.do(lambda e, i=i, c=c, lhs=lhs: e.matmul(
                    rsum[:, i:i + 1], lhs, onesf[0:TP, 0:1], start=c == 0 and i == 0, stop=c == TC - 1,
                    skip_group_check=True), free[7], sig=i == TC - 1)
        t = dve.do(lambda e: e.reciprocal(sT[:, 2, :], rsum), tr_)
        free[7] = t
        for i in range(TC):
            xt[i] = free[i] = dve.do(lambda e, i=i: e.scalar_tensor_tensor(
                x[:, i, :], bank[i][0:TP, :], sT[:, 2, i:i + 1], x[:, i, :], ALU.mult, ALU.add), t, xt[i])
        xn_free.extend(tu)
        mem["work"] = xt[TC - 1]

        def swiglu(ei, G, U, S, H, t_gu, *tokens):
            p = lambda i: actp[:, ei, i:i + 1]
            t = dve.do(lambda e: e.tensor_scalar(G, G, ngc[:, ei, 3:4], spl[:, ei, 3:4], ALU.max, ALU.min), t_gu, t_sp)
            ts_ = act.do(lambda e: e.activation(S, G, ACT.Sigmoid, scale=p(0)), t)
            t1 = dve.do(lambda e: e.tensor_scalar(U, U, ngc[:, ei, 4:5], spl[:, ei, 4:5], ALU.max, ALU.min))
            t1 = dve.do(lambda e: e.scalar_tensor_tensor(U, U, p(2), G, ALU.add, ALU.mult), t1, t)
            return dve.do(lambda e: e.scalar_tensor_tensor(H, U, p(1), S, ALU.mult, ALU.mult), t1, ts_, *tokens)

        shT = HT[:, 0:1875].rearrange("p (f n) -> p f n", f=3)

        def shared(tT):
            w1 = slot(w_sh1).rearrange("p (k f) -> p k f", k=DC)
            th = []
            for h0, n in ((0, 313), (313, 312)):
                base = 10805
                G, U, S = (W[:, base + 939 * i:base + 939 * i + 3 * n] for i in range(3))
                tg = []
                for f in range(6):
                    for d in range(DC):
                        t = pe.do(lambda e, f=f, d=d, h0=h0, n=n: e.matmul(
                            bank[f][:, 0:n], w1[:, d, f * P:(f + 1) * P], xnT[:, d, h0:h0 + n],
                            start=d == 0, stop=d == DC - 1), tT, landed[w_sh1], free[f], sig=d == DC - 1)
                    dst = (G if f < 3 else U)[:, (f % 3) * n:(f % 3 + 1) * n]
                    bias = b1[0][:, 96 + f:97 + f]
                    if f < 3:
                        t = act.do(lambda e, f=f, n=n, dst=dst, bias=bias: e.activation(
                            dst, bank[f][:, 0:n], ACT.Identity, bias=bias), t, t_in, th, mem["work"])
                    else:
                        t = dve.do(lambda e, f=f, n=n, dst=dst, bias=bias: e.tensor_scalar(
                            dst, bank[f][:, 0:n], bias, None, ALU.add), t, t_in, th, mem["work"])
                    free[f] = t
                    tg.append(t)
                Hv = shT[:, :, h0:h0 + n]
                v3 = lambda a: a.rearrange("p (f n) -> p f n", f=3)
                th.append(swiglu(16, v3(G), v3(U), v3(S), Hv, tg))
            release(w_sh1, t_pe())
            mem["sh"] = th
            mem["yt"] = [list(th) for _ in range(6)]

        def shared_rows(c):
            w2 = slot(w_sh2).rearrange("p (k d) -> p k d", k=3)
            pe.do(lambda e: e.matmul(bank[c][0:TP, :], onesf[0:1, 0:TP], b2s[:, :], start=False, stop=False), t_in, sig=False)
            for f in range(3):
                t = pe.do(lambda e, f=f: e.matmul(bank[c][0:TP, :], shT[:, f, c * TP:(c + 1) * TP], w2[:, f, :],
                                                  start=False, stop=f == 2), mem["sh"], landed[w_sh2], sig=f == 2)
            if c == TC - 1:
                release(w_sh2, t)
                mem["work"] = t
            return t

        def mm1(psum, w, cols, xg, *tokens):
            for j, f in enumerate(cols):
                for d in range(DC):
                    last = j == len(cols) - 1 and d == DC - 1
                    t2 = pe.do(lambda e, j=j, f=f, d=d: e.matmul(
                        psum[:, j * P:(j + 1) * P], w[:, d, f * P:(f + 1) * P], xg[:, d * P:(d + 1) * P],
                        start=d == 0, stop=d == DC - 1), *tokens, sig=last)
            return t2

        def mm2(yb, H, w, hs, first, last, *tokens):
            for j, h in enumerate(hs):
                t2 = pe.do(lambda e, j=j, h=h: e.matmul(
                    bank[yb][:, :], H[:, h * P:(h + 1) * P], w[:, j, :],
                    start=first and j == 0, stop=last and j == len(hs) - 1), *tokens, sig=j == len(hs) - 1)
            return t2

        wv = lambda n, k: slot(n).rearrange("p (k f) -> p k f", k=k)

        def expert0(e_, yb, xg, t_x):
            n1, n2 = w_l0[e_]
            w1 = wv(n1, DC)
            w2 = wv(n2, 6)[:, 3 * (e_ % 2):3 * (e_ % 2) + 3, :]
            q = e_ % 2
            gb, ub = (3, 4) if q else (5, 6)
            H = HT[:, 384 * q:384 * q + 384]
            G, U, S = ((HT[:, 768:1920] if q else TMP)[:, 384 * i:384 * i + 384] for i in range(3))
            tg = mm1(bank[gb], w1, [0, 1, 2], xg, t_x, landed[n1], free[gb])
            for j in range(3):
                t = act.do(lambda e, j=j: e.activation(G[:, j * P:(j + 1) * P], bank[gb][:, j * P:(j + 1) * P],
                                                       ACT.Identity, bias=b1[0][:, e_ * 6 + j:e_ * 6 + j + 1]),
                           tg, mem.get(("h", q)), mem["work"])
            free[gb] = t
            tu = mm1(bank[ub], w1, [3, 4, 5], xg, t_x, free[ub])
            for j in range(3):
                t2 = dve.do(lambda e, j=j: e.tensor_scalar(U[:, j * P:(j + 1) * P], bank[ub][:, j * P:(j + 1) * P],
                                                           b1[0][:, e_ * 6 + 3 + j:e_ * 6 + 4 + j], None, ALU.add),
                            tu, mem.get(("h", q)), mem["work"])
            free[ub] = t2
            th = swiglu(e_, G, U, S, H, [t, t2], mem.get(("hp", q)))
            mem["h", q] = th

            def second():
                t = mm2(yb, H, w2, [0, 1, 2], True, True, th, landed[n2], free[yb])
                mem["hp", q] = mem["hp"] = t
                return t
            return second

        def expert1(e_, yb, xg, t_x):
            na, nb, n2 = w_l1[e_]
            w2 = wv(n2, 8)
            tg = []
            for g, n1 in enumerate((na, nb)):
                w1 = wv(n1, DC)
                hb, ub = 3 + 2 * g, 4 + 2 * g
                S = TMP[:, 512 * g:512 * g + 512]
                th = mm1(bank[hb], w1, [0, 1, 2, 3], xg, t_x, landed[n1], free[hb])
                tS = []
                for j in range(4):
                    c = e_ * 16 + 4 * g + j
                    tS.append(act.do(lambda e, j=j, c=c, S=S, hb=hb: e.activation(
                        S[:, j * P:(j + 1) * P], bank[hb][:, j * P:(j + 1) * P], ACT.Silu, bias=b1[1][:, c:c + 1]),
                        th, mem.get(("s", g)), mem["work"]))
                free[hb] = tS[-1]
                tu = mm1(bank[ub], w1, [4, 5, 6, 7], xg, t_x, free[ub])
                for j in range(4):
                    c = e_ * 16 + 8 + 4 * g + j
                    h = 4 * g + j
                    t = dve.do(lambda e, j=j, c=c, h=h, S=S, ub=ub: e.scalar_tensor_tensor(
                        HT[:, h * P:(h + 1) * P], bank[ub][:, j * P:(j + 1) * P], b1[1][:, c:c + 1],
                        S[:, j * P:(j + 1) * P], ALU.add, ALU.mult), tu, tS[j], mem.get("hp"), mem["work"])
                free[ub] = t
                mem[("s", g)] = t
                tg.append(t)

            def second():
                mm2(yb, HT, w2[:, 0:4, :], [0, 1, 2, 3], True, False, tg[0], landed[n2], free[yb])
                mem["hp"] = mm2(yb, HT, w2[:, 4:8, :], [4, 5, 6, 7], False, True, tg[1])
                return mem["hp"]
            return second

        def expert2(e_, yb, xg, t_x):
            n1, n2 = w_l2[e_][0:2], w_l2[e_][2:4]
            tg = []
            for g in range(4):
                w1 = wv(n1[g // 2], DC)
                hb = 3 + g
                th = mm1(bank[hb], w1, [4 * (g % 2) + j for j in range(4)], xg, t_x, landed[n1[g // 2]], free[hb])
                for j in range(4):
                    h = 4 * g + j
                    t = act.do(lambda e, j=j, h=h, hb=hb: e.activation(
                        HT[:, h * P:(h + 1) * P], bank[hb][:, j * P:(j + 1) * P], ACT.Silu,
                        bias=b1[2][:, e_ * 16 + h:e_ * 16 + h + 1]), th, mem.get("hp"), mem["work"])
                free[hb] = t
                tg.append(t)

            def second():
                for g in range(4):
                    w2 = wv(n2[g // 2], 8)
                    t = mm2(yb, HT, w2[:, 4 * (g % 2):4 * (g % 2) + 4, :], [4 * g + j for j in range(4)], g == 0, g == 3,
                            tg[g], landed[n2[g // 2]], free[yb])
                mem["hp"] = t
                return t
            return second

        def expert3(e_, yb, xg, t_x):
            n1, n2 = w_l3[e_]
            w1, w2 = wv(n1, DC), wv(n2, 8)
            tg = []
            for g in range(2):
                hb = 3 + 2 * g + (yb - 1)
                th = mm1(bank[hb], w1, [4 * g + j for j in range(4)], xg, t_x, landed[n1], free[hb])
                for j in range(4):
                    h = 4 * g + j
                    t = dve.do(lambda e, j=j, h=h, hb=hb: e.tensor_scalar(
                        HT[:, h * P:(h + 1) * P], bank[hb][:, j * P:(j + 1) * P],
                        b1[3][:, e_ * 8 + h:e_ * 8 + h + 1], 0.0, ALU.add, ALU.max), th, mem.get("hp"), mem["work"])
                free[hb] = t
                tg.append(t)

            def second():
                mm2(yb, HT, w2[:, 0:4, :], [0, 1, 2, 3], True, False, tg[0], landed[n2], free[yb])
                mem["hp"] = mm2(yb, HT, w2[:, 4:8, :], [4, 5, 6, 7], False, True, tg[1])
                return mem["hp"]
            return second

        def done(e_, rel):
            if e_ % 2 == 0:
                rel(w_l0[e_][0], t_pe())
            else:
                rel(w_l0[e_][1], t_pe())
                rel(w_l0[e_][0], t_pe())

        moe(0, 16, I["L0_b2"], expert0, shared, shared_rows, group=2)

        t_vec = load_vecs(("L1_gnn_bias", "L1_gnn_gamma", "L1_gnn_beta"), mem["work"])
        ts, tT = layernorm()
        Av = A.rearrange("p (c i) -> p c i", c=TC)
        halves = ((0, 313), (313, 312))
        rdeg = W[:, 6209:6209 + N]
        for h, (h0, n) in enumerate(halves):
            for c in range(TC):
                t = pe.do(lambda e, h=h, h0=h0, n=n, c=c: e.matmul(
                    bank[5 + h][:, 0:n], onesf[0:TP, :], Av[:, c, h0:h0 + n], start=c == 0, stop=c == TC - 1),
                    free[5 + h], t_Adone, sig=c == TC - 1)
            t = dve.do(lambda e, h=h, h0=h0, n=n: e.tensor_scalar(
                rdeg[:, h0:h0 + n], bank[5 + h][:, 0:n], 1.0, None, ALU.max), t, mem["work"])
            free[5 + h] = t
        t_rd = dve.do(lambda e: e.reciprocal(rdeg, rdeg), t)
        nmT = W[:, 3125:3125 + 2500].rearrange("p (k n) -> p k n", k=DC)
        tn = []
        for m in range(DC):
            for h, (h0, n) in enumerate(halves):
                b = (2 * m + h) % 8
                for c in range(TC):
                    t = pe.do(lambda e, m=m, b=b, h0=h0, n=n, c=c: e.matmul(
                        bank[b][:, 0:n], xn[:, c, m * P:(m + 1) * P], Av[:, c, h0:h0 + n],
                        start=c == 0, stop=c == TC - 1), ts[c], free[b], sig=c == TC - 1)
                free[b] = dve.do(lambda e, m=m, b=b, h0=h0, n=n: e.tensor_tensor(
                    nmT[:, m, h0:h0 + n], bank[b][:, 0:n], rdeg[:, h0:h0 + n], ALU.mult), t, t_rd, mem["work"])
                tn.append(free[b])
        xn_free.append(t_pe())
        hrow = W[0:TP, 6840:6840 + 2560].rearrange("p (c d) -> p c d", c=TC)

        def norm_rows(c, psum, t, t_vec):
            h = hrow[:, c, :]
            tf = t = dve.do(lambda e: e.tensor_tensor(h, psum, vec(0), ALU.add), t, t_vec, mem["work"])
            t = dve.do(lambda e: e.bn_stats(stats[:, c, :], h), t)
            t = dve.do(lambda e: e.bn_aggr(mv[:, c, :], stats[:, c, :]), t)
            tr = act.do(lambda e: e.activation(rstd[:, c:c + 1], mv[:, c, 1:2], ACT.Sqrt, bias=eps[0:TP, :]), t, t_eps, xn_free)
            t = dve.do(lambda e: e.scalar_tensor_tensor(h, h, mv[:, c, 0:1], vec(1), ALU.subtract, ALU.mult), t)
            tr = dve.do(lambda e: e.reciprocal(rstd[:, c:c + 1], rstd[:, c:c + 1]), tr)
            xt[c] = dve.do(lambda e: e.scalar_tensor_tensor(
                x[:, c, :], h, rstd[:, c:c + 1], x[:, c, :], ALU.mult, ALU.add), t, tr, xt[c])
            return tf

        def add_beta(ts):
            for c in range(TC):
                xt[c] = pool.do(lambda e, c=c: e.tensor_tensor(x[:, c, :], x[:, c, :], vec(2), ALU.add), ts[c], t_vec)

        add_beta(ts)
        wg1 = wv(w_l1g, 8)
        for c in range(TC):
            for d in range(8):
                lhs = (xnT if d < DC else nmT)[:, d % DC, c * TP:(c + 1) * TP]
                t = pe.do(lambda e, c=c, d=d, lhs=lhs: e.matmul(bank[c][0:TP, :], lhs, wg1[:, d, :], start=d == 0, stop=d == 7),
                          tT[c], tn, landed[w_l1g], free[c], sig=d == 7)
            free[c] = norm_rows(c, bank[c][0:TP, :], t, t_vec)
        hold(w_l1g, t_pe())
        xnT_free.append(t_pe())
        mem["work"] = xt[TC - 1]
        mem["gt"] = [mem["work"]] * 8

        def edges(tT):
            OF = [W[0:TP, 8757 + 625 * i:8757 + 625 * (i + 1)] for i in range(4)]
            fr = [None] * 4
            for c in range(EC):
                b = c % 4
                t = dve.do(lambda e, b=b, c=c: e.tensor_scalar(
                    OF[b], iota[0:TP, :], ef[:, 1, c:c + 1], None, ALU.is_equal), fr[b], mem["work"])
                n, o = (w_ea[0], c) if c < 42 else (w_ea[1], c - 42)
                lhs = slot(n)[:, o * 96:(o + 1) * 96]
                for h, (h0, nn) in enumerate(halves):
                    t2 = pe.do(lambda e, b=b, c=c, lhs=lhs, h=h, h0=h0, nn=nn: e.matmul(
                        bank[h][0:96, 0:nn], lhs, OF[b][:, h0:h0 + nn], start=c == 0, stop=c == EC - 1),
                        t, landed[n], free[h], sig=h == 1)
                fr[b] = t2
                if c in (41, 84):
                    release(n, t2)
            for h, (h0, nn) in enumerate(halves):
                free[h] = act.do(lambda e, h=h, h0=h0, nn=nn: e.activation(
                    aggT[:, h0:h0 + nn], bank[h][0:96, 0:nn], ACT.Copy), t2)
            mem["agg"] = free[1]
            mem["work"] = t2

        def done(e_, rel):
            for n in w_l1[e_]:
                rel(n, t_pe())

        moe(1, 8, I["L1_b2"], expert1, edges, None)

        t_vec = load_vecs(("L2_gnn_b3", "L2_gnn_gamma", "L2_gnn_beta"), mem["work"])
        ts, tT = layernorm()
        add_beta(ts)
        h1 = W[:, 0:5000].rearrange("p (f n) -> p f n", f=8)
        w1a, w1b = wv(w_l2g[0], DC), slot(w_l2g[1])
        th1 = []
        for f in range(8):
            for h, (h0, n) in enumerate(halves):
                b = (2 * f + h) % 8
                for d in range(DC + 1):
                    lhs = w1a[:, d, f * P:(f + 1) * P] if d < DC else w1b[:, f * P:(f + 1) * P]
                    rhs = xnT[:, d, h0:h0 + n] if d < DC else aggT[:, h0:h0 + n]
                    t = pe.do(lambda e, b=b, n=n, d=d, lhs=lhs, rhs=rhs: e.matmul(
                        bank[b][:, 0:n], lhs, rhs, start=d == 0, stop=d == DC), tT, mem["agg"],
                        landed[w_l2g[0]], landed[w_l2g[1]], free[b], sig=d == DC)
                free[b] = act.do(lambda e, b=b, n=n, h0=h0, f=f: e.activation(
                    h1[:, f, h0:h0 + n], bank[b][:, 0:n], ACT.Relu, bias=gb1[:, f:f + 1]), t, t_in, mem["work"])
                th1.append(free[b])
        release(w_l2g[0], t_pe())
        release(w_l2g[1], t_pe())
        t_h1 = t_pe()
        w3 = wv(w_l2g[4], 8)
        th2_free = [t_h1]
        h2f = xnT[:, :, :].rearrange("p k n -> p (k n)")
        for g, (c0, c1) in enumerate(((0, 2), (2, 4), (4, 5))):
            h0, n = c0 * TP, (c1 - c0) * TP
            hv = h2f[:, 0:8 * n].rearrange("p (f n) -> p f n", f=8)
            th2 = []
            for f in range(8):
                b = f
                for d in range(8):
                    w2 = wv(w_l2g[2 + d // 4], DC)
                    t = pe.do(lambda e, b=b, n=n, d=d, f=f, h0=h0, w2=w2: e.matmul(
                        bank[b][:, 0:n], w2[:, d % 4, f * P:(f + 1) * P], h1[:, d, h0:h0 + n],
                        start=d == 0, stop=d == 7), th1, landed[w_l2g[2]], landed[w_l2g[3]], free[b], sig=d == 7)
                free[b] = act.do(lambda e, b=b, n=n, f=f, hv=hv: e.activation(
                    hv[:, f, :], bank[b][:, 0:n], ACT.Relu, bias=gb1[:, 8 + f:9 + f]), t, th2_free)
                th2.append(free[b])
            for c in range(c0, c1):
                b = c
                for f in range(8):
                    t = pe.do(lambda e, b=b, f=f, c=c, hv=hv, c0=c0: e.matmul(
                        bank[b][0:TP, :], hv[:, f, (c - c0) * TP:(c - c0 + 1) * TP], w3[:, f, :],
                        start=f == 0, stop=f == 7), th2, landed[w_l2g[4]], free[b], sig=f == 7)
                free[b] = norm_rows(c, bank[b][0:TP, :], t, t_vec)
            th2_free = [t_pe()]
        for n in w_l2g[2:5]:
            hold(n, t_pe())
        xnT_free.append(t_pe())
        mem["work"] = xt[TC - 1]
        mem["gt"] = [mem["work"]] * 8

        def done(e_, rel):
            for n in w_l2[e_]:
                rel(n, t_pe())

        moe(2, 8, I["L2_b2"], expert2, lambda tT: None, None)

        ts, tT = layernorm()
        xnT_free.append(tT)
        inv = sT[:, 3, :]
        t_inv = dve.do(lambda e: e.reciprocal(inv, cs), t_seg)
        B3 = W[0:TP, 0:3125].rearrange("p (c i) -> p c i", c=TC)
        dgs = [W[0:TP, 3125 + TP * i:3125 + TP * (i + 1)] for i in range(TC)]
        for c in range(TC):
            t = dve.do(lambda e, c=c: e.tensor_scalar(dgs[c], ident[0:TP, 0:TP], gg[:, c:c + 1], None, ALU.mult),
                       t_seg, mem["work"])
            b, o = (5, c * TP) if c < 4 else (6, 0)
            t = pe.do(lambda e, b=b, o=o, c=c: e.matmul(
                bank[b][0:TP, o:o + TP], onesf[0:TP, 0:TP], dgs[c], start=True, stop=True), t, free[b])
        tB = []
        for c in range(TC):
            dve.do(lambda e, c=c: e.tensor_scalar(B3[:, c, 0:500], bank[5][0:TP, 0:500], sg[:, c:c + 1], None, ALU.is_equal), t)
            tB.append(dve.do(lambda e, c=c: e.tensor_scalar(B3[:, c, 500:N], bank[6][0:TP, 0:TP], sg[:, c:c + 1], None, ALU.is_equal)))
        free[5] = free[6] = tB[-1]
        for i in range(TC):
            for j in range(TC):
                t = pe.do(lambda e, i=i, j=j: e.matmul(
                    bank[i][0:TP, :], B3[:, j, i * TP:(i + 1) * TP], xn[:, j, :], start=j == 0, stop=j == TC - 1),
                    ts[j], tB[j], free[i], sig=j == TC - 1)
            xt[i] = free[i] = dve.do(lambda e, i=i: e.scalar_tensor_tensor(
                x[:, i, :], bank[i][0:TP, :], inv[:, i:i + 1], x[:, i, :], ALU.mult, ALU.add), t, xt[i], t_inv)
        xn_free.append(t_pe())
        mem["work"] = [mem["work"], t_pe()]

        def done(e_, rel):
            for n in w_l3[e_]:
                rel(n, t_pe())

        moe(3, 8, I["L3_b2"], expert3, lambda tT: None, None)

        for c in range(TC):
            for a, b in ((0, 120), (120, 125)):
                t_out = act.dma(d_out, lambda e, a=a, b=b, c=c: e.dma_start(out_v[a:b, c, :], x[a:b, c, :]), xt[c])
        act.wait(t_out)

        block = ctx.enter_context(nc.Block())

        @block.sync
        def _(eng):
            sp.emit(eng)

        @block.gpsimd
        def _(eng):
            pool.emit(eng)

        @block.scalar
        def _(eng):
            act.emit(eng)

        @block.vector
        def _(eng):
            dve.emit(eng)

        @block.tensor
        def _(eng):
            pe.emit(eng)


def kernel(**a):
    import numpy as np
    import concourse.bacc as bacc
    from concourse.bass_utils import run_bass_kernel_spmd

    a = {k: np.asarray(v) for k, v in a.items()}

    def blocks(w):
        *lead, k, f = w.shape
        w = w.reshape(*lead, k // P, P, f)
        return np.moveaxis(w, -2, -3).reshape(*lead, P, k // P * f)

    def split_gu(w):
        return np.concatenate([w[..., 0::2], w[..., 1::2]], -1)

    def cols(b):
        return b.reshape(-1, P).T

    row = lambda v: v.reshape(1, -1)
    ins = {
        "x": a["x"], "src": a["src"], "dst": a["dst"],
        "L0_gnn_W": blocks(a["L0_gnn_W"]), "L0_gnn_b": row(a["L0_gnn_b"]),
        "L0_a_src": row(a["L0_gnn_a"][:D]), "L0_a_dst": row(a["L0_gnn_a"][D:]),
        "act": row(np.concatenate([a["L0_ffn_expert_act"], a["L0_ffn_shared_act"][None]], 0)),
        "sh_w1": blocks(split_gu(a["L0_ffn_shared_w1"])), "sh_w2": blocks(a["L0_ffn_shared_w2"]),
        "sh_b2": row(a["L0_ffn_shared_b2"]),
        "L0_w1": blocks(split_gu(a["L0_ffn_expert_w1"])),
        "L0_w2": np.concatenate([blocks(a["L0_ffn_expert_w2"][0::2]), blocks(a["L0_ffn_expert_w2"][1::2])], -1),
        "L0_b1": cols(split_gu(np.concatenate([a["L0_ffn_expert_b1"], a["L0_ffn_shared_b1"][None]], 0))),
        "L0_b2": a["L0_ffn_expert_b2"],
        "L1_gnn_W": blocks(np.concatenate([a["L1_gnn_W_self"].T, a["L1_gnn_W_neigh"].T], 0)),
        "L1_gnn_bias": row(a["L1_gnn_bias"]), "L1_gnn_gamma": row(a["L1_gnn_gamma"]), "L1_gnn_beta": row(a["L1_gnn_beta"]),
        "L1_b1": cols(a["L1_ffn_fc1_b"]), "L1_b2": a["L1_ffn_fc2_b"],
        "L1_w2": blocks(np.swapaxes(a["L1_ffn_fc2_w"], 1, 2)),
        "L2_gnn_W1a": blocks(a["L2_gnn_W1"][:D]), "L2_gnn_W1b": a["L2_gnn_W1"][D:],
        "L2_gnn_W2": blocks(a["L2_gnn_W2"].reshape(2, 512, 1024)), "L2_gnn_W3": blocks(a["L2_gnn_W3"]),
        "L2_gnn_b": cols(np.stack([a["L2_gnn_b1"], a["L2_gnn_b2"]])),
        "L2_gnn_b3": row(a["L2_gnn_b3"]), "L2_gnn_gamma": row(a["L2_gnn_gamma"]), "L2_gnn_beta": row(a["L2_gnn_beta"]),
        "L2_w1": blocks(np.moveaxis(a["L2_ffn_W1"].reshape(8, D, 2, 1024), 2, 1)),
        "L2_w2": blocks(a["L2_ffn_W2"].reshape(8, 2, 1024, D)),
        "L2_b1": cols(a["L2_ffn_b1"]), "L2_b2": a["L2_ffn_b2"],
        "L3_w1": blocks(a["L3_ffn_w1"]), "L3_w2": blocks(a["L3_ffn_w2"]),
        "L3_b1": cols(a["L3_ffn_b1"]), "L3_b2": a["L3_ffn_b2"],
        "L0_gb": row(a["L0_ffn_gate_b"]), "L1_gb": row(a["L1_ffn_router_b"]),
        "L2_gb": row(a["L2_ffn_bg"]), "L3_gb": row(a["L3_ffn_gate_b"]),
    }
    f1 = np.swapaxes(a["L1_ffn_fc1_w"], 1, 2).reshape(8, D, 2, 2, 512)
    ins["L1_w1"] = blocks(np.ascontiguousarray(np.transpose(f1, (0, 3, 1, 2, 4))).reshape(8, 2, D, 1024))
    for nm, g in (("L0", a["L0_ffn_gate_w"]), ("L1", a["L1_ffn_router_w"].T), ("L2", a["L2_ffn_Wg"]), ("L3", a["L3_ffn_gate_w"])):
        ins[nm + "_gate"] = np.moveaxis(g.reshape(DC, P, -1), 1, 0)
    ea = a["edge_attr_96"].reshape(TP, EC, 96)
    ins["ea0"] = ea[:, :42].reshape(TP, -1)
    ins["ea1"] = ea[:, 42:].reshape(TP, -1)

    nc = bacc.Bacc("TRN2", target_bir_lowering=False, num_devices=1)
    arrays, aps = {}, {}
    for k, v in ins.items():
        v = np.ascontiguousarray(v)
        arrays["in_" + k] = v
        aps[k] = nc.dram_tensor("in_" + k, v.shape, mybir.dt.from_np(v.dtype), kind="ExternalInput").ap()
    out = nc.dram_tensor("out_x", (N, D), F32, kind="ExternalOutput").ap()
    program(nc, aps, out)
    r = run_bass_kernel_spmd(nc, [arrays], core_ids=[0])
    return r.results[0]["out_x"]
```

```python
from contextlib import ExitStack

import concourse.bass as bass
from concourse import mybir

F32 = mybir.dt.float32
BF = mybir.dt.bfloat16
F16 = mybir.dt.float16
F32R = mybir.dt.float32r
I32 = mybir.dt.int32
U32 = mybir.dt.uint32
ALU = mybir.AluOpType
ACT = mybir.ActivationFunctionType
AX = mybir.AxisListType

N, D, P, TP, TC = 625, 512, 128, 125, 5
NE, EC = 10625, 85
DC = D // P
SLOTW, NSLOT = 4128, 6
CH, NCH = 128, 5
NEAR = 24
FAR = 1 << 20
WORK = 15541
WIDTHS = (128, 144, 160, 224, 256, 288, 320)
WIDE = WIDTHS[-1]


class Eng:

    def __init__(self, sem):
        self.sem, self.n, self.ops, self.seen, self.stack = sem, 0, [], {}, []

    def wait(self, *tokens):
        for t in tokens:
            if t is None:
                continue
            if isinstance(t, list):
                self.wait(*t)
                continue
            sem, v = t
            if v > 0 and self.seen.get(sem.name, 0) < v:
                self.seen[sem.name] = v
                self.ops.append(("wait", sem, v))

    def do(self, fn, *tokens, sig=True):
        self.wait(*tokens)
        if sig:
            self.n += 1
        self.ops.append(("do", fn, self.sem if sig else None, 1))
        return (self.sem, self.n) if sig else None

    def dma(self, d, fn, *tokens):
        self.wait(*tokens)
        d.n += 16
        self.ops.append(("do", fn, d.sem, 16))
        return (d.sem, d.n)

    def begin(self, e, k, dmas=()):
        self.stack.append((e, k, self.ops, self.n, dict(self.seen), [(d, d.n) for d in dmas]))
        self.ops = []

    def end(self):
        e, k, outer, n, seen, dmas = self.stack.pop()
        outer.append(("if", e, k, self.ops, self.n - n, [(d.sem, v, d.n - v) for d, v in dmas if d.n > v]))
        self.ops, self.seen = outer, seen

    def lift(self, n):
        if n > self.n:
            if self.ops and self.ops[-1][0] == "do" and self.ops[-1][2] is self.sem:
                _, fn, sem, inc = self.ops[-1]
                self.ops[-1] = ("do", fn, sem, inc + n - self.n)
            else:
                self.ops.append(("pad", n - self.n))
        self.n = n

    def emit(self, eng, ops=None, regs=None):
        regs = {} if regs is None else regs
        for op in self.ops if ops is None else ops:
            if op[0] == "wait":
                eng.wait_ge(op[1], op[2])
            elif op[0] == "do":
                ins = op[1](eng)
                if op[2] is not None:
                    ins.then_inc(op[2], op[3])
            elif op[0] == "pad":
                eng.drain().then_inc(self.sem, op[1])
            elif op[0] == "count":
                regs[op[1]] = eng.value_load(op[2], min_val=0, max_val=N)
            elif op[0] == "either":
                _, e, bodies = op
                for i, (body, inc) in enumerate(bodies):
                    with eng.If(regs[e] > 0) if i == 0 else eng.Else():
                        self.emit(eng, body, regs)
                        if inc:
                            eng.drain().then_inc(self.sem, inc)
            elif op[0] == "widths":
                self.narrowest(eng, op[1], list(zip(WIDTHS + (N,), op[2])), regs)
            else:
                _, e, k, body, inc, skipped = op
                with eng.If(regs[e] > CH * k):
                    self.emit(eng, body, regs)
                with eng.Else():
                    for sem, before, more in skipped:
                        eng.wait_ge(sem, before)
                        eng.inc_swdge_sem([sem], [more])
                    if inc:
                        eng.drain().then_inc(self.sem, inc)

    def narrowest(self, eng, e, bodies, regs):
        if len(bodies) == 1:
            self.emit(eng, bodies[0][1], regs)
            return
        half = len(bodies) // 2
        with eng.If(regs[e] > bodies[half - 1][0]):
            self.narrowest(eng, e, bodies[half:], regs)
        with eng.Else():
            self.narrowest(eng, e, bodies[:half], regs)


def either(engs, e, general, usual):
    start = [(en.n, en.seen, en.ops) for en in engs]
    made = []
    for f in (general, usual):
        for en, (n, seen, _) in zip(engs, start):
            en.n, en.seen, en.ops = n, dict(seen), []
        f()
        made.append([(en.ops, en.n) for en in engs])
    for i, (en, (_, seen, ops)) in enumerate(zip(engs, start)):
        n = max(m[i][1] for m in made)
        ops.append(("either", e, [(m[i][0], n - m[i][1]) for m in made]))
        en.n, en.seen, en.ops = n, seen, ops


class Dma:
    def __init__(self, sem):
        self.sem, self.n = sem, 0


def program(nc, I, out):
    ctx = ExitStack()
    with ctx:
        def sb(name, shape, dt=F32):
            return ctx.enter_context(nc.sbuf_tensor(name, shape, dt))

        def sem(name):
            return ctx.enter_context(nc.semaphore(name))

        def dram(name, shape, dt=F32):
            return nc.dram_tensor(name, shape, dt, kind="Internal").ap()

        pe, act, dve, pool, sp = (Eng(sem("s_" + n)) for n in ("pe", "act", "dve", "pool", "sp"))
        bank = [ctx.enter_context(nc.psum_tensor(f"bank{i}", [P, 512], F32)) for i in range(8)]
        free = [None] * 8

        with nc.sbuf_tensor("work_r", [P, WORK], F32R) as R:
            pass
        W = sb("work", [P, WORK])
        ring = sb("ring", [P, NSLOT * SLOTW])
        x = sb("x", [TP, TC, D])
        xn = sb("xn", [TP, TC, D])
        xnT = sb("xnT", [P, DC, N])
        ident = sb("ident", [P, P])
        onesf = sb("onesf", [P, P])
        onesb = sb("onesb", [P, P], BF)
        upper = sb("upper", [P, P], BF)
        iota = sb("iota", [P, 632], F16)
        iotaE = sb("iotaE", [P, 16])
        tok = sb("tok", [TP, TC], I32)
        tokf = sb("tokf", [TP, TC])
        eps = sb("eps", [P, 1])
        gate = sb("gate", [P, 4, DC, 16])
        gbias = sb("gbias", [P, 4, 16])
        b1 = [sb(f"b1_{i}", [P, n]) for i, n in enumerate((17 * 6, 8 * 16, 8 * 16, 8 * 8))]
        gb1 = sb("gb1", [P, 16])
        actp = sb("actp", [P, 17, 5])
        spl = sb("spl", [P, 17, 5])
        spt = sb("spt", [P, 17, 5])
        ngc = sb("ngc", [P, 17, 5])
        b2 = sb("b2", [16, D])
        cwT = sb("cwT", [16, N])
        aggT = sb("aggT", [96, N])
        b2s = aggT[0:1, 0:D]
        stats = sb("stats", [TP, TC, 6])
        mv = sb("mv", [TP, TC, 2])
        rstd = sb("rstd", [TP, TC])
        nmr = sb("nmr", [TP, TC])
        lg = sb("lg", [TP, TC, 16])
        mx = sb("mx", [TP, TC, 8])
        ix = sb("ix", [TP, TC, 8], U32)
        ixf = sb("ixf", [TP, 2, TC])
        s12 = sb("s12", [TP, 2 * TC, 16])
        t12 = sb("t12", [TP, 2 * TC, 16])
        sel = sb("sel", [TP, TC * 16], BF)
        rk = sb("rk", [TP, 2, TC])
        kk = sb("kk", [TP, 4, 2 * TC])
        dw = sb("dw", [TP, TC])
        wt = sb("wt", [TP, 2, TC])
        cw = sb("cw", [TP, TC, 16])
        cnt = sb("cnt", [1, 16], I32)
        idx = sb("idx", [P, 160], I32)
        idz = sb("idz", [P, 160])
        tok1 = sb("tok1", [TP, 1, TC])
        seg = sb("seg", [TP, 12, TC])
        segi = sb("segi", [TP, 4, TC], I32)
        esrc = sb("esrc", [TP, 2, EC], I32)
        ef = sb("ef", [TP, 2, EC])
        edge = W[0:TP, 10118:10118 + EC]
        far = sb("far", [1, 1], I32)
        sT = sb("sT", [TP, 4, TC])

        Y = dram("ybuf", [2 * N, D])
        xnd = dram("xnd", [N, D])

        d_in = Dma(sem("d_in"))
        d_x = Dma(sem("d_x"))
        d_e = Dma(sem("d_e"))
        d_v = Dma(sem("d_v"))
        d_b2 = Dma(sem("d_b2"))
        d_xn = Dma(sem("d_xn"))
        d_y = [Dma(sem(f"d_y{i}")) for i in range(6)]
        d_g = [Dma(sem(f"d_g{i}")) for i in range(9)]
        d_c = [Dma(sem(f"d_c{i}")) for i in range(TC)]
        d_s = Dma(sem("d_s"))
        d_out = Dma(sem("d_out"))
        d_r = [Dma(sem(f"d_r{i}")) for i in range(NSLOT)]

        loads = []

        def plan(src, parts, words):
            loads.append((src, parts, words))
            return len(loads) - 1

        landed = {}

        def load(n, *tokens):
            if n >= len(loads):
                return
            src, parts, words = loads[n]
            s = n % NSLOT
            dst = ring[0:parts, s * SLOTW:s * SLOTW + words]
            landed[n] = sp.dma(d_r[s], lambda e: e.dma_start(dst, src), *tokens)

        def slot(n):
            _, parts, words = loads[n]
            s = n % NSLOT
            return ring[0:parts, s * SLOTW:s * SLOTW + words]

        held = []

        def release(n, token):
            load(n + NSLOT, token)

        def hold(n, token):
            held.append((n + NSLOT, token))

        def unhold(*tokens):
            for n, token in held:
                load(n, token, *tokens)
            held.clear()

        w_l0g = plan(I["L0_gnn_W"], P, 2048)
        w_sh1 = plan(I["sh_w1"], P, 3072)
        w_sh2 = plan(I["sh_w2"], P, 1536)
        w_l0 = []
        for e in range(0, 16, 2):
            a = plan(I["L0_w1"][e], P, 3072)
            c = plan(I["L0_w2"][e // 2], P, 3072)
            b = plan(I["L0_w1"][e + 1], P, 3072)
            w_l0 += [(a, c), (b, c)]
        w_l1g = plan(I["L1_gnn_W"], P, 4096)
        w_ea = [plan(I["ea0"], TP, 42 * 96), plan(I["ea1"], TP, 43 * 96)]
        w_l1 = [[plan(I["L1_w1"][e, 0], P, 4096), plan(I["L1_w1"][e, 1], P, 4096),
                 plan(I["L1_w2"][e], P, 4096)] for e in range(8)]
        w_l2g = [plan(I["L2_gnn_W1a"], P, 4096), plan(I["L2_gnn_W1b"], 96, 1024),
                 plan(I["L2_gnn_W2"][0], P, 4096), plan(I["L2_gnn_W2"][1], P, 4096),
                 plan(I["L2_gnn_W3"], P, 4096)]
        w_l2 = [[plan(I["L2_w1"][e, 0], P, 4096), plan(I["L2_w1"][e, 1], P, 4096),
                 plan(I["L2_w2"][e, 0], P, 4096), plan(I["L2_w2"][e, 1], P, 4096)] for e in range(8)]
        w_l3 = [[plan(I["L3_w1"][e], P, 4096), plan(I["L3_w2"][e], P, 4096)] for e in range(8)]

        x_in = I["x"].rearrange("(c p) d -> p c d", p=TP)
        out_v = out.rearrange("(c p) d -> p c d", p=TP)
        xnd_v = xnd.rearrange("(c p) d -> p c d", p=TP)
        for i, nm in enumerate(("src", "dst")):
            t_e = sp.dma(d_e, lambda e, i=i, nm=nm: e.dma_start(esrc[:, i, :], I[nm + "_c"]))
        for a, b in ((0, 120), (120, 125)):
            t_x = sp.dma(d_x, lambda e, a=a, b=b: e.dma_start(x[a:b], x_in[a:b]))
        load(0)
        t_yt0 = pool.do(lambda e: e.memset(W[:, 12469:15541], 0.0))
        vec = lambda i: W[0:TP, WORK - 1536 + 512 * i:WORK - 1024 + 512 * i]

        def load_vecs(names, *tokens):
            for i, nm in enumerate(names):
                v = I[nm].to_broadcast([TP, D])
                t = act.dma(d_v, lambda e, i=i, v=v: e.dma_start(vec(i), v), *tokens)
            return t

        for i, (nm, E) in enumerate((("L0", 16), ("L1", 8), ("L2", 8), ("L3", 8))):
            t_in = act.dma(d_in, lambda e, i=i, nm=nm, E=E: e.dma_start(gate[:, i, :, 0:E], I[nm + "_gate"]))
            t_in = act.dma(d_in, lambda e, i=i, nm=nm, E=E: e.dma_start(
                gbias[:, i, 0:E], I[nm + "_gb"].to_broadcast([P, E])))
            t_in = act.dma(d_in, lambda e, i=i, nm=nm: e.dma_start(b1[i][:, :], I[nm + "_b1"]))
        t_in = act.dma(d_in, lambda e: e.dma_start(gb1[:, :], I["L2_gnn_b"]))
        t_in = act.dma(d_in, lambda e: e.dma_start(b2s[:, :], I["sh_b2"]))
        t_in = act.dma(d_in, lambda e: e.dma_start(actp[:, :, :].rearrange("p a b -> p (a b)"),
                                                   I["act"].to_broadcast([P, 85])))
        t_vec = load_vecs(("L0_gnn_b", "L0_a_src", "L0_a_dst"), t_yt0)
        for n in range(1, NSLOT):
            load(n)

        t = pool.do(lambda e: e.memset(ident[:, :], 0.0))
        t_id = pool.do(lambda e: e.affine_select(out=ident[:, :], in_=ident[:, :], compare_op=ALU.not_equal,
                                                 fill=1.0, base=0, pattern=[[-1, P]], channel_multiplier=1), t)
        t_io = pool.do(lambda e: e.iota(iota[:, :], [[1, 632]], base=0, channel_multiplier=0,
                                        allow_small_or_imprecise_dtypes=True))
        t_ones = dve.do(lambda e: e.memset(onesf[:, :], 1.0))
        t_onesb = dve.do(lambda e: e.memset(onesb[:, :], 1.0))
        t_eps = dve.do(lambda e: e.memset(eps[:, :], 1e-5))
        pool.do(lambda e: e.iota(iotaE[:, :], [[1, 16]], base=0, channel_multiplier=0,
                                 allow_small_or_imprecise_dtypes=True))
        pool.do(lambda e: e.iota(tok[:, :], [[TP, TC]], base=0, channel_multiplier=1))
        t_tokf = pool.do(lambda e: e.iota(tokf[:, :], [[TP, TC]], base=0, channel_multiplier=1,
                                          allow_small_or_imprecise_dtypes=True))
        t = pool.do(lambda e: e.affine_select(out=upper[:, :], in_=onesb[:, :], compare_op=ALU.is_gt, fill=0.0,
                                              base=0, pattern=[[1, P]], channel_multiplier=-1), t_onesb)
        for j in range(1):
            pool.do(lambda e, j=j: e.tensor_scalar(tok1[:, j, :], tokf[:, :], 1.0, 1.0 + N * j, ALU.mult, ALU.add), t_tokf)
        t_edge = pool.do(lambda e: e.iota(edge[:, :], [[TP, EC]], base=0, channel_multiplier=1,
                                          allow_small_or_imprecise_dtypes=True))
        t_pc = pool.do(lambda e: e.memset(W[:, 3125:7733], 0.0))

        qf, low, high, d_, mid, val, g_, u_ = (seg[:, i, :] for i in range(8))
        mi = segi[:, 0, :]
        vi = segi[:, 1, :]
        src_g = I["src"].rearrange("(n o) -> n o", o=1)
        dst_g = I["dst"].rearrange("(n o) -> n o", o=1)

        def gather5(dst_t, src_ap, idx_t, *tokens):
            for c in range(TC):
                t = pool.dma(d_s, lambda e, c=c: e.indirect_dma_start(
                    out=dst_t[:, c:c + 1], out_offset=None, in_=src_ap,
                    in_offset=bass.IndirectOffsetOnAxis(ap=idx_t[:, c:c + 1], axis=0)), *tokens)
            return t

        def search_steps(levels, t=None):
            if t is None:
                pool.do(lambda e: e.memset(low, 0.0))
                t = pool.do(lambda e: e.memset(high, float(NE)))
            for _ in range(levels):
                t = pool.do(lambda e: e.tensor_tensor(d_, high, low, ALU.subtract), t)
                t = pool.do(lambda e: e.tensor_scalar(d_, d_, 0.5, -0.25, ALU.mult, ALU.add), t)
                t = pool.do(lambda e: e.tensor_scalar(d_, d_, 8388608.0, -8388608.0, ALU.add, ALU.add), t)
                t = pool.do(lambda e: e.tensor_tensor(mid, low, d_, ALU.add), t)
                t = pool.do(lambda e: e.tensor_copy(mi, mid), t)
                t = gather5(vi, src_g, mi, t)
                t = pool.do(lambda e: e.tensor_copy(val, vi), t)
                t = pool.do(lambda e: e.tensor_tensor(val, tokf[:, :], val, ALU.subtract), t)
                t = pool.do(lambda e: e.tensor_scalar(g_, val, 0.0, None, ALU.is_lt), t)
                pool.do(lambda e: e.tensor_tensor(u_, low, mid, ALU.subtract), t)
                t = pool.do(lambda e: e.tensor_tensor(d_, mid, high, ALU.subtract), t)
                pool.do(lambda e: e.tensor_tensor(u_, u_, g_, ALU.mult), t)
                t = pool.do(lambda e: e.tensor_tensor(d_, d_, g_, ALU.mult), t)
                pool.do(lambda e: e.tensor_tensor(low, mid, u_, ALU.add), t)
                t = pool.do(lambda e: e.tensor_tensor(high, high, d_, ALU.add), t)
            return t

        sg, gg, cs = seg[:, 8, :], seg[:, 9, :], seg[:, 10, :]

        def search_end(t):
            t = pool.do(lambda e: e.tensor_scalar(sg, high, 1.0, -1.0, ALU.mult, ALU.add), t)
            t = pool.do(lambda e: e.tensor_scalar(g_, sg, 0.0, None, ALU.is_lt), t)
            t = pool.do(lambda e: e.tensor_scalar(g_, g_, float(NE), 0.0, ALU.mult, ALU.add), t)
            t = pool.do(lambda e: e.tensor_tensor(gg, sg, g_, ALU.add), t)
            t = pool.do(lambda e: e.tensor_copy(mi, gg), t)
            gather5(segi[:, 2, :], src_g, mi, t)
            t = gather5(segi[:, 3, :], dst_g, mi, t)
            t = pool.do(lambda e: e.tensor_copy(cs, segi[:, 3, :]), t)
            t = pool.do(lambda e: e.tensor_copy(seg[:, 11, :], segi[:, 2, :]), t)
            t = pool.do(lambda e: e.tensor_tensor(cs, cs, seg[:, 11, :], ALU.subtract), t)
            return pool.do(lambda e: e.tensor_scalar(cs, cs, 1.0, 1.0, ALU.mult, ALU.add), t)


        t_search = search_steps(11)

        def t_pe():
            return (pe.sem, pe.n)

        xt = [t_x] * TC
        xn_free = []
        xnT_free = []
        tT = [None] * TC

        warm = sb("warm", [1, 1])

        def table(func):
            act.do(lambda e: e.activation(warm[:, :], eps[0:1, :], func), t_eps, sig=False)

        def ln_stats(c):
            t = dve.do(lambda e: e.bn_stats(stats[:, c, :], x[:, c, :]), xt[c])
            t = dve.do(lambda e: e.bn_aggr(mv[:, c, :], stats[:, c, :]), t)
            return act.do(lambda e: e.activation(rstd[:, c:c + 1], mv[:, c, 1:2], ACT.Sqrt, bias=eps[0:TP, :]), t, t_eps, xn_free)

        def ln_apply(c, t, dst):
            t = dve.do(lambda e: e.reciprocal(rstd[:, c:c + 1], rstd[:, c:c + 1]), t)
            t = dve.do(lambda e: e.scalar_tensor_tensor(
                nmr[:, c:c + 1], mv[:, c, 0:1], -1.0, rstd[:, c:c + 1], ALU.mult, ALU.mult), t)
            return act.do(lambda e: e.activation(
                dst[:, c, :], x[:, c, :], ACT.Identity, bias=nmr[:, c:c + 1], scale=rstd[:, c:c + 1]), t, xn_free)

        def ln_tiles(produce, dst, after=None, banks=None, lag=1):
            ts, p = [], {}
            keep_lag = max(2, lag)

            def turn(c):
                b = banks[c]
                for d in range(DC):
                    t = pe.do(lambda e, d=d: e.transpose(
                        bank[b][:, d * TP:(d + 1) * TP], dst[:, c, d * P:(d + 1) * P], ident[0:TP, 0:TP]),
                        ts[c], t_id, free[b], sig=d == DC - 1)
                p[c] = t

            def keep(c):
                b = banks[c]
                src = bank[b][:, 0:DC * TP].rearrange("p (d t) -> p d t", d=DC)
                tT[c] = free[b] = act.do(lambda e: e.activation(xnT[:, :, c * TP:(c + 1) * TP], src, ACT.Copy), p[c], xnT_free)

            for c in range(TC + lag + 2):
                if c < TC:
                    produce(c)
                    t = ln_stats(c)
                if 1 <= c <= TC:
                    ts.append(ln_apply(c - 1, t1, dst))
                t1 = t
                if banks and 0 <= c - lag < TC:
                    turn(c - lag)
                if banks and 0 <= c - keep_lag < TC:
                    keep(c - keep_lag)
                if after and 0 <= c - lag - 2:
                    after(c - lag - 2)
            xn_free.clear()
            if banks:
                xnT_free.clear()
                xn_free.append(t_pe())
            return ts

        def rows_out(psum, c, t):
            return dve.do(lambda e: e.tensor_tensor(x[:, c, :], x[:, c, :], psum, ALU.add), t, xt[c])

        GT = [W[:, 3125 + 512 * i:3637 + 512 * i] for i in range(9)]
        XG = [W[:, 7733 + 512 * i:8245 + 512 * i] for i in range(3)]
        HT = W[:, 9269:11317]
        TMP = W[:, 11317:12469]
        XGW = W[:, 0:1280].rearrange("p (d n) -> p d n", d=DC)
        YTT = W[:, 1280:2560].rearrange("p (d n) -> p d n", d=DC)
        XG2 = W[:, 2560:3072].rearrange("p (d n) -> p d n", d=DC)
        HW = W[:, 7221:12341].rearrange("p (h n) -> p h n", h=16)
        SW = [HW[:, 8 + 2 * i:10 + 2 * i, :] for i in range(2)]
        YT = [W[:, 12469 + 512 * i:12981 + 512 * i] for i in range(6)]
        CMB = W[0:TP, 3125:3125 + 5120].rearrange("p (c j d) -> p c j d", c=TC, j=2)
        S1 = HT[0:TP, 0:640].bitcast(F16).rearrange("p (i s) -> p i s", i=2 * TC)
        R1 = HT[0:TP, 640:1440].bitcast(F16).rearrange("p (i s) -> p i s", i=2 * TC)
        Yv = Y.rearrange("(j c p) d -> p c j d", j=2, p=TP)
        mem = {"gt": [None] * 9, "yt": [None] * 6, "work": None, "b2": None, "xg": [None] * 3}

        def logits(L, E):
            def after(c):
                for d in range(DC):
                    pe.do(lambda e, d=d: e.matmul(
                        bank[5][0:TP, c * E:(c + 1) * E], xnT[:, d, c * TP:(c + 1) * TP], gate[:, L, d, 0:E],
                        start=d == 0, stop=d == DC - 1), tT[c], t_in, free[5], sig=d == DC - 1)
            return after

        def moe(L, E, b2_src, expert, between, extra_bias, ts, onward, group=1):
            K = E * NCH
            t_b2 = act.dma(d_b2, lambda e: e.dma_start(b2[0:E, :], b2_src), mem["b2"])
            t_xnd = None
            for a, b in ((0, 120), (120, 125)):
                t_xnd = sp.dma(d_xn, lambda e, a=a, b=b: e.dma_start(xnd_v[a:b], xn[a:b]), ts)
            xn_free.append(t_xnd)
            table(ACT.Sigmoid)
            lgp, t = bank[5][0:TP, 0:TC * E], t_pe()
            lgv = lg[:, :, 0:E]
            t = dve.do(lambda e: e.tensor_tensor(
                lgv, lgp.rearrange("p (c e) -> p c e", e=E),
                gbias[0:TP, L:L + 1, 0:E].to_broadcast([TP, TC, E]), ALU.add), t, t_in)
            free[5] = t
            for c in range(TC):
                t2 = dve.do(lambda e, c=c: e.max(mx[:, c, :], lg[:, c, 0:E]), t)
            for c in range(TC):
                t2 = dve.do(lambda e, c=c: e.max_index(ix[:, c, :], mx[:, c, :], lg[:, c, 0:E]), t2)
            t = dve.do(lambda e: e.tensor_copy(ixf[:, :, :], ix[:, :, 0:2].rearrange("p c k -> p k c")), t2)
            ixv = ixf[:, :, :].rearrange("p k c -> p (k c)")
            sv, tv = s12[:, :, 0:E], t12[:, :, 0:E]
            t_s = dve.do(lambda e: e.tensor_tensor(
                sv, iotaE[0:TP, 0:E].rearrange("p (o e) -> p o e", o=1).to_broadcast([TP, 2 * TC, E]),
                ixv.rearrange("p (k o) -> p k o", o=1).to_broadcast([TP, 2 * TC, E]), ALU.is_equal), t, t_pc)
            sel_v = sel[:, 0:TC * E].rearrange("p (c e) -> p c e", e=E)
            t = dve.do(lambda e: e.tensor_tensor(sel_v, s12[:, 0:TC, 0:E], s12[:, TC:2 * TC, 0:E], ALU.add), t_s)
            rkp = bank[6][0:TP, 0:TC * E]
            pe.do(lambda e: e.matmul(rkp, upper[0:TP, 0:TP], sel[:, 0:TC * E], start=True, stop=True,
                                     skip_group_check=True), t, free[6], t_pc, sig=False)
            for s in range(1, TC):
                tr = pe.do(lambda e, s=s: e.matmul(rkp[:, s * E:], onesb[0:TP, 0:TP], sel[:, 0:(TC - s) * E],
                                                   start=False, stop=True, skip_group_check=True),
                           t_onesb, sig=s == TC - 1)
            ctp = bank[7][0:TP, 0:E]
            for c in range(TC):
                tc = pe.do(lambda e, c=c: e.matmul(ctp, onesb[0:TP, 0:TP], sel[:, c * E:(c + 1) * E],
                                                   start=c == 0, stop=c == TC - 1), free[7], sig=c == TC - 1)
            t = dve.do(lambda e: e.tensor_tensor(
                t12[:, 0:TC, 0:E], s12[:, 0:TC, 0:E], rkp.rearrange("p (c e) -> p c e", e=E), ALU.mult), tr)
            t = dve.do(lambda e: e.tensor_tensor(
                t12[:, TC:2 * TC, 0:E], s12[:, TC:2 * TC, 0:E],
                rkp.rearrange("p (c e) -> p c e", e=E), ALU.mult))
            free[6] = t
            rv = rk[:, :, :].rearrange("p k c -> p (k c)")
            t = dve.do(lambda e: e.tensor_reduce(rv, tv, AX.X, ALU.add), t)
            k0, k1, k2, k3 = (kk[:, i, :] for i in range(4))
            t = dve.do(lambda e: e.tensor_scalar(k0, rv, float(CH), None, ALU.is_ge), t)
            for j in range(2, NCH):
                a, b = (k0, k1) if j % 2 == 0 else (k1, k0)
                t = dve.do(lambda e, a=a, b=b, j=j: e.scalar_tensor_tensor(
                    b, rv, float(CH * j), a, ALU.is_ge, ALU.add), t)
            kf = k1 if (NCH - 2) % 2 == 1 else k0
            dve.do(lambda e: e.scalar_tensor_tensor(k2, ixv, float(NCH), kf, ALU.mult, ALU.add), t)
            t = dve.do(lambda e: e.scalar_tensor_tensor(k3, kf, -float(CH), rv, ALU.mult, ALU.add), t)
            idp = bank[5][:, 0:2 * K]
            for n, i in enumerate([*range(TC, 2 * TC), *range(TC)]):
                j, c = divmod(i, TC)
                t1 = (pool if n >= 2 * TC - 3 else dve).do(lambda e, i=i: e.tensor_scalar(
                    S1[:, i, :], iota[0:TP, 0:P], k3[:, i:i + 1], None, ALU.is_equal),
                    t, t_io, mem["work"], mem.get("hp"))
                t2 = dve.do(lambda e, i=i, c=c: e.tensor_scalar(
                    R1[:, i, 0:K], iota[0:TP, 0:K], k2[:, i:i + 1], tok1[:, 0, c:c + 1], ALU.is_equal, ALU.mult),
                    t, t_io, mem["work"], mem.get("hp"))
                if j:
                    t2 = dve.do(lambda e, i=i: e.tensor_scalar(
                        R1[:, i, K:2 * K], iota[0:TP, 0:K], k2[:, i:i + 1], float(N), ALU.is_equal, ALU.mult))
                ti = pe.do(lambda e, i=i, j=j, n=n: e.matmul(
                    idp[:, 0:K * (1 + j)], S1[:, i, :], R1[:, i, 0:K * (1 + j)], start=n == 0, stop=True,
                    skip_group_check=True), t1, t2, free[5], sig=n == 2 * TC - 1)
            t = dve.do(lambda e: e.tensor_scalar(idz[:, 0:K], idp[:, 0:K], 0.0, float(FAR), ALU.is_equal, ALU.mult), ti)
            t = dve.do(lambda e: e.scalar_tensor_tensor(
                idz[:, 0:K], idp[:, 0:K], -1.0, idz[:, 0:K], ALU.add, ALU.add), t)
            t_idx = dve.do(lambda e: e.tensor_copy(idx[:, 0:K], idz[:, 0:K]), t, mem.get("y"))
            t_idy = dve.do(lambda e: e.tensor_tensor(idx[:, K:2 * K], idz[:, 0:K], idp[:, K:2 * K], ALU.add), t)
            free[5] = t_idy
            t_cnt = dve.do(lambda e: e.tensor_copy(cnt[0:1, 0:E], ctp[0:1, :]), tc)
            free[7] = t_cnt

            def place(e_, k):
                if group > 1:
                    b = e_ % 4 if k == 0 else 4 + e_ % 2 if k == 1 else 4 + k
                    return b, b
                b = 2 * k + e_ % 2 if k < 3 else 3 + k
                return b, b

            def gather(e_, k):
                b, i = place(e_, k)
                v = e_ * NCH + k
                t = pool.dma(d_g[i], lambda e: e.indirect_dma_start(
                    out=GT[b], out_offset=None, in_=xnd,
                    in_offset=bass.IndirectOffsetOnAxis(ap=idx[:, v:v + 1], axis=0),
                    bounds_check=N - 1, oob_is_err=False), t_idx, t_xnd, mem["gt"][b], (d_g[i].sem, d_g[i].n), mem["work"])
                return b, t

            def scatter(e_, k, t):
                y = e_ % 2 if k == 0 else 1 + k
                v = K + e_ * NCH + k
                s = d_y[e_ % 2 if k == 0 else k + 1]
                t = pool.dma(s, lambda e: e.indirect_dma_start(
                    out=Y, out_offset=bass.IndirectOffsetOnAxis(ap=idx[:, v:v + 1], axis=0),
                    in_=YT[y], in_offset=None, bounds_check=2 * N - 1, oob_is_err=False), t, t_idy)
                mem["yt"][y] = t

            def gathers(e_, ks):
                d_of = lambda k: d_g[place(e_, k)[1]]
                for i, k in enumerate(ks):
                    if k:
                        pool.begin((L, e_), k, [d_of(j) for j in ks[i:]])
                    got[e_, k] = gather(e_, k)
                for k in ks:
                    if k:
                        pool.end()

            def scatters(e_):
                for k in range(1, NCH):
                    pool.begin((L, e_), k, d_y[k + 1:])
                    scatter(e_, k, t_o[e_, k])
                for k in range(1, NCH):
                    pool.end()

            got, t_o = {}, {}
            pool.wait(t_cnt)
            for e_ in range(E):
                pool.ops.append(("count", (L, e_), cnt[0:1, e_:e_ + 1]))
            gathers(0, [0])
            unhold(got[0, 0][1])
            if group > 1:
                for e_ in (1, 2, 3):
                    gathers(e_, [0])
                gathers(0, [1])
                gathers(0, [2, 3, 4])
                gathers(1, [1])
            else:
                gathers(0, [1, 2])
                gathers(1, [0])
                gathers(1, [1, 2])
                gathers(0, [3, 4])
            tw = dve.do(lambda e: e.tensor_tensor(dw[:, :], mx[:, :, 0], mx[:, :, 1], ALU.subtract))
            act.do(lambda e: e.activation(wt[:, 0, :], dw[:, :], ACT.Sigmoid), tw)
            tw = act.do(lambda e: e.activation(wt[:, 1, :], dw[:, :], ACT.Sigmoid, scale=-1.0))
            t = dve.do(lambda e: e.tensor_tensor(
                tv, sv, wt[:, :, :].rearrange("p k (c o) -> p (k c) o", o=1).to_broadcast([TP, 2 * TC, E]), ALU.mult), tw)
            t = dve.do(lambda e: e.tensor_tensor(cw[:, :, 0:E], t12[:, 0:TC, 0:E], t12[:, TC:2 * TC, 0:E], ALU.add), t)
            for c in range(TC):
                b, o = (6, c * TP) if c < 4 else (7, 0)
                tt = pe.do(lambda e, c=c, b=b, o=o: e.transpose(
                    bank[b][0:E, o:o + TP], cw[:, c, 0:E], ident[0:TP, 0:TP]), t, free[b])
                if c == 3:
                    t6 = act.do(lambda e: e.activation(cwT[0:E, 0:4 * TP], bank[6][0:E, 0:4 * TP], ACT.Copy), tt)
            t7 = act.do(lambda e: e.activation(cwT[0:E, 4 * TP:N], bank[7][0:E, 0:TP], ACT.Copy), tt)
            free[6], free[7] = t6, t7
            if L in (1, 2):
                table(ACT.Silu)
            between()
            for c in range(TC):
                last = not extra_bias
                t = pe.do(lambda e, c=c, last=last: e.matmul(
                    bank[c][0:TP, :], cwT[0:E, c * TP:(c + 1) * TP], b2[0:E, :], start=True, stop=last),
                    free[c], t7, t_b2, sig=last)
                if extra_bias:
                    t = extra_bias(c)
                xt[c] = free[c] = rows_out(bank[c][0:TP, :], c, t)
            mem["b2"] = t_pe()
            xnT_free.append(t_pe())

            def bring(e_, k):
                b, t_g = got[e_, k]
                x_ = e_ % 2 if k == 0 else 2
                tb = 7 if k == 0 and e_ % 2 else 0
                for d in range(DC):
                    t = pe.do(lambda e, d=d: e.transpose(
                        bank[tb][:, d * P:(d + 1) * P], GT[b][:, d * P:(d + 1) * P], ident[:, :]),
                        t_g, free[tb], sig=d == DC - 1)
                mem["gt"][b] = t
                free[tb] = dve.do(lambda e: e.tensor_copy(XG[x_], bank[tb][:, :]), t, mem["xg"][x_], mem["work"])
                return XG[x_], free[tb]

            def leave(e_, k, yb, t, n=CH):
                y = e_ % 2 if k == 0 else 1 + k
                t = act.do(lambda e: e.activation(YT[y][0:n], bank[yb][0:n, :], ACT.Copy), t, mem["yt"][y], mem["work"])
                free[yb] = t
                return t

            def bring_wide(e_, k):
                b, t_g = got[e_, k]
                tb, n = 7 * (k % 2), min(CH, WIDE - CH * k)
                for d in range(DC):
                    t = pe.do(lambda e, d=d: e.transpose(
                        bank[tb][:, d * P:(d + 1) * P], GT[b][:, d * P:(d + 1) * P], ident[:, :]),
                        t_g, free[tb], sig=d == DC - 1)
                mem["gt"][b] = t
                free[tb] = dve.do(lambda e: e.tensor_copy(
                    XGW[:, :, CH * k:CH * k + n], bank[tb][:, :].rearrange("p (d n) -> p d n", d=DC)[:, :, 0:n]),
                    t, mem["xg"][0], mem["work"])
                return free[tb]

            def bring2(e_, k):
                b, t_g = got[e_, k]
                for d in range(DC):
                    t = pe.do(lambda e, d=d: e.transpose(
                        bank[0][:, d * P:(d + 1) * P], GT[b][:, d * P:(d + 1) * P], ident[:, :]),
                        t_g, free[0], sig=d == DC - 1)
                mem["gt"][b] = t
                free[0] = dve.do(lambda e: e.tensor_copy(
                    XG2, bank[0][:, :].rearrange("p (d n) -> p d n", d=DC)), t, mem["xg"][2], mem["work"])
                return free[0]

            def rows(e_, k, t_y):
                n, b = min(CH, WIDE - CH * k), (1, 2, 6)[k]
                for d in range(DC):
                    t = pe.do(lambda e, d=d: e.transpose(
                        bank[b][0:n, d * P:(d + 1) * P], YTT[:, d, CH * k:CH * k + n], ident[:, :]),
                        t_y, free[b], sig=d == DC - 1)
                return leave(e_, k, b, t, n)

            def whole(e_, n, t_x, more, mark):
                ks = range(1, -(-n // CH))
                t_x = [t_x] + [bring_wide(e_, k) for k in ks]
                tg = expert[0](e_, n, XGW, t_x)
                mem["xg"] = [t_pe()] + mem["xg"][1:]
                t_y = expert[2](e_, n, tg)
                mem["hp"] = t_pe()
                mark(act)
                if more:
                    for k in range(2, NCH):
                        if k > 2:
                            for en in (pe, act, dve):
                                en.begin((L, e_), k)
                        t = bring2(e_, k)
                        tk = expert[0](e_, CH, XG2, t)
                        mem["xg"] = mem["xg"][:2] + [t_pe()]
                        leave(e_, k, 1 + k % 2, expert[1](e_, 0, 1 + k % 2, tk))
                    for k in range(3, NCH):
                        for en in (pe, act, dve):
                            en.end()
                if e_ + 1 < E:
                    bring_wide(e_ + 1, 0)
                for k in [0, *ks]:
                    rows(e_, k, t_y)
                for en in (pe, act, dve):
                    mark(en)

            def step(e_, t_x):
                engs = (pe, act, dve)
                start = [(en.n, en.seen, en.ops) for en in engs]
                free0, mem0, most = list(free), dict(mem), {}
                for final in (False, True):
                    made = []
                    for n in WIDTHS + (2 * CH,):
                        for en, (v, seen, _) in zip(engs, start):
                            en.n, en.seen, en.ops = v, dict(seen), []
                        free[:] = free0
                        mem.clear()
                        mem.update(mem0)
                        mem["gt"] = list(mem0["gt"])
                        passed, last = [], {en.sem.name: en.n for en in engs}

                        def mark(en):
                            i, at_ = len(passed), last[en.sem.name]
                            passed.append(i)
                            if final:
                                en.lift(at_ + most[i])
                            else:
                                most[i] = max(most.get(i, 0), en.n - at_)
                            last[en.sem.name] = en.n
                            reached[i] = en.n

                        reached = {}
                        whole(e_, n, t_x, len(made) == len(WIDTHS), mark)
                        made.append([en.ops for en in engs])
                for i, (en, (_, seen, ops)) in enumerate(zip(engs, start)):
                    ops.append(("widths", (L, e_), [m[i] for m in made]))
                    en.seen, en.ops = seen, ops
                t_a, t_d = (act.sem, act.n), (dve.sem, dve.n)
                mem.clear()
                mem.update(mem0)
                mem["xg"], mem["hp"], mem["ytt"] = [t_pe()] * 3, t_pe(), t_pe()
                mem["gt"] = [t_pe()] * 9
                mem["s", 0] = mem["s", 1] = t_d
                free[:] = [t_d, t_a, t_a, *[[(act.sem, reached[0]), t_d]] * 3, [t_a, t_d], t_d]
                for k in range(NCH):
                    t_o[e_, k] = t_a
                done(e_, hold if e_ >= E - 1 else release)
                scatter(e_, 0, t_a)
                scatters(e_)
                if e_ + 3 < E:
                    gathers(e_ + 3, [0])
                if e_ + 2 < E:
                    gathers(e_ + 2, [1, 2])
                if e_ + 1 < E:
                    gathers(e_ + 1, [3, 4])
                return t_d

            if group == 1:
                for en in (pe, act, dve):
                    en.wait(t_cnt)
                    for e_ in range(E):
                        en.ops.append(("count", (L, e_), cnt[0:1, e_:e_ + 1]))
                if L == 1:
                    mem["ytt"] = pool.do(lambda e: e.memset(W[:, 1280:2560], 0.0), mem["work"])
                t_x = bring_wide(0, 0)
                gathers(2, [0])
                for e_ in range(E):
                    t_x = step(e_, t_x)
            else:
                ready = {e_: bring(e_, 0) for e_ in range(group)}
                for e0 in range(0, E, group):
                    es = range(e0, e0 + group)
                    second = []
                    for e_ in es:
                        if e_ + 4 < E:
                            gathers(e_ + 4, [0])
                    for e_ in es:
                        second.append(expert(e_, 1 + e_ % 2, *ready[e_]))
                        mem["xg"][e_ % 2] = t_pe()
                    for e_ in range(e0 + group, min(E, e0 + 2 * group)):
                        ready[e_] = bring(e_, 0)
                    for e_, m2 in zip(es, second):
                        t_o[e_, 0] = leave(e_, 0, 1 + e_ % 2, m2())
                        scatter(e_, 0, t_o[e_, 0])
                    for e_ in es:
                        for en in (pe, act, dve):
                            en.wait(t_cnt)
                            en.ops.append(("count", (L, e_), cnt[0:1, e_:e_ + 1]))
                        for k in range(1, NCH):
                            for en in (pe, act, dve):
                                en.begin((L, e_), k)
                            xg, t = bring(e_, k)
                            yb = 1 + (e_ + k) % 2
                            m2 = expert(e_, yb, xg, t)
                            mem["xg"][2] = t_pe()
                            t_o[e_, k] = leave(e_, k, yb, m2())
                        for en in (pe, act, dve):
                            for k in range(1, NCH):
                                en.end()
                        scatters(e_)
                        if e_ + 2 < E:
                            gathers(e_ + 2, [1])
                        if e_ + 1 < E:
                            gathers(e_ + 1, [2, 3, 4])
                        done(e_, hold if e_ >= E - group else release)
            table(ACT.Sqrt)
            t_y = [(d.sem, d.n) for d in d_y]
            mem["y"] = t_y
            t_last = [t_pe()] + [(d.sem, d.n) for d in d_g]
            t_c = []
            for c in range(TC):
                for a, b in ((0, 120), (120, 125)):
                    t = act.dma(d_c[c], lambda e, a=a, b=b, c=c: e.dma_start(CMB[a:b, c], Yv[a:b, c]), t_y, t_last)
                t_c.append(t)

            def produce(c):
                for j in range(2):
                    xt[c] = dve.do(lambda e, c=c, j=j: e.scalar_tensor_tensor(
                        x[:, c, :], CMB[:, c, j, :], wt[:, j, c:c + 1], x[:, c, :], ALU.mult, ALU.add), t_c[c], xt[c], tw)

            ts = onward(produce)
            unhold(t_c[-1])
            mem["work"] = xt[TC - 1]
            mem["gt"] = [xt[TC - 1]] * 9
            return ts

        def done(e_, rel):
            pass

        A = W[0:TP, 0:3125]
        AT = W[0:TP, 3125:6250].rearrange("p (c i) -> p c i", c=TC)
        tef = dve.do(lambda e: e.tensor_copy(ef[:, :, :], esrc[:, :, :]), t_e)
        OH = W[0:TP, 9948:9948 + 8 * 313].bitcast(BF)

        emb = W[0:TP, 6250:6250 + 2560].rearrange("p (c d) -> p c d", c=TC)
        scr = W[0:TP, 8810:8810 + 512]
        dgl = [W[0:TP, 9322 + TP * c:9322 + TP * (c + 1)] for c in range(TC)]
        xnf = xn[:, :, :].rearrange("p c d -> p (c d)")
        Sb = xnf[:, 0:N]
        ub = [xnf[:, N * (1 + i):N * (2 + i)] for i in range(3)]
        wg0 = slot(w_l0g).rearrange("p (k d) -> p k d", k=DC)
        at = {"r": None, "s": [], "temb": [], "u": {}, "tu": [None] * 3}

        def start_emb(c, b):
            for d in range(DC):
                t = pe.do(lambda e, d=d: e.matmul(
                    bank[b][0:TP, :], xnT[:, d, c * TP:(c + 1) * TP], wg0[:, d, :], start=d == 0, stop=d == DC - 1),
                    tT[c], landed[w_l0g], free[b], sig=d == DC - 1)
            at["emb", c] = t

        def start_sums(c, b):
            t = at["emb", c]
            t = free[b] = dve.do(lambda e: e.tensor_tensor(emb[:, c, :], bank[b][0:TP, :], vec(0), ALU.add), t, t_vec, t_pc)
            at["temb"].append(t)
            for i in range(2):
                t = at["r"] = dve.do(lambda e, i=i: e.tensor_tensor_reduce(
                    scr, emb[:, c, :], vec(1 + i), 1.0, 0.0, ALU.mult, ALU.add, sT[:, i, c:c + 1]), t, at["r"])
            if c == TC - 1:
                release(w_l0g, t_pe())
                xnT_free.append(t_pe())
                xn_free.append(t_pe())

        def start_row(cs, b):
            for c in cs:
                t = dve.do(lambda e, c=c: e.tensor_scalar(
                    dgl[c], ident[0:TP, 0:TP], sT[:, 0, c:c + 1], None, ALU.mult), at["r"], t_id)
                t = pe.do(lambda e, c=c: e.matmul(
                    bank[b][0:TP, (c - cs[0]) * TP:(c - cs[0] + 1) * TP], onesf[0:TP, 0:TP], dgl[c], start=True, stop=True),
                    t, free[b], t_ones)
            n = TP * len(cs)
            free[b] = act.do(lambda e: e.activation(Sb[:, cs[0] * TP:cs[0] * TP + n], bank[b][0:TP, 0:n], ACT.Copy), t, xn_free)
            at["s"].append(free[b])

        def start_u(c):
            u = ub[c % 3]
            at["u", c] = act.do(lambda e: e.activation(u, Sb, ACT.Identity, bias=sT[:, 1, c:c + 1]), at["s"], at["tu"][c % 3])

        def start_leaky(c):
            u = ub[c % 3]
            at["u"][c] = dve.do(lambda e: e.scalar_tensor_tensor(u, u, 0.1, u, ALU.mult, ALU.max), at["u", c])

        dev, dev2 = (W[0:TP, 9948 + EC * i:9948 + EC * (i + 1)] for i in range(2))
        bad = nmr[:, 0:1]
        t = dve.do(lambda e: e.scalar_tensor_tensor(dev, ef[:, 1, :], NE / N, edge[:, :], ALU.mult, ALU.subtract), tef, t_edge)
        t = dve.do(lambda e: e.tensor_tensor(dev2, dev, dev, ALU.mult), t)
        t = dve.do(lambda e: e.tensor_scalar(dev, dev2, float((NEAR * NE // N) ** 2), None, ALU.is_gt), t)
        t = dve.do(lambda e: e.tensor_reduce(bad, dev, AX.X, ALU.add), t)
        t = pe.do(lambda e: e.matmul(bank[7][0:1, 0:1], bad, onesf[0:TP, 0:1], start=True, stop=True), t, t_ones)
        t_far = free[7] = dve.do(lambda e: e.tensor_scalar(far[:, :], bank[7][0:1, 0:1], 1.0, None, ALU.min), t)

        def reach(c, width):
            q = NE // N
            lo, hi = max(0, TP * c // q - NEAR), min(N - 1, (TP * c + TP - 1) // q + 1 + NEAR)
            return range(lo // width, hi // width + 1)

        def counts(tiles_of):
            oh_free, seen_banks = [None] * 4, set()
            for c in range(EC):
                b, ms = c % 4, tiles_of(c)
                m0 = ms[0]
                oh = [OH[:, (2 * b + i) * 626:(2 * b + i) * 626 + n] for i, n in enumerate((N, len(ms) * TP))]
                for i, o in enumerate((0, m0 * TP)):
                    t = dve.do(lambda e, i=i, c=c, oh=oh, o=o: e.tensor_scalar(
                        oh[i], iota[0:TP, o:o + oh[i].shape[-1]], ef[:, i, c:c + 1], None, ALU.is_equal), tef, t_io, oh_free[b])
                for m in ms:
                    lhs = oh[1][:, (m - m0) * TP:(m - m0 + 1) * TP]
                    bb, o = (5, 113 * m) if m < 4 else (6, 0)
                    firsts = [k not in seen_banks for k in (m, bb)]
                    seen_banks.update((m, bb))
                    pe.do(lambda e, m=m, lhs=lhs, oh=oh, f=firsts[0]: e.matmul(
                        bank[m][0:TP, :], lhs, oh[0][:, 0:512], start=f, stop=True, skip_group_check=True), t, sig=False)
                    oh_free[b] = pe.do(lambda e, m=m, lhs=lhs, oh=oh, bb=bb, o=o, f=firsts[1]: e.matmul(
                        bank[bb][0:TP, o:o + 113], lhs, oh[0][:, 512:N], start=f, stop=True,
                        skip_group_check=True), sig=m == ms[-1])

        for en in (dve, pe):
            en.wait(t_far)
            en.ops.append(("count", "far", far[0:1, 0:1]))
        either((dve, pe), "far", lambda: counts(lambda c: range(TC)), lambda: counts(lambda c: reach(c, TP)))
        t_A = t_pe()
        t = act.do(lambda e: e.activation(spt[:, :, :], actp[:, :, :], ACT.Abs), t_in)
        t = act.do(lambda e: e.activation(spt[:, :, :], spt[:, :, :], ACT.Exp, scale=-1.0), t)
        at["ln"] = act.do(lambda e: e.activation(spt[:, :, :], spt[:, :, :], ACT.Ln, bias=onesf[:, 0:1]), t, t_ones)
        t_at = dve.do(lambda e: e.tensor_copy(
            AT[:, 0:4, 512:N], bank[5][0:TP, 0:452].rearrange("p (m i) -> p m i", m=4)), t_A, t_pc)
        free[5] = t_at
        for m in range(TC):
            if m % 2 == 0:
                free[m] = act.do(lambda e, m=m: e.activation(AT[:, m, 0:512], bank[m][0:TP, :], ACT.Copy), t_A, t_pc)
            else:
                free[m] = dve.do(lambda e, m=m: e.tensor_copy(AT[:, m, 0:512], bank[m][0:TP, :]), t_A, t_pc)
        free[6] = dve.do(lambda e: e.tensor_copy(AT[:, 4, 512:N], bank[6][0:TP, 0:113]))
        ats = free[0:7]

        t_Adone = []
        for g in range(7):
            b = (1, 2, 3, 4, 5, 6, 7)[g]
            n = min(4, 25 - 4 * g)
            for j in range(n):
                f = 4 * g + j
                a_, b_ = f // 5, f % 5
                t = pe.do(lambda e, b=b, j=j, a_=a_, b_=b_: e.transpose(
                    bank[b][0:TP, j * TP:(j + 1) * TP], AT[:, b_, a_ * TP:(a_ + 1) * TP], ident[0:TP, 0:TP]),
                    ats, free[b], sig=j == n - 1)
            if g % 2:
                free[b] = dve.do(lambda e, g=g, b=b, n=n: e.tensor_copy(
                    A[:, 500 * g:500 * g + n * TP], bank[b][0:TP, 0:n * TP]), t)
            else:
                free[b] = act.do(lambda e, g=g, b=b, n=n: e.activation(
                    A[:, 500 * g:500 * g + n * TP], bank[b][0:TP, 0:n * TP], ACT.Copy), t)
            t_Adone.append(free[b])
        t_Atr = t
        ln_tiles(lambda c: None, xn, None, [7, 0, 1, 2, 3])
        for c in range(TC):
            start_emb(c, (4, 5, 6, 7, 0)[c])
            start_sums(c, (4, 5, 6, 7, 0)[c])
        start_row([0, 1, 2, 3], 1)
        start_row([4], 2)
        for c in range(3):
            start_u(c)
            start_leaky(c)
        temb = at["temb"]
        rsum = bank[7][0:TP, 0:TC]
        for c in range(TC):
            u = ub[c % 3]
            t = dve.do(lambda e, c=c, u=u: e.scalar_tensor_tensor(u, AT[:, c, :], 1e30, u, ALU.mult, ALU.min), at["u"][c], ats)
            t = act.do(lambda e, u=u: e.activation(u, u, ACT.Exp), t)
            t = at["tu"][c % 3] = dve.do(lambda e, c=c, u=u: e.tensor_tensor(AT[:, c, :], AT[:, c, :], u, ALU.mult), t, t_Atr)
            if c + 3 < TC:
                start_u(c + 3)
                start_leaky(c + 3)
            for i in range(TC):
                lhs = AT[:, c, i * TP:(i + 1) * TP]
                pe.do(lambda e, i=i, c=c, lhs=lhs: e.matmul(
                    bank[i][0:TP, :], lhs, emb[:, c, :], start=c == 0, stop=c == TC - 1),
                    t, temb, free[i], sig=False)
                tr_ = pe.do(lambda e, i=i, c=c, lhs=lhs: e.matmul(
                    rsum[:, i:i + 1], lhs, onesf[0:TP, 0:1], start=c == 0 and i == 0, stop=c == TC - 1,
                    skip_group_check=True), free[7], sig=i == TC - 1)
        t = dve.do(lambda e: e.reciprocal(sT[:, 2, :], rsum), tr_)
        free[7] = t
        xn_free.extend(at["tu"])

        def attended(i):
            xt[i] = free[i] = dve.do(lambda e: e.scalar_tensor_tensor(
                x[:, i, :], bank[i][0:TP, :], sT[:, 2, i:i + 1], x[:, i, :], ALU.mult, ALU.add), t, xt[i])

        table(ACT.Sqrt)
        t = dve.do(lambda e: e.scalar_tensor_tensor(spl[:, :, :], actp[:, :, :], 0.0, spt[:, :, :], ALU.max, ALU.add), at["ln"], t_in)
        t_sp = dve.do(lambda e: e.tensor_scalar(ngc[:, :, :], spl[:, :, :], -1.0, None, ALU.mult), t)
        ts = ln_tiles(attended, xn, logits(0, 16), [0, 1, 2, 3, 4])
        mem["work"] = xt[TC - 1]

        def swiglu(ei, G, U, S, H, t_gu, *tokens):
            p = lambda i: actp[:, ei, i:i + 1]
            t = dve.do(lambda e: e.tensor_scalar(G, G, ngc[:, ei, 3:4], spl[:, ei, 3:4], ALU.max, ALU.min), t_gu, t_sp)
            ts_ = act.do(lambda e: e.activation(S, G, ACT.Sigmoid, scale=p(0)), t)
            t1 = dve.do(lambda e: e.tensor_scalar(U, U, ngc[:, ei, 4:5], spl[:, ei, 4:5], ALU.max, ALU.min))
            t1 = dve.do(lambda e: e.scalar_tensor_tensor(U, U, p(2), G, ALU.add, ALU.mult), t1, t)
            return dve.do(lambda e: e.scalar_tensor_tensor(H, U, p(1), S, ALU.mult, ALU.mult), t1, ts_, *tokens)

        shT = HT[:, 0:1875].rearrange("p (f n) -> p f n", f=3)

        def shared():
            w1 = slot(w_sh1).rearrange("p (k f) -> p k f", k=DC)
            th = []
            for h0, n in ((0, 313), (313, 312)):
                base = 11317
                G, U, S = (W[:, base + 939 * i:base + 939 * i + 3 * n] for i in range(3))
                tg = []
                for f in range(6):
                    for d in range(DC):
                        t = pe.do(lambda e, f=f, d=d, h0=h0, n=n: e.matmul(
                            bank[f][:, 0:n], w1[:, d, f * P:(f + 1) * P], xnT[:, d, h0:h0 + n],
                            start=d == 0, stop=d == DC - 1), tT, landed[w_sh1], free[f], sig=d == DC - 1)
                    dst = (G if f < 3 else U)[:, (f % 3) * n:(f % 3 + 1) * n]
                    bias = b1[0][:, 96 + f:97 + f]
                    if f < 3:
                        t = act.do(lambda e, f=f, n=n, dst=dst, bias=bias: e.activation(
                            dst, bank[f][:, 0:n], ACT.Identity, bias=bias), t, t_in, th, mem["work"])
                    else:
                        t = dve.do(lambda e, f=f, n=n, dst=dst, bias=bias: e.tensor_scalar(
                            dst, bank[f][:, 0:n], bias, None, ALU.add), t, t_in, th, mem["work"])
                    free[f] = t
                    tg.append(t)
                Hv = shT[:, :, h0:h0 + n]
                v3 = lambda a: a.rearrange("p (f n) -> p f n", f=3)
                th.append(swiglu(16, v3(G), v3(U), v3(S), Hv, tg))
            release(w_sh1, t_pe())
            mem["sh"] = th
            mem["seg"] = search_end(search_steps(3, t_search))
            mem["yt"] = [list(th) for _ in range(6)]

        def shared_rows(c):
            w2 = slot(w_sh2).rearrange("p (k d) -> p k d", k=3)
            pe.do(lambda e: e.matmul(bank[c][0:TP, :], onesf[0:1, 0:TP], b2s[:, :], start=False, stop=False), t_in, sig=False)
            for f in range(3):
                t = pe.do(lambda e, f=f: e.matmul(bank[c][0:TP, :], shT[:, f, c * TP:(c + 1) * TP], w2[:, f, :],
                                                  start=False, stop=f == 2), mem["sh"], landed[w_sh2], sig=f == 2)
            if c == TC - 1:
                release(w_sh2, t)
                mem["work"] = t
            return t

        def mm1(psum, w, cols, xg, *tokens):
            for j, f in enumerate(cols):
                for d in range(DC):
                    last = j == len(cols) - 1 and d == DC - 1
                    t2 = pe.do(lambda e, j=j, f=f, d=d: e.matmul(
                        psum[:, j * P:(j + 1) * P], w[:, d, f * P:(f + 1) * P], xg[:, d * P:(d + 1) * P],
                        start=d == 0, stop=d == DC - 1), *tokens, sig=last)
            return t2

        def mm2(yb, H, w, hs, first, last, *tokens):
            for j, h in enumerate(hs):
                t2 = pe.do(lambda e, j=j, h=h: e.matmul(
                    bank[yb][:, :], H[:, h * P:(h + 1) * P], w[:, j, :],
                    start=first and j == 0, stop=last and j == len(hs) - 1), *tokens, sig=j == len(hs) - 1)
            return t2

        wv = lambda n, k: slot(n).rearrange("p (k f) -> p k f", k=k)

        def expert0(e_, yb, xg, t_x):
            n1, n2 = w_l0[e_]
            w1 = wv(n1, DC)
            w2 = wv(n2, 6)[:, 3 * (e_ % 2):3 * (e_ % 2) + 3, :]
            q = e_ % 2
            gb, ub = (3, 4) if q else (5, 6)
            H = HT[:, 384 * q:384 * q + 384]
            G, U, S = ((HT[:, 768:1920] if q else TMP)[:, 384 * i:384 * i + 384] for i in range(3))
            tg = mm1(bank[gb], w1, [0, 1, 2], xg, t_x, landed[n1], free[gb])
            for j in range(3):
                t = act.do(lambda e, j=j: e.activation(G[:, j * P:(j + 1) * P], bank[gb][:, j * P:(j + 1) * P],
                                                       ACT.Identity, bias=b1[0][:, e_ * 6 + j:e_ * 6 + j + 1]),
                           tg, mem.get(("h", q)), mem["work"])
            free[gb] = t
            tu = mm1(bank[ub], w1, [3, 4, 5], xg, t_x, free[ub])
            for j in range(3):
                t2 = dve.do(lambda e, j=j: e.tensor_scalar(U[:, j * P:(j + 1) * P], bank[ub][:, j * P:(j + 1) * P],
                                                           b1[0][:, e_ * 6 + 3 + j:e_ * 6 + 4 + j], None, ALU.add),
                            tu, mem.get(("h", q)), mem["work"])
            free[ub] = t2
            th = swiglu(e_, G, U, S, H, [t, t2], mem.get(("hp", q)))
            mem["h", q] = th

            def second():
                t = mm2(yb, H, w2, [0, 1, 2], True, True, th, landed[n2], free[yb])
                mem["hp", q] = mem["hp"] = t
                return t
            return second

        def mm1w(b, w, cols, xg, n, *tokens):
            for j, f in enumerate(cols):
                for d in range(DC):
                    last = j == len(cols) - 1 and d == DC - 1
                    t = pe.do(lambda e, j=j, f=f, d=d: e.matmul(
                        bank[b][:, j * 256:j * 256 + n], w[:, d, f * P:(f + 1) * P], xg[:, d, 0:n],
                        start=d == 0, stop=d == DC - 1), *tokens, free[b], sig=last)
            return t

        share = lambda n: 2 if n <= 256 else 1

        def second(nh, slots):
            def m2(e_, off, yb, tg):
                for h in range(nh):
                    n2 = slots(e_)[h // 8]
                    w2 = wv(n2, 8)
                    t = pe.do(lambda e, h=h, w2=w2: e.matmul(
                        bank[yb][:, :], HW[:, h, off:off + CH], w2[:, h % 8, :], start=h == 0, stop=h == nh - 1),
                        tg[h // 2], landed[n2], free[yb], sig=h == nh - 1)
                mem["hp"] = t
                return t
            return m2

        def second_wide(nh, slots):
            def m2(e_, n, tg):
                m = share(n)
                for d in range(DC):
                    b, o = 1 + d // m, 256 * (d % m)
                    for h in range(nh):
                        n2 = slots(e_)[h // 8]
                        w2 = wv(n2, 8)
                        t = pe.do(lambda e, h=h, d=d, w2=w2, b=b, o=o: e.matmul(
                            bank[b][:, o:o + n], w2[:, h % 8, d * P:(d + 1) * P], HW[:, h, 0:n],
                            start=h == 0, stop=h == nh - 1), tg[h // 2], landed[n2], free[b], sig=h == nh - 1)
                    if d % m == m - 1:
                        free[b] = act.do(lambda e, d=d, b=b: e.activation(
                            YTT[:, d + 1 - m:d + 1, 0:n],
                            bank[b][:, :].rearrange("p (d n) -> p d n", d=m)[:, :, 0:n],
                            ACT.Copy), t, mem["ytt"], mem["work"])
                return (act.sem, act.n)
            return m2

        def first1(e_, n, xg, t_x):
            tg, m = [], share(n)
            for g in range(8 // m):
                hs = range(m * g, m * g + m)
                n1 = w_l1[e_][hs[0] // 4]
                w1, c = wv(n1, DC), [h % 4 for h in hs]
                hb, ub = 3 + 2 * (g % 2), 4 + 2 * (g % 2)
                th = mm1w(hb, w1, c, xg, n, t_x, landed[n1])
                tS = []
                for j, h in enumerate(hs):
                    S = SW[h // 2 % 2][:, h % 2, 0:n]
                    tS.append(act.do(lambda e, j=j, h=h, S=S, hb=hb: e.activation(
                        S, bank[hb][:, j * 256:j * 256 + n], ACT.Silu, bias=b1[1][:, e_ * 16 + h:e_ * 16 + h + 1]),
                        th, mem.get(("s", h // 2 % 2)), mem.get("hp"), mem["work"]))
                free[hb] = tS[-1]
                tu = mm1w(ub, w1, [4 + i for i in c], xg, n, t_x)
                for j, h in enumerate(hs):
                    S = SW[h // 2 % 2][:, h % 2, 0:n]
                    t = dve.do(lambda e, j=j, h=h, S=S, ub=ub: e.scalar_tensor_tensor(
                        HW[:, h, 0:n], bank[ub][:, j * 256:j * 256 + n], b1[1][:, e_ * 16 + 8 + h:e_ * 16 + 9 + h],
                        S, ALU.add, ALU.mult), tu, tS[j], mem.get("hp"), mem["work"])
                    if h % 2:
                        mem["s", h // 2 % 2] = t
                        tg.append(t)
                free[ub] = t
            return tg

        def first2(e_, n, xg, t_x):
            tg, m = [], share(n)
            for g in range(16 // m):
                hs = range(m * g, m * g + m)
                n1 = w_l2[e_][hs[0] // 8]
                b = 3 + g % 4
                th = mm1w(b, wv(n1, DC), [h % 8 for h in hs], xg, n, t_x, landed[n1])
                for j, h in enumerate(hs):
                    t = act.do(lambda e, j=j, h=h, b=b: e.activation(
                        HW[:, h, 0:n], bank[b][:, j * 256:j * 256 + n], ACT.Silu,
                        bias=b1[2][:, e_ * 16 + h:e_ * 16 + h + 1]), th, mem.get("hp"), mem["work"])
                    if h % 2:
                        tg.append(t)
                free[b] = t
            return tg

        def first3(e_, n, xg, t_x):
            tg, m = [], share(n)
            n1 = w_l3[e_][0]
            for g in range(8 // m):
                hs = range(m * g, m * g + m)
                b = 3 + g % 4
                th = mm1w(b, wv(n1, DC), hs, xg, n, t_x, landed[n1])
                for j, h in enumerate(hs):
                    t = dve.do(lambda e, j=j, h=h, b=b: e.tensor_scalar(
                        HW[:, h, 0:n], bank[b][:, j * 256:j * 256 + n],
                        b1[3][:, e_ * 8 + h:e_ * 8 + h + 1], 0.0, ALU.add, ALU.max), th, mem.get("hp"), mem["work"])
                    if h % 2:
                        tg.append(t)
                free[b] = t
            return tg

        expert1 = (first1, second(8, lambda e_: w_l1[e_][2:]), second_wide(8, lambda e_: w_l1[e_][2:]))
        expert2 = (first2, second(16, lambda e_: w_l2[e_][2:]), second_wide(16, lambda e_: w_l2[e_][2:]))
        expert3 = (first3, second(8, lambda e_: w_l3[e_][1:]), second_wide(8, lambda e_: w_l3[e_][1:]))

        def done(e_, rel):
            if e_ % 2 == 0:
                rel(w_l0[e_][0], t_pe())
            else:
                rel(w_l0[e_][1], t_pe())
                rel(w_l0[e_][0], t_pe())

        ts = moe(0, 16, I["L0_b2"], expert0, shared, shared_rows, ts,
                 lambda f: ln_tiles(f, xn, None, [0, 1, 2, 3, 4]), group=2)

        t_vec = load_vecs(("L1_gnn_bias", "L1_gnn_gamma", "L1_gnn_beta"), mem["work"])
        Av = A.rearrange("p (c i) -> p c i", c=TC)
        halves = ((0, 313), (313, 312))
        rdeg = W[:, 6209:6209 + N]
        for h, (h0, n) in enumerate(halves):
            for c in range(TC):
                t = pe.do(lambda e, h=h, h0=h0, n=n, c=c: e.matmul(
                    bank[5 + h][:, 0:n], onesf[0:TP, :], Av[:, c, h0:h0 + n], start=c == 0, stop=c == TC - 1),
                    free[5 + h], t_Adone, sig=c == TC - 1)
            t = dve.do(lambda e, h=h, h0=h0, n=n: e.tensor_scalar(
                rdeg[:, h0:h0 + n], bank[5 + h][:, 0:n], 1.0, None, ALU.max), t, mem["work"])
            free[5 + h] = t
        t_rd = dve.do(lambda e: e.reciprocal(rdeg, rdeg), t)
        nmT = W[:, 3125:3125 + 2500].rearrange("p (k n) -> p k n", k=DC)
        tn = []
        for m in range(DC):
            for h, (h0, n) in enumerate(halves):
                b = (2 * m + h) % 8
                for c in range(TC):
                    t = pe.do(lambda e, m=m, b=b, h0=h0, n=n, c=c: e.matmul(
                        bank[b][:, 0:n], xn[:, c, m * P:(m + 1) * P], Av[:, c, h0:h0 + n],
                        start=c == 0, stop=c == TC - 1), ts[c], free[b], sig=c == TC - 1)
                free[b] = dve.do(lambda e, m=m, b=b, h0=h0, n=n: e.tensor_tensor(
                    nmT[:, m, h0:h0 + n], bank[b][:, 0:n], rdeg[:, h0:h0 + n], ALU.mult), t, t_rd, mem["work"])
                tn.append(free[b])
        xn_free.append(t_pe())
        hrow = W[0:TP, 6840:6840 + 2560].rearrange("p (c d) -> p c d", c=TC)

        def norm_rows(c, psum, t, t_vec):
            h = hrow[:, c, :]
            tf = t = dve.do(lambda e: e.tensor_tensor(h, psum, vec(0), ALU.add), t, t_vec, mem["work"])
            t = dve.do(lambda e: e.bn_stats(stats[:, c, :], h), t)
            t = dve.do(lambda e: e.bn_aggr(mv[:, c, :], stats[:, c, :]), t)
            tr = act.do(lambda e: e.activation(rstd[:, c:c + 1], mv[:, c, 1:2], ACT.Sqrt, bias=eps[0:TP, :]), t, t_eps, xn_free)
            t = dve.do(lambda e: e.scalar_tensor_tensor(h, h, mv[:, c, 0:1], vec(1), ALU.subtract, ALU.mult), t)
            tr = dve.do(lambda e: e.reciprocal(rstd[:, c:c + 1], rstd[:, c:c + 1]), tr)
            xt[c] = dve.do(lambda e: e.scalar_tensor_tensor(
                x[:, c, :], h, rstd[:, c:c + 1], x[:, c, :], ALU.mult, ALU.add), t, tr, xt[c])
            return tf

        def add_beta(ts):
            for c in range(TC):
                xt[c] = pool.do(lambda e, c=c: e.tensor_tensor(x[:, c, :], x[:, c, :], vec(2), ALU.add), ts[c], t_vec)

        add_beta(ts)
        OF = [R[0:TP, 8758 + 630 * i:8758 + 630 * (i + 1)] for i in range(4)]
        B = 8

        def halve(c, q, free_, eng):
            n, o = (w_ea[0], c) if c < 42 else (w_ea[1], c - 42)
            m = min(B, (43 if c >= 42 else 42) - o)
            parts = R[0:TP, 1536 * q:1536 * q + 192 * m].rearrange("p (c h f) -> p c h f", c=m, h=2)
            raw = slot(n)[:, o * 96:(o + m) * 96].rearrange("p (c f) -> p c f", c=m)
            th = act.do(lambda e: e.activation(parts[:, :, 0], raw, ACT.Copy), landed[n], free_)
            return th, eng.do(lambda e: e.tensor_tensor(
                parts[:, :, 1], raw, parts[:, :, 0].bitcast(F32), ALU.subtract), th, landed[n], free_)

        def edge_sums(tiles_of):
            fr, th, tl = [None] * 4, None, None
            hi_free = [None] * 2
            q, begun = 1, set()
            for c in range(EC):
                b, ms = c % 4, tiles_of(c)
                n, o = (w_ea[0], c) if c < 42 else (w_ea[1], c - 42)
                if o % B == 0:
                    q = 1 - q
                    th, tl = early[c] if c in early else halve(c, q, hi_free[q], dve if c // B % 2 else pool)
                t = dve.do(lambda e, b=b, c=c, ms=ms: e.tensor_scalar(
                    OF[b][:, 0:126 * len(ms)], iota[0:TP, 126 * ms[0]:126 * (ms[-1] + 1)], ef[:, 1, c:c + 1], None,
                    ALU.is_equal), fr[b], mem["work"])
                for i, m in enumerate(ms):
                    rhs = R[0:TP, 1536 * q + 192 * (o % B):1536 * q + 192 * (o % B + 1)]
                    first = m not in begun
                    begun.add(m)
                    fr[b] = pe.do(lambda e, b=b, i=i, m=m, rhs=rhs, first=first: e.matmul(
                        bank[m][0:126, 0:192], OF[b][:, 126 * i:126 * (i + 1)], rhs, start=first, stop=True,
                        skip_group_check=True), t, th, tl, free[m], sig=m == ms[-1])
                if o % B == B - 1 or c == 41:
                    hi_free[q] = fr[b]

        t_nb = t_pe()
        early = {c: halve(c, c // B, t_nb, pool) for c in (0, B)}
        wg1 = wv(w_l1g, 8)

        def rows1(c):
            for d in range(8):
                lhs = (xnT if d < DC else nmT)[:, d % DC, c * TP:(c + 1) * TP]
                t = pe.do(lambda e, c=c, d=d, lhs=lhs: e.matmul(bank[c][0:TP, :], lhs, wg1[:, d, :], start=d == 0, stop=d == 7),
                          tT[c], tn, landed[w_l1g], free[c], sig=d == 7)
            free[c] = norm_rows(c, bank[c][0:TP, :], t, t_vec)
        ts = ln_tiles(rows1, xn, logits(1, 8), [0, 1, 2, 3, 4], 2)
        hold(w_l1g, t_pe())
        xnT_free.append(t_pe())
        mem["work"] = xt[TC - 1]
        mem["gt"] = [mem["work"]] * 9

        def edges():
            for en in (act, pool):
                en.ops.append(("count", "far", far[0:1, 0:1]))
            either((dve, pe, act, pool), "far", lambda: edge_sums(lambda c: range(TC)),
                   lambda: edge_sums(lambda c: reach(c, 126)))
            t = t_pe()
            for n in w_ea:
                release(n, t)
            sums = [W[0:126, 96 * m:96 * (m + 1)] for m in range(TC)]
            for m in range(TC):
                t1 = act.do(lambda e, m=m: e.activation(sums[m], bank[m][0:126, 0:96], ACT.Copy), t)
                free[m] = dve.do(lambda e, m=m: e.tensor_tensor(sums[m], sums[m], bank[m][0:126, 96:192], ALU.add), t1)
            for m in range(TC):
                b, o = (5, 126 * m) if m < 4 else (6, 0)
                t = pe.do(lambda e, m=m, b=b, o=o: e.transpose(
                    bank[b][0:96, o:o + 126], sums[m], ident[0:126, 0:126]), free[m], free[b])
            free[5] = act.do(lambda e: e.activation(aggT[:, 0:504], bank[5][0:96, 0:504], ACT.Copy), t)
            free[6] = act.do(lambda e: e.activation(aggT[:, 504:N], bank[6][0:96, 0:N - 504], ACT.Copy), t)
            mem["agg"] = free[6]
            mem["work"] = t

        def done(e_, rel):
            for n in w_l1[e_]:
                rel(n, t_pe())

        ts = moe(1, 8, I["L1_b2"], expert1, edges, None, ts, lambda f: ln_tiles(f, xn, None, [0, 1, 2, 3, 4]))

        t_vec = load_vecs(("L2_gnn_b3", "L2_gnn_gamma", "L2_gnn_beta"), mem["work"])
        add_beta(ts)
        h1 = W[:, 0:5000].rearrange("p (f n) -> p f n", f=8)
        w1a, w1b = wv(w_l2g[0], DC), slot(w_l2g[1])
        th1 = []
        for f in range(8):
            for h, (h0, n) in enumerate(halves):
                b = (2 * f + h) % 8
                for d in range(DC + 1):
                    lhs = w1a[:, d, f * P:(f + 1) * P] if d < DC else w1b[:, f * P:(f + 1) * P]
                    rhs = xnT[:, d, h0:h0 + n] if d < DC else aggT[:, h0:h0 + n]
                    t = pe.do(lambda e, b=b, n=n, d=d, lhs=lhs, rhs=rhs: e.matmul(
                        bank[b][:, 0:n], lhs, rhs, start=d == 0, stop=d == DC), tT, mem["agg"],
                        landed[w_l2g[0]], landed[w_l2g[1]], free[b], sig=d == DC)
                free[b] = act.do(lambda e, b=b, n=n, h0=h0, f=f: e.activation(
                    h1[:, f, h0:h0 + n], bank[b][:, 0:n], ACT.Relu, bias=gb1[:, f:f + 1]), t, t_in, mem["work"])
                th1.append(free[b])
        release(w_l2g[0], t_pe())
        release(w_l2g[1], t_pe())
        t_h1 = t_pe()
        w3 = wv(w_l2g[4], 8)
        h2f = W[:, 9402:11402]
        def group2(c0, c1):
            h0, n = c0 * TP, (c1 - c0) * TP
            hv = h2f[:, 0:8 * n].rearrange("p (f n) -> p f n", f=8)
            th2 = []
            for f in range(8):
                for d in range(8):
                    w2 = wv(w_l2g[2 + d // 4], DC)
                    t = pe.do(lambda e, d=d, f=f, w2=w2: e.matmul(
                        bank[f][:, 0:n], w2[:, d % 4, f * P:(f + 1) * P], h1[:, d, h0:h0 + n],
                        start=d == 0, stop=d == 7), th1, landed[w_l2g[2]], landed[w_l2g[3]], free[f], sig=d == 7)
                free[f] = act.do(lambda e, f=f: e.activation(
                    hv[:, f, :], bank[f][:, 0:n], ACT.Relu, bias=gb1[:, 8 + f:9 + f]), t, mem["h2"])
                th2.append(free[f])
            return hv, th2

        mem["h2"] = t_h1
        now = {}

        def rows2(c):
            if c % 2 == 0:
                now["c0"], now["h"] = c, group2(c, min(c + 2, TC))
            c0, (hv, th2) = now["c0"], now["h"]
            for f in range(8):
                t = pe.do(lambda e, f=f: e.matmul(
                    bank[c][0:TP, :], hv[:, f, (c - c0) * TP:(c - c0 + 1) * TP], w3[:, f, :],
                    start=f == 0, stop=f == 7), th2, landed[w_l2g[4]], free[c], sig=f == 7)
            mem["h2"] = t
            free[c] = norm_rows(c, bank[c][0:TP, :], t, t_vec)

        ts = ln_tiles(rows2, xn, logits(2, 8), [0, 1, 2, 3, 4], 2)
        for n in w_l2g[2:5]:
            hold(n, t_pe())
        xnT_free.append(t_pe())
        mem["work"] = xt[TC - 1]
        mem["gt"] = [mem["work"]] * 9

        def done(e_, rel):
            for n in w_l2[e_]:
                rel(n, t_pe())

        xnB = W[0:TP, 10805:10805 + TC * D].rearrange("p (c d) -> p c d", c=TC)
        ts = moe(2, 8, I["L2_b2"], expert2, lambda: None, None, ts, lambda f: ln_tiles(f, xnB))

        t_seg = mem["seg"]
        inv = sT[:, 3, :]
        t_inv = dve.do(lambda e: e.reciprocal(inv, cs), t_seg)
        B3 = W[0:TP, 0:3125].rearrange("p (c i) -> p c i", c=TC)
        dgs = [W[0:TP, 3125 + TP * i:3125 + TP * (i + 1)] for i in range(TC)]
        for c in range(TC):
            t = dve.do(lambda e, c=c: e.tensor_scalar(dgs[c], ident[0:TP, 0:TP], gg[:, c:c + 1], None, ALU.mult),
                       t_seg, mem["work"])
            b, o = (5, c * TP) if c < 4 else (6, 0)
            t = pe.do(lambda e, b=b, o=o, c=c: e.matmul(
                bank[b][0:TP, o:o + TP], onesf[0:TP, 0:TP], dgs[c], start=True, stop=True), t, free[b])
        tB = []
        for c in range(TC):
            dve.do(lambda e, c=c: e.tensor_scalar(B3[:, c, 0:500], bank[5][0:TP, 0:500], sg[:, c:c + 1], None, ALU.is_equal), t)
            tB.append(dve.do(lambda e, c=c: e.tensor_scalar(B3[:, c, 500:N], bank[6][0:TP, 0:TP], sg[:, c:c + 1], None, ALU.is_equal)))
        free[5] = free[6] = tB[-1]

        def averaged(i):
            for j in range(TC):
                t = pe.do(lambda e, j=j: e.matmul(
                    bank[i][0:TP, :], B3[:, j, i * TP:(i + 1) * TP], xnB[:, j, :], start=j == 0, stop=j == TC - 1),
                    ts[j], tB[j], free[i], sig=j == TC - 1)
            xt[i] = free[i] = dve.do(lambda e: e.scalar_tensor_tensor(
                x[:, i, :], bank[i][0:TP, :], inv[:, i:i + 1], x[:, i, :], ALU.mult, ALU.add), t, xt[i], t_inv)

        ts3 = ln_tiles(averaged, xn, logits(3, 8), [0, 1, 2, 3, 4], 2)
        mem["work"] = [mem["work"], t_pe()]

        def done(e_, rel):
            for n in w_l3[e_]:
                rel(n, t_pe())

        t_out = []

        def finish(produce):
            for c in range(TC):
                produce(c)
                for a, b in ((0, 120), (120, 125)):
                    t_out.append(act.dma(d_out, lambda e, a=a, b=b, c=c: e.dma_start(out_v[a:b, c, :], x[a:b, c, :]), xt[c]))

        moe(3, 8, I["L3_b2"], expert3, lambda: None, None, ts3, finish)
        act.wait(t_out[-1])

        block = ctx.enter_context(nc.Block())

        @block.sync
        def _(eng):
            sp.emit(eng)

        @block.gpsimd
        def _(eng):
            pool.emit(eng)

        @block.scalar
        def _(eng):
            act.emit(eng)

        @block.vector
        def _(eng):
            dve.emit(eng)

        @block.tensor
        def _(eng):
            pe.emit(eng)


def kernel(**a):
    import numpy as np
    import concourse.bacc as bacc
    from concourse.bass_utils import run_bass_kernel_spmd

    a = {k: np.asarray(v) for k, v in a.items()}

    def blocks(w):
        *lead, k, f = w.shape
        w = w.reshape(*lead, k // P, P, f)
        return np.moveaxis(w, -2, -3).reshape(*lead, P, k // P * f)

    def split_gu(w):
        return np.concatenate([w[..., 0::2], w[..., 1::2]], -1)

    def cols(b):
        return b.reshape(-1, P).T

    row = lambda v: v.reshape(1, -1)
    ins = {
        "x": a["x"], "src": a["src"], "dst": a["dst"],
        "src_c": a["src"].reshape(EC, TP).T, "dst_c": a["dst"].reshape(EC, TP).T,
        "L0_gnn_W": blocks(a["L0_gnn_W"]), "L0_gnn_b": row(a["L0_gnn_b"]),
        "L0_a_src": row(a["L0_gnn_a"][:D]), "L0_a_dst": row(a["L0_gnn_a"][D:]),
        "act": row(np.concatenate([a["L0_ffn_expert_act"], a["L0_ffn_shared_act"][None]], 0)),
        "sh_w1": blocks(split_gu(a["L0_ffn_shared_w1"])), "sh_w2": blocks(a["L0_ffn_shared_w2"]),
        "sh_b2": row(a["L0_ffn_shared_b2"]),
        "L0_w1": blocks(split_gu(a["L0_ffn_expert_w1"])),
        "L0_w2": np.concatenate([blocks(a["L0_ffn_expert_w2"][0::2]), blocks(a["L0_ffn_expert_w2"][1::2])], -1),
        "L0_b1": cols(split_gu(np.concatenate([a["L0_ffn_expert_b1"], a["L0_ffn_shared_b1"][None]], 0))),
        "L0_b2": a["L0_ffn_expert_b2"],
        "L1_gnn_W": blocks(np.concatenate([a["L1_gnn_W_self"].T, a["L1_gnn_W_neigh"].T], 0)),
        "L1_gnn_bias": row(a["L1_gnn_bias"]), "L1_gnn_gamma": row(a["L1_gnn_gamma"]), "L1_gnn_beta": row(a["L1_gnn_beta"]),
        "L1_b1": cols(a["L1_ffn_fc1_b"]), "L1_b2": a["L1_ffn_fc2_b"],
        "L1_w2": blocks(np.swapaxes(a["L1_ffn_fc2_w"], 1, 2)),
        "L2_gnn_W1a": blocks(a["L2_gnn_W1"][:D]), "L2_gnn_W1b": a["L2_gnn_W1"][D:],
        "L2_gnn_W2": blocks(a["L2_gnn_W2"].reshape(2, 512, 1024)), "L2_gnn_W3": blocks(a["L2_gnn_W3"]),
        "L2_gnn_b": cols(np.stack([a["L2_gnn_b1"], a["L2_gnn_b2"]])),
        "L2_gnn_b3": row(a["L2_gnn_b3"]), "L2_gnn_gamma": row(a["L2_gnn_gamma"]), "L2_gnn_beta": row(a["L2_gnn_beta"]),
        "L2_w1": blocks(np.moveaxis(a["L2_ffn_W1"].reshape(8, D, 2, 1024), 2, 1)),
        "L2_w2": blocks(a["L2_ffn_W2"].reshape(8, 2, 1024, D)),
        "L2_b1": cols(a["L2_ffn_b1"]), "L2_b2": a["L2_ffn_b2"],
        "L3_w1": blocks(a["L3_ffn_w1"]), "L3_w2": blocks(a["L3_ffn_w2"]),
        "L3_b1": cols(a["L3_ffn_b1"]), "L3_b2": a["L3_ffn_b2"],
        "L0_gb": row(a["L0_ffn_gate_b"]), "L1_gb": row(a["L1_ffn_router_b"]),
        "L2_gb": row(a["L2_ffn_bg"]), "L3_gb": row(a["L3_ffn_gate_b"]),
    }
    f1 = np.swapaxes(a["L1_ffn_fc1_w"], 1, 2).reshape(8, D, 2, 2, 512)
    ins["L1_w1"] = blocks(np.ascontiguousarray(np.transpose(f1, (0, 3, 1, 2, 4))).reshape(8, 2, D, 1024))
    for nm, g in (("L0", a["L0_ffn_gate_w"]), ("L1", a["L1_ffn_router_w"].T), ("L2", a["L2_ffn_Wg"]), ("L3", a["L3_ffn_gate_w"])):
        ins[nm + "_gate"] = np.moveaxis(g.reshape(DC, P, -1), 1, 0)
    ea = a["edge_attr_96"].reshape(EC, TP, 96).transpose(1, 0, 2)
    ins["ea0"] = ea[:, :42].reshape(TP, -1)
    ins["ea1"] = ea[:, 42:].reshape(TP, -1)

    nc = bacc.Bacc("TRN2", target_bir_lowering=False, num_devices=1)
    arrays, aps = {}, {}
    for k, v in ins.items():
        v = np.ascontiguousarray(v)
        arrays["in_" + k] = v
        aps[k] = nc.dram_tensor("in_" + k, v.shape, mybir.dt.from_np(v.dtype), kind="ExternalInput").ap()
    out = nc.dram_tensor("out_x", (N, D), F32, kind="ExternalOutput").ap()
    program(nc, aps, out)
    r = run_bass_kernel_spmd(nc, [arrays], core_ids=[0])
    return r.results[0]["out_x"]
```
